# Optimizing a Trainium2 kernel written in Bass

```python
import numpy as np
import jax
import jax.numpy as jnp

def _softmax(x, axis=-1):
    return jax.nn.softmax(x, axis=axis)

def _gelu(x):
    return jax.nn.gelu(x, approximate=True)

def _silu(x):
    return jax.nn.silu(x)

def _sigmoid(x):
    return jax.nn.sigmoid(x)

def _layernorm(x, axis=-1, eps=1e-05):
    m = jnp.mean(x, axis=axis, keepdims=True)
    v = jnp.var(x, axis=axis, keepdims=True)
    return (x - m) / jnp.sqrt(v + eps)

def _scatter_add(tgt, idx, src, axis=0):
    return tgt.at[idx].add(src)

def _segment_sum(src, seg, n):
    return jax.ops.segment_sum(src, seg, n)
kernel_name = 'mk_gps_d1_gnn_r32_a93633'

def setup_inputs(seed: int=0):
    np.random.seed(seed)
    _w = jnp.asarray

    def _rec_inputs():
        import jax
        import jax.numpy as jnp
        _gk = jax.random.key(seed)
        x = -0.0002117 + 1 * jax.random.normal(jax.random.fold_in(_gk, 1), (3125, 256), jnp.float32)
        src = jax.random.randint(jax.random.fold_in(_gk, 2), (50000,), 0, 3125, jnp.int32)
        dst = jax.random.randint(jax.random.fold_in(_gk, 3), (50000,), 0, 3125, jnp.int32)
        _o = jnp.argsort(dst, stable=True)
        src = src[_o]
        dst = dst[_o]
        return (x, src, dst)
    x, src, dst = _rec_inputs()

    def _L0_gnn_setup():
        import jax, jax.numpy as jnp
        import numpy as np
        N_NODES = 3125
        N_EDGES = 9375
        HIDDEN = 256
        N_LAYERS = 3
        LN_EPS = 1e-05

        def _layer_norm(x, g, b):
            mu = jnp.mean(x, axis=-1, keepdims=True)
            var = jnp.mean(jnp.square(x - mu), axis=-1, keepdims=True)
            return (x - mu) * jax.lax.rsqrt(var + LN_EPS) * g + b

        def _gin_layer(h, src, dst, W1, b1, W2, b2, eps, gamma, beta):
            agg = jax.ops.segment_sum(h[src], dst, num_segments=N_NODES)
            z = (1.0 + eps) * h + agg
            m = jax.nn.relu(z @ W1 + b1) @ W2 + b2
            return jax.nn.relu(_layer_norm(m + h, gamma, beta))
        key = jax.random.key(seed)
        ks = jax.random.split(key, 6)
        h = jax.random.normal(ks[0], (N_NODES, HIDDEN), dtype=jnp.float32)
        edge_index = jax.random.randint(ks[1], (2, N_EDGES), 0, N_NODES, dtype=jnp.int64)
        scale = 1.0 / np.sqrt(HIDDEN)
        W1 = jax.random.normal(ks[2], (N_LAYERS, HIDDEN, HIDDEN), dtype=jnp.float32) * scale
        W2 = jax.random.normal(ks[3], (N_LAYERS, HIDDEN, HIDDEN), dtype=jnp.float32) * scale
        b1 = jnp.zeros((N_LAYERS, HIDDEN), dtype=jnp.float32)
        b2 = jnp.zeros((N_LAYERS, HIDDEN), dtype=jnp.float32)
        eps = jnp.zeros((N_LAYERS,), dtype=jnp.float32)
        gamma = jnp.ones((N_LAYERS, HIDDEN), dtype=jnp.float32)
        beta = jnp.zeros((N_LAYERS, HIDDEN), dtype=jnp.float32)
        return {'h': h, 'edge_index': edge_index, 'W1': W1, 'b1': b1, 'W2': W2, 'b2': b2, 'eps': eps, 'gamma': gamma, 'beta': beta}
    _L0_gnn_all = _L0_gnn_setup()
    _L0_gnn_in = {k: v for k, v in _L0_gnn_all.items() if k in ('W1', 'b1', 'W2', 'b2', 'eps', 'gamma', 'beta')}
    del _L0_gnn_all

    def _L0_mix_setup():
        import jax, jax.numpy as jnp
        import numpy as np
        DIM = 256
        HEADS = 4
        HEAD_DIM = DIM // HEADS
        MLP_HIDDEN = DIM * 3
        B, N = (8, 128)
        EPS = 1e-05

        def _layernorm(x, g, b):
            mu = jnp.mean(x, axis=-1, keepdims=True)
            var = jnp.mean(jnp.square(x - mu), axis=-1, keepdims=True)
            return (x - mu) * jax.lax.rsqrt(var + EPS) * g + b
        key = jax.random.key(seed)
        ks = jax.random.split(key, 8)
        s = 0.02
        return {'x': jax.random.normal(ks[0], (B, N, DIM), dtype=jnp.float32), 'w_qkv': jax.random.normal(ks[1], (DIM, 3 * DIM), dtype=jnp.float32) * s, 'b_qkv': jnp.zeros((3 * DIM,), dtype=jnp.float32), 'norm_g': jnp.ones((DIM,), dtype=jnp.float32), 'norm_b': jnp.zeros((DIM,), dtype=jnp.float32), 'w_fc1': jax.random.normal(ks[2], (DIM, MLP_HIDDEN), dtype=jnp.float32) * s, 'b_fc1': jnp.zeros((MLP_HIDDEN,), dtype=jnp.float32), 'w_fc2': jax.random.normal(ks[3], (MLP_HIDDEN, DIM), dtype=jnp.float32) * s, 'b_fc2': jnp.zeros((DIM,), dtype=jnp.float32)}
    _L0_mix_all = _L0_mix_setup()
    _L0_mix_in = {k: v for k, v in _L0_mix_all.items() if k in ('w_qkv', 'b_qkv', 'norm_g', 'norm_b', 'w_fc1', 'b_fc1', 'w_fc2', 'b_fc2')}
    del _L0_mix_all

    def _L0_ffn_setup():
        import jax, jax.numpy as jnp
        import numpy as np
        NUM_EXPERTS = 8
        TOP_K = 2
        B, S, D = (8, 256, 256)

        def _moe(tokens, router_w, w1, b1, w2, b2):
            N = tokens.shape[0]
            E = router_w.shape[0]
            logits = tokens.astype(jnp.float32) @ router_w.astype(jnp.float32).T
            probs = jax.nn.softmax(logits, axis=-1)
            rw, re = jax.lax.top_k(probs, TOP_K)
            if TOP_K > 1:
                rw = rw / jnp.maximum(rw.sum(-1, keepdims=True), 1e-12)
            rw = rw.astype(tokens.dtype)
            combine = jnp.zeros((N, E), tokens.dtype).at[jnp.arange(N)[:, None], re].set(rw)
            out = tokens
            for e in range(E):
                h = jax.nn.gelu(tokens @ w1[e] + b1[e], approximate=False)
                y = h @ w2[e] + b2[e]
                out = out + combine[:, e:e + 1] * y
            return out
        key = jax.random.key(seed)
        ks = jax.random.split(key, 4)
        scale = 1.0 / np.sqrt(D).astype(np.float32)
        return {'input_embeddings': jax.random.normal(ks[0], (B, S, D), jnp.float32), 'router_w': jax.random.normal(ks[1], (NUM_EXPERTS, D), jnp.float32) * scale, 'w1': jax.random.normal(ks[2], (NUM_EXPERTS, D, D), jnp.float32) * scale, 'b1': jnp.zeros((NUM_EXPERTS, D), jnp.float32), 'w2': jax.random.normal(ks[3], (NUM_EXPERTS, D, D), jnp.float32) * scale, 'b2': jnp.zeros((NUM_EXPERTS, D), jnp.float32)}
    _L0_ffn_all = _L0_ffn_setup()
    _L0_ffn_in = {k: v for k, v in _L0_ffn_all.items() if k in ('router_w', 'w1', 'b1', 'w2', 'b2')}
    del _L0_ffn_all
    return {'x': x, 'src': src, 'dst': dst, 'L0_gnn_W1': _L0_gnn_in['W1'], 'L0_gnn_b1': _L0_gnn_in['b1'], 'L0_gnn_W2': _L0_gnn_in['W2'], 'L0_gnn_b2': _L0_gnn_in['b2'], 'L0_gnn_eps': _L0_gnn_in['eps'], 'L0_gnn_gamma': _L0_gnn_in['gamma'], 'L0_gnn_beta': _L0_gnn_in['beta'], 'L0_mix_w_qkv': _L0_mix_in['w_qkv'], 'L0_mix_b_qkv': _L0_mix_in['b_qkv'], 'L0_mix_norm_g': _L0_mix_in['norm_g'], 'L0_mix_norm_b': _L0_mix_in['norm_b'], 'L0_mix_w_fc1': _L0_mix_in['w_fc1'], 'L0_mix_b_fc1': _L0_mix_in['b_fc1'], 'L0_mix_w_fc2': _L0_mix_in['w_fc2'], 'L0_mix_b_fc2': _L0_mix_in['b_fc2'], 'L0_ffn_router_w': _L0_ffn_in['router_w'], 'L0_ffn_w1': _L0_ffn_in['w1'], 'L0_ffn_b1': _L0_ffn_in['b1'], 'L0_ffn_w2': _L0_ffn_in['w2'], 'L0_ffn_b2': _L0_ffn_in['b2']}

def reference(x, src, dst, L0_gnn_W1, L0_gnn_b1, L0_gnn_W2, L0_gnn_b2, L0_gnn_eps, L0_gnn_gamma, L0_gnn_beta, L0_mix_w_qkv, L0_mix_b_qkv, L0_mix_norm_g, L0_mix_norm_b, L0_mix_w_fc1, L0_mix_b_fc1, L0_mix_w_fc2, L0_mix_b_fc2, L0_ffn_router_w, L0_ffn_w1, L0_ffn_b1, L0_ffn_w2, L0_ffn_b2):
    import jax
    import jax.numpy as jnp

    def _L0_gnn_ref(h, edge_index, W1, b1, W2, b2, eps, gamma, beta):
        import jax, jax.numpy as jnp
        import numpy as np
        N_NODES = 3125
        N_EDGES = 9375
        HIDDEN = 256
        N_LAYERS = 3
        LN_EPS = 1e-05

        def _layer_norm(x, g, b):
            mu = jnp.mean(x, axis=-1, keepdims=True)
            var = jnp.mean(jnp.square(x - mu), axis=-1, keepdims=True)
            return (x - mu) * jax.lax.rsqrt(var + LN_EPS) * g + b

        def _gin_layer(h, src, dst, W1, b1, W2, b2, eps, gamma, beta):
            agg = jax.ops.segment_sum(h[src], dst, num_segments=N_NODES)
            z = (1.0 + eps) * h + agg
            m = jax.nn.relu(z @ W1 + b1) @ W2 + b2
            return jax.nn.relu(_layer_norm(m + h, gamma, beta))
        src, dst = (edge_index[0], edge_index[1])
        for l in range(N_LAYERS):
            h = _gin_layer(h, src, dst, W1[l], b1[l], W2[l], b2[l], eps[l], gamma[l], beta[l])
        return h

    def _L0_mix_ref(x, w_qkv, b_qkv, norm_g, norm_b, w_fc1, b_fc1, w_fc2, b_fc2):
        import jax, jax.numpy as jnp
        import numpy as np
        DIM = 256
        HEADS = 4
        HEAD_DIM = DIM // HEADS
        MLP_HIDDEN = DIM * 3
        B, N = (8, 128)
        EPS = 1e-05

        def _layernorm(x, g, b):
            mu = jnp.mean(x, axis=-1, keepdims=True)
            var = jnp.mean(jnp.square(x - mu), axis=-1, keepdims=True)
            return (x - mu) * jax.lax.rsqrt(var + EPS) * g + b
        Bx, Nx, C = x.shape
        scale = HEAD_DIM ** (-0.5)
        qkv = (x @ w_qkv + b_qkv).reshape(Bx, Nx, 3, HEADS, HEAD_DIM)
        qkv = jnp.transpose(qkv, (2, 0, 3, 1, 4))
        q, k, v = (qkv[0], qkv[1], qkv[2])
        k = k * scale
        attn = jnp.einsum('bhnd,bhne->bhde', k, v)
        attn = jax.nn.softmax(attn, axis=-1)
        xf = jnp.einsum('bhde,bhne->bhnd', attn, q)
        xf = jnp.transpose(xf, (0, 2, 1, 3)).reshape(Bx, Nx, C)
        x = x + xf
        h = _layernorm(x, norm_g, norm_b)
        h = jax.nn.gelu(h @ w_fc1 + b_fc1, approximate=False) @ w_fc2 + b_fc2
        return x + h

    def _L0_ffn_ref(input_embeddings, router_w, w1, b1, w2, b2):
        import jax, jax.numpy as jnp
        import numpy as np
        NUM_EXPERTS = 8
        TOP_K = 2
        B, S, D = (8, 256, 256)

        def _moe(tokens, router_w, w1, b1, w2, b2):
            N = tokens.shape[0]
            E = router_w.shape[0]
            logits = tokens.astype(jnp.float32) @ router_w.astype(jnp.float32).T
            probs = jax.nn.softmax(logits, axis=-1)
            rw, re = jax.lax.top_k(probs, TOP_K)
            if TOP_K > 1:
                rw = rw / jnp.maximum(rw.sum(-1, keepdims=True), 1e-12)
            rw = rw.astype(tokens.dtype)
            combine = jnp.zeros((N, E), tokens.dtype).at[jnp.arange(N)[:, None], re].set(rw)
            out = tokens
            for e in range(E):
                h = jax.nn.gelu(tokens @ w1[e] + b1[e], approximate=False)
                y = h @ w2[e] + b2[e]
                out = out + combine[:, e:e + 1] * y
            return out
        b, s, d = input_embeddings.shape
        tokens = input_embeddings.reshape(b * s, d)
        return _moe(tokens, router_w, w1, b1, w2, b2).reshape(b, s, d)
    edge_index = jnp.stack([src, dst])
    xn = _layernorm(x, axis=-1)
    x = x + _L0_gnn_ref(xn, edge_index, L0_gnn_W1, L0_gnn_b1, L0_gnn_W2, L0_gnn_b2, L0_gnn_eps, L0_gnn_gamma, L0_gnn_beta) + _L0_mix_ref(xn[None], L0_mix_w_qkv, L0_mix_b_qkv, L0_mix_norm_g, L0_mix_norm_b, L0_mix_w_fc1, L0_mix_b_fc1, L0_mix_w_fc2, L0_mix_b_fc2)[0]
    x = x + _L0_ffn_ref(_layernorm(x, axis=-1)[None], L0_ffn_router_w, L0_ffn_w1, L0_ffn_b1, L0_ffn_w2, L0_ffn_b2)[0]
    return x

_drawn_inputs = setup_inputs


def setup_inputs(seed=0):
    import zlib

    import numpy as np

    out = dict(_drawn_inputs(seed))
    spreads = {'L0_gnn_b1': (0.0, 0.568),
     'L0_gnn_b2': (0.0, 0.387),
     'L0_gnn_eps': (0.0, 0.8),
     'L0_gnn_gamma': (1.0, 0.2),
     'L0_gnn_beta': (0.0, 0.1),
     'L0_mix_b_qkv': (0.0, 0.1),
     'L0_mix_norm_g': (1.0, 0.6),
     'L0_mix_norm_b': (0.0, 0.8),
     'L0_mix_b_fc1': (0.0, 0.343),
     'L0_mix_b_fc2': (0.0, 0.1),
     'L0_ffn_b1': (0.0, 0.493),
     'L0_ffn_b2': (0.0, 0.338)}
    factors = {}
    for name, (base, spread) in spreads.items():
        noise = np.random.default_rng([zlib.crc32(name.encode()), seed]).standard_normal(out[name].shape)
        drawn = base * np.exp(spread * noise) if base else spread * noise
        out[name] = jnp.asarray(drawn.astype(out[name].dtype))
    for name, factor in factors.items():
        out[name] = (out[name] * factor).astype(out[name].dtype)
    return out
```

```python
import concourse.bass as bass
from concourse import mybir
from contextlib import ExitStack


def pipelined(eng, steps, count, unroll=2, head=2):
    lag = max(l for l, _ in steps)
    start = -(-(lag + head) // unroll) * unroll
    end = count // unroll * unroll

    def peeled(i):
        for l, fn in steps:
            if 0 <= i - l < count:
                fn(i - l, (i - l) % unroll, (i - l) // unroll)

    if end - start < 2 * unroll:
        for i in range(count + lag):
            peeled(i)
        return
    for i in range(start):
        peeled(i)
    with eng.Fori(start // unroll, end // unroll) as turn:
        for u in range(unroll):
            for l, fn in steps:
                slot = (u - l) % unroll
                back = (u - l - slot) // unroll
                fn(turn * unroll + (u - l), slot, turn + back)
    for i in range(end, count + lag):
        peeled(i)


def graph_block_kernel(nc, x, src, dst, gW1, gb1, gW2, gb2, geps, ggamma, gbeta,
                       w_qkv, b_qkv, norm_g, norm_b, w_fc1, b_fc1, w_fc2, b_fc2,
                       router_w, e_w1, e_b1, e_w2, e_b2, out, h_dram, acc_dram):
    fp32 = mybir.dt.float32
    i32 = mybir.dt.int32
    u32 = mybir.dt.uint32
    ALU = mybir.AluOpType
    ACT = mybir.ActivationFunctionType
    AX = mybir.AxisListType

    N, D = x.shape
    E = src.shape[0]
    L = gW1.shape[0]
    X = router_w.shape[0]
    F = w_fc1.shape[1]
    P = 125
    NT = N // P
    KD = D // 128
    KF = F // 128
    HD = 64
    ET = E // P
    CH = 4 * P
    NC = -(-N // CH)
    EPS = 1e-5
    assert NT * P == N and ET * P == E and NT % 2 == 1

    ctx = ExitStack()
    with ctx:
        ctx.enter_context(nc.allow_non_contiguous_dma(reason="biases as columns, a few hundred elements"))

        def sb(name, shape, dt=fp32):
            return ctx.enter_context(nc.sbuf_tensor(name, shape, dt))

        def sem(name):
            return ctx.enter_context(nc.semaphore(name))

        def sems(name, n=2):
            return [ctx.enter_context(nc.semaphore(f"{name}{i}")) for i in range(n)]

        ident = sb("ident", [128, 128])
        ones_row = sb("ones_row", [1, 128])
        zT = sb("zT", [128, KD, N])
        eps1 = sb("eps1", [128, L + 1])
        half = sb("half", [128, 1])
        tin = sb("tin", [P, 2, D])
        tin2 = sb("tin2", [P, 2, D])
        xn = sb("xn", [P, 2, D + 1])
        pre = sb("pre", [P, 2, D])
        base = sb("base", [P, 2, D])
        res = sb("res", [P, 2, D])
        st = sb("st", [P, 2, 6])
        mv = sb("mv", [P, 2, 2])
        ve = sb("ve", [P, 2])
        rs = sb("rs", [P, 2])
        tTs = sb("tTs", [128, 2, KD, P])
        hmT = sb("hmT", [128, 2, KD, P])
        gT = sb("gT", [128, 2, KF, P])
        wqkv = sb("wqkv", [128, KD, 3 * D])
        bqkv = sb("bqkv", [1, 3 * D])
        bqcol = sb("bqcol", [128, KD])
        fc1 = sb("fc1", [128, KD, F])
        fc2 = sb("fc2", [128, KF, D])
        ngcol = sb("ngcol", [128, KD])
        nbcol = sb("nbcol", [128, KD])
        bf1 = sb("bf1", [128, KF])
        b1p = sb("b1p", [128, KF])
        bf2 = sb("bf2", [P, D])
        Gs = sb("Gs", [128, KD, D + 1])
        grow = sb("grow", [1, D + 1])
        Ts = sb("Ts", [128, KD, D])
        trow = sb("trow", [1, D])
        attn = sb("attn", [128, KD, 128])
        attnT = sb("attnT", [128, KD, 128])
        amax = sb("amax", [128, KD])
        asum = sb("asum", [128, KD])
        arec = sb("arec", [128, KD])
        wqT = sb("wqT", [128, KD, D])
        Mw = sb("Mw", [128, KD, D])
        crow = sb("crow", [1, D])
        cbc = sb("cbc", [P, D])
        W1 = sb("W1", [128, KD, D])
        W2 = sb("W2", [128, KD, D])
        b1c = sb("b1c", [128, KD])
        b2bc = sb("b2bc", [P, D])
        gabc = sb("gabc", [P, D])
        bebc = sb("bebc", [P, D])
        src_sb = sb("src_sb", [P, ET], i32)
        dst_sb = sb("dst_sb", [P, ET], i32)
        dst_f = sb("dst_f", [P, ET])
        idx = sb("idx", [P, 2], i32)
        rows = sb("rows", [P, 2, D])
        rwT = sb("rwT", [128, KD, X])
        lg = sb("lg", [P, NT, X])
        pr = sb("pr", [P, NT, X])
        key = sb("key", [P, NT, X])
        oh1 = sb("oh1", [P, NT, X])
        oh2 = sb("oh2", [P, NT, X])
        rank8 = sb("rank8", [P, NT, X])
        rmax = sb("rmax", [P, NT, 3])
        comb = sb("comb", [P, NT, X])
        cslot = sb("cslot", [P, 2, X])
        combT = sb("combT", [X, 2, P])
        eb1 = sb("eb1", [128, X, KD])
        eb2 = sb("eb2", [X, D])
        arena = sb("arena", [128, 21000])
        tT = arena[:, 0:KD * N].rearrange("p (k n) -> p k n", k=KD)
        acc = arena[0:P, 6400:6400 + NT * D].rearrange("p (t d) -> p t d", t=NT)
        w1e = arena[:, 12800:12800 + X * KD * D].rearrange("p (x k d) -> p x k d", x=X, k=KD)
        w2e = arena[:, 16896:16896 + X * KD * D].rearrange("p (x k d) -> p x k d", x=X, k=KD)
        iota_n = arena[0:P, 0:N]
        onehot = arena[0:P, 3200:3200 + 2 * N].rearrange("p (s n) -> p s n", s=2)

        bank = [ctx.enter_context(nc.psum_tensor(f"bank{i}", [128, 512], fp32)) for i in range(8)]

        s_const, s_wld, s_eps = sem("s_const"), sem("s_wld"), sem("s_eps")
        x_ld = sems("x_ld"); xn_st = sems("xn_st")
        s_bn, s_mv, s_ve, s_rs, s_xn = sem("s_bn"), sem("s_mv"), sem("s_ve"), sem("s_rs"), sem("s_xn")
        s_xT, s_zT, s_G = sem("s_xT"), sem("s_zT"), sem("s_G")
        f_pe, f_dve, f_act = sem("f_pe"), sem("f_dve"), sem("f_act")
        m_ld = sems("m_ld"); m_ldx = sems("m_ldx"); m_st = sems("m_st")
        m_xT, m_xTs, m_xf, m_xb, m_pre = sem("m_xT"), sem("m_xTs"), sem("m_xf"), sem("m_xb"), sem("m_pre")
        m_bn, m_mv, m_ve, m_rs, m_hm = sem("m_bn"), sem("m_mv"), sem("m_ve"), sem("m_rs"), sem("m_hm")
        m_r1, m_res, m_hT, m_hTs, m_f1 = sem("m_r1"), sem("m_res"), sem("m_hT"), sem("m_hTs"), sem("m_f1")
        m_g, m_f2, m_out = sem("m_g"), sem("m_f2"), sem("m_out")
        a_tab, a_iota, a_idx, a_oh, a_mm, a_add = (sem("a_tab"), sem("a_iota"), sem("a_idx"), sem("a_oh"),
                                                   sem("a_mm"), sem("a_add"))
        a_row = sems("a_row")
        l_w = sem("l_w")
        l_ld = sems("l_ld"); l_st = sems("l_st")
        l_m1, l_re, l_m2, l_hb, l_pre = sem("l_m1"), sem("l_re"), sem("l_m2"), sem("l_hb"), sem("l_pre")
        l_bn, l_mv, l_ve, l_rs, l_nrm = sem("l_bn"), sem("l_mv"), sem("l_ve"), sem("l_rs"), sem("l_nrm")
        l_ga, l_be, l_h, l_hT, l_zT = sem("l_ga"), sem("l_be"), sem("l_h"), sem("l_hT"), sem("l_zT")
        e_w = sem("e_w")
        t_ld = sems("t_ld"); t_ld2 = sems("t_ld2")
        t_x2, t_bn, t_mv, t_ve, t_rs, t_t = (sem("t_x2"), sem("t_bn"), sem("t_mv"), sem("t_ve"), sem("t_rs"), sem("t_t"))
        t_acc, t_T, t_Ts, t_cp, t_lg, t_lgs = (sem("t_acc"), sem("t_T"), sem("t_Ts"), sem("t_cp"), sem("t_lg"), sem("t_lgs"))
        r_d, r_a, r_p = sem("r_d"), sem("r_a"), sem("r_p")
        c_sl, c_T, c_Ts, c_b, c_acc = sem("c_sl"), sem("c_T"), sem("c_Ts"), sem("c_b"), sem("c_acc")
        x_m1, x_g, x_m2, x_acc, x_out = sem("x_m1"), sem("x_g"), sem("x_m2"), sem("x_acc"), sem("x_out")

        past = {e.engine: sem(f"past_{n}") for n, e in (('sp', nc.sync), ('pe', nc.tensor), ('dve', nc.vector),
                                                        ('act', nc.scalar), ('pool', nc.gpsimd))}

        x_t = x.rearrange("(t p) d -> t p d", p=P)

        def rows_of(t):
            return bass.ds(t * P, P)

        block = ctx.enter_context(nc.Block())

        def alone(eng):
            eng.sem_inc(past[eng.engine], 1)

        NW = 15
        NE = 6

        @block.sync
        def _(sp):
            sp.dma_start(eps1[:, 0:L], geps.rearrange("(a l) -> a l", a=1).broadcast_to([128, L])).then_inc(s_eps, 16)
            sp.dma_start(wqkv[:, :, :], w_qkv.rearrange("(k p) n -> p k n", p=128)).then_inc(s_wld, 16)
            sp.dma_start(bqkv[:, :], b_qkv.rearrange("(a n) -> a n", a=1)).then_inc(s_wld, 16)
            sp.dma_start(bqcol[:, :], b_qkv[0:D].rearrange("(k p) -> p k", p=128)).then_inc(s_wld, 16)
            sp.dma_start(fc1[:, :, :], w_fc1.rearrange("(k p) n -> p k n", p=128)).then_inc(s_wld, 16)
            sp.dma_start(fc2[:, :, :], w_fc2.rearrange("(k p) n -> p k n", p=128)).then_inc(s_wld, 16)
            sp.dma_start(ngcol[:, :], norm_g.rearrange("(k p) -> p k", p=128)).then_inc(s_wld, 16)
            sp.dma_start(nbcol[:, :], norm_b.rearrange("(k p) -> p k", p=128)).then_inc(s_wld, 16)
            sp.dma_start(bf1[:, :], b_fc1.rearrange("(k p) -> p k", p=128)).then_inc(s_wld, 16)
            sp.dma_start(bf2[:, :], b_fc2.rearrange("(a n) -> a n", a=1).broadcast_to([P, D])).then_inc(s_wld, 16)
            for k in range(KD):
                sp.dma_start(rwT[:, k, :], router_w[:, k * 128:(k + 1) * 128].rearrange("e p -> p e")).then_inc(s_wld, 16)
                sp.dma_start(eb1[:, :, k], e_b1[:, k * 128:(k + 1) * 128].rearrange("e p -> p e")).then_inc(s_wld, 16)
            sp.dma_start(eb2[:, :], e_b2).then_inc(s_wld, 16)
            sp.dma_start(src_sb[:, :], src.rearrange("(p t) -> p t", p=P)).then_inc(s_wld, 16)
            sp.dma_start(dst_sb[:, :], dst.rearrange("(p t) -> p t", p=P)).then_inc(a_tab, 16)

            def load_x(t, s, turn):
                if not (isinstance(t, int) and t < 2):
                    sp.wait_ge(s_xn, t - 1)
                sp.dma_start(tin[:, s, :], x[rows_of(t), :]).then_inc(x_ld[s], 16)

            def store_xn(t, s, turn):
                sp.wait_ge(s_xn, t + 1)
                sp.dma_start(h_dram[rows_of(t), :], xn[:, s, 0:D]).then_inc(xn_st[s], 16)

            pipelined(sp, [(0, load_x), (2, store_xn)], NT)

            sp.wait_ge(xn_st[0], 16 * (NT - NT // 2))
            sp.wait_ge(xn_st[1], 16 * (NT // 2))

            def load_mix(t, s, turn):
                if not (isinstance(t, int) and t < 2):
                    sp.wait_ge(m_xb, t - 1)
                    sp.wait_ge(m_xT, t - 1)
                    sp.wait_ge(m_res, t - 1)
                sp.dma_start(tin[:, s, :], h_dram[rows_of(t), :]).then_inc(m_ld[s], 16)
                sp.dma_start(tin2[:, s, :], x[rows_of(t), :]).then_inc(m_ldx[s], 16)

            def store_mix(t, s, turn):
                sp.wait_ge(m_out, t + 1)
                sp.dma_start(acc_dram[rows_of(t), :], pre[:, s, :]).then_inc(m_st[s], 16)

            pipelined(sp, [(0, load_mix), (3, store_mix)], NT)
            sp.wait_ge(m_st[0], 16 * (NT - NT // 2))
            sp.wait_ge(m_st[1], 16 * (NT // 2))

            with sp.Fori(0, L) as l:
                sp.wait_ge(l_zT, l * NT)
                sp.wait_ge(l_h, l * NT)
                sp.dma_start(W1[:, :, :], gW1[bass.ds(l, 1), :, :].rearrange("a (k p) n -> p (a k) n", p=128)).then_inc(l_w, 16)
                sp.dma_start(W2[:, :, :], gW2[bass.ds(l, 1), :, :].rearrange("a (k p) n -> p (a k) n", p=128)).then_inc(l_w, 16)
                sp.dma_start(b1c[:, :], gb1[bass.ds(l, 1), :].rearrange("a (k p) -> p (a k)", p=128)).then_inc(l_w, 16)
                sp.dma_start(b2bc[:, :], gb2[bass.ds(l, 1), :].broadcast_to([P, D])).then_inc(l_w, 16)
                sp.dma_start(gabc[:, :], ggamma[bass.ds(l, 1), :].broadcast_to([P, D])).then_inc(l_w, 16)
                sp.dma_start(bebc[:, :], gbeta[bass.ds(l, 1), :].broadcast_to([P, D])).then_inc(l_w, 16)

                def load_h(t, s, turn):
                    if not (isinstance(t, int) and t < 2):
                        sp.wait_ge(l_hb, l * NT + t - 1)
                    sp.dma_start(tin[:, s, :], h_dram[rows_of(t), :]).then_inc(l_ld[s], 16)

                def store_h(t, s, turn):
                    sp.wait_ge(l_h, l * NT + t + 1)
                    sp.dma_start(h_dram[rows_of(t), :], res[:, s, :]).then_inc(l_st[s], 16)

                sp.wait_ge(a_add, (l + 1) * KD)
                pipelined(sp, [(0, load_h), (2, store_h)], NT)
                sp.wait_ge(l_st[0], 16 * (NT - NT // 2) * (l + 1))
                alone(sp)
                sp.wait_ge(l_st[1], 16 * (NT // 2) * (l + 1))
                alone(sp)

            for x0 in range(0, X, X // 2):
                sp.dma_start(w1e[:, x0:x0 + X // 2, :, :].rearrange("p x k d -> p (x k) d"),
                             e_w1[x0:x0 + X // 2, :, :].rearrange("x (k p) d -> p (x k) d", p=128)).then_inc(e_w, 16)
                sp.dma_start(w2e[:, x0:x0 + X // 2, :, :].rearrange("p x k d -> p (x k) d"),
                             e_w2[x0:x0 + X // 2, :, :].rearrange("x (k p) d -> p (x k) d", p=128)).then_inc(e_w, 16)

            def load_t(t, s, turn):
                if not (isinstance(t, int) and t < 2):
                    sp.wait_ge(t_x2, t - 1)
                sp.dma_start(tin[:, s, :], h_dram[rows_of(t), :]).then_inc(t_ld[s], 16)
                sp.dma_start(tin2[:, s, :], acc_dram[rows_of(t), :]).then_inc(t_ld2[s], 16)

            pipelined(sp, [(0, load_t)], NT)

            def store_out(t, s, turn):
                sp.wait_ge(x_acc, X * (t + 1))
                sp.dma_start(out[rows_of(t), :], acc[:, bass.ds(t, 1), :].rearrange("p a d -> p (a d)")).then_inc(x_out, 16)

            pipelined(sp, [(0, store_out)], NT)
            sp.wait_ge(x_out, 16 * NT)

        @block.tensor
        def _(pe):
            mm = nc.tensor.matmul
            pe.wait_ge(s_const, 5)

            def first(t):
                return isinstance(t, int) and t == 0

            def last(t):
                return isinstance(t, int) and t == NT - 1

            def norm_x(t, s, turn):
                pe.wait_ge(s_xn, t + 1)
                if not (isinstance(t, int) and t < 2):
                    pe.wait_ge(s_zT, t - 1)
                for k in range(KD):
                    i = nc.tensor.transpose(bank[s][:, k * P:(k + 1) * P], xn[:, s, k * 128:(k + 1) * 128], ident[0:P, 0:P])
                i.then_inc(s_xT, 1)
                for k in range(KD):
                    i = mm(bank[2 + k][:, 0:D + 1], lhsT=xn[:, s, k * 128:(k + 1) * 128], rhs=xn[:, s, :],
                           start=first(t), stop=last(t))
                i.then_inc(s_G, 1)

            pipelined(pe, [(0, norm_x)], NT)

            pe.wait_ge(s_wld, 16 * NW)
            pe.wait_ge(s_zT, NT)
            pe.wait_ge(f_dve, 1)
            for k in range(KD):
                i = mm(bank[4][0:1, k * 128:(k + 1) * 128], lhsT=Gs[:, k, D:D + 1], rhs=ident[:, :], start=True, stop=True)
            i.then_inc(f_pe, 1)
            for k in range(KD):
                for a in range(KD):
                    i = nc.tensor.transpose(bank[5][:, (a * KD + k) * 128:(a * KD + k + 1) * 128],
                                            wqkv[:, k, a * 128:(a + 1) * 128], ident[:, :])
            i.then_inc(f_pe, 1)
            for m in range(KF):
                for k in range(KD):
                    i = mm(bank[6][:, m:m + 1], lhsT=fc1[:, k, m * 128:(m + 1) * 128], rhs=nbcol[:, k:k + 1],
                           start=(k == 0), stop=(k == KD - 1))
            i.then_inc(f_pe, 1)
            pe.wait_ge(f_dve, 2)
            for m in range(KD + 1):
                cols = slice(m * 128, (m + 1) * 128) if m < KD else slice(D, D + 1)
                o = bank[m][:, 0:D] if m < KD else bank[4][0:1, 0:D]
                for k in range(KD):
                    mm(o, lhsT=Gs[:, k, cols], rhs=wqkv[:, k, 2 * D:3 * D], start=(k == 0), stop=False)
                i = mm(o, lhsT=grow[0:1, cols], rhs=bqkv[0:1, 2 * D:3 * D], start=False, stop=True)
            i.then_inc(f_pe, 1)
            pe.wait_ge(f_dve, 5)
            for a in range(KD):
                for k in range(KD):
                    mm(bank[7][:, a * 128:(a + 1) * 128], lhsT=wqkv[:, k, D + a * 128:D + (a + 1) * 128],
                       rhs=Ts[:, k, a * 128:(a + 1) * 128], start=(k == 0), stop=False)
                i = mm(bank[7][:, a * 128:(a + 1) * 128], lhsT=bqkv[0:1, D + a * 128:D + (a + 1) * 128],
                       rhs=trow[0:1, a * 128:(a + 1) * 128], start=False, stop=True)
            i.then_inc(f_pe, 1)
            pe.wait_ge(f_dve, 7)
            for a in range(KD):
                i = nc.tensor.transpose(bank[5][:, a * 128:(a + 1) * 128], attn[:, a, :], ident[:, :])
            i.then_inc(f_pe, 1)
            pe.wait_ge(f_dve, 8)
            for m in range(KD):
                for a in range(KD):
                    mm(bank[m][:, a * 128:(a + 1) * 128], lhsT=wqT[:, a, m * 128:(m + 1) * 128], rhs=attnT[:, a, :],
                       start=True, stop=True)
            for a in range(KD):
                i = mm(bank[4][0:1, a * 128:(a + 1) * 128], lhsT=bqcol[:, a:a + 1], rhs=attnT[:, a, :], start=True, stop=True)
            i.then_inc(f_pe, 1)
            pe.wait_ge(f_dve, 9)
            mm(bank[6][0:P, 0:D], lhsT=ones_row[0:1, 0:P], rhs=crow[0:1, :], start=True, stop=True).then_inc(f_pe, 1)
            pe.wait_ge(f_dve, 10)

            def mix_T(t, s, turn):
                pe.wait_ge(m_ld[s], 16 * (turn + 1))
                if not (isinstance(t, int) and t == 0):
                    pe.wait_ge(m_xTs, t)
                for k in range(KD):
                    i = nc.tensor.transpose(bank[0][:, k * P:(k + 1) * P], tin[:, s, k * 128:(k + 1) * 128], ident[0:P, 0:P])
                i.then_inc(m_xT, 1)

            def mix_xf(t, s, turn):
                pe.wait_ge(m_xTs, t + 1)
                if not (isinstance(t, int) and t == 0):
                    pe.wait_ge(m_pre, t)
                for k in range(KD):
                    i = mm(bank[2][0:P, 0:D], lhsT=tTs[:, s, k, :], rhs=Mw[:, k, :], start=(k == 0), stop=(k == KD - 1))
                i.then_inc(m_xf, 1)

            def mix_hT(t, s, turn):
                pe.wait_ge(m_hm, t + 1)
                if not (isinstance(t, int) and t == 0):
                    pe.wait_ge(m_hTs, t)
                for k in range(KD):
                    i = nc.tensor.transpose(bank[1][:, k * P:(k + 1) * P], xn[:, s, k * 128:(k + 1) * 128], ident[0:P, 0:P])
                i.then_inc(m_hT, 1)

            def mix_f1(t, s, turn):
                pe.wait_ge(m_hTs, t + 1)
                if not (isinstance(t, int) and t < 2):
                    pe.wait_ge(m_g, t - 1)
                for m in range(KF):
                    o = bank[4 + 2 * s + m // 4][:, m % 4 * P:(m % 4 + 1) * P]
                    for k in range(KD):
                        i = mm(o, lhsT=fc1[:, k, m * 128:(m + 1) * 128], rhs=hmT[:, s, k, :], start=(k == 0), stop=(k == KD - 1))
                i.then_inc(m_f1, 1)

            def mix_f2(t, s, turn):
                pe.wait_ge(m_g, t + 1)
                if not (isinstance(t, int) and t == 0):
                    pe.wait_ge(m_out, t)
                for k in range(KF):
                    i = mm(bank[3][0:P, 0:D], lhsT=gT[:, s, k, :], rhs=fc2[:, k, :], start=(k == 0), stop=(k == KF - 1))
                i.then_inc(m_f2, 1)

            pipelined(pe, [(0, mix_T), (0, mix_xf), (1, mix_hT), (1, mix_f1), (2, mix_f2)], NT)
            pe.wait_ge(m_out, NT)

            with pe.Fori(0, L) as l:
                for f in range(KD):
                    def agg(t, s, turn):
                        pe.wait_ge(a_row[s], 16 * ((l * KD + f) * (ET // 2) + turn + 1))
                        pe.wait_ge(a_oh, (l * KD + f) * ET + t + 1)
                        for c in range(NC):
                            w = min(CH, N - c * CH)
                            i = mm(bank[c][:, 0:w], lhsT=rows[:, s, f * 128:(f + 1) * 128], rhs=onehot[:, s, c * CH:c * CH + w],
                                   start=(isinstance(t, int) and t == 0), stop=(isinstance(t, int) and t == ET - 1))
                        i.then_inc(a_mm, 1)

                    pe.wait_ge(a_add, l * KD + f)
                    pe.wait_ge(l_zT, l * NT)
                    agg(0, 0, 0)
                    agg(1, 1, 0)
                    with pe.Fori(1, ET // 2 - 1) as turn:
                        agg(2 * turn, 0, turn)
                        agg(2 * turn + 1, 1, turn)
                    agg(ET - 2, 0, ET // 2 - 1)
                    agg(ET - 1, 1, ET // 2 - 1)

                pe.wait_ge(a_add, (l + 1) * KD)
                pe.wait_ge(l_w, (l + 1) * 96)

                def mlp1(t, s, turn):
                    if not (isinstance(t, int) and t < 2):
                        pe.wait_ge(l_re, l * NT + t - 1)
                    for m in range(KD):
                        for k in range(KD):
                            i = mm(bank[s][:, m * P:(m + 1) * P], lhsT=W1[:, k, m * 128:(m + 1) * 128],
                                   rhs=zT[:, k, rows_of(t)], start=(k == 0), stop=(k == KD - 1))
                    i.then_inc(l_m1, 1)

                def mlp2(t, s, turn):
                    pe.wait_ge(l_re, l * NT + t + 1)
                    if not (isinstance(t, int) and t < 2):
                        pe.wait_ge(l_pre, l * NT + t - 1)
                    for k in range(KD):
                        i = mm(bank[2 + s][0:P, 0:D], lhsT=tTs[:, s, k, :], rhs=W2[:, k, :], start=(k == 0), stop=(k == KD - 1))
                    i.then_inc(l_m2, 1)

                def h_T(t, s, turn):
                    pe.wait_ge(l_h, l * NT + t + 1)
                    if not (isinstance(t, int) and t < 2):
                        pe.wait_ge(l_zT, l * NT + t - 1)
                    for k in range(KD):
                        i = nc.tensor.transpose(bank[4 + s][:, k * P:(k + 1) * P], res[:, s, k * 128:(k + 1) * 128], ident[0:P, 0:P])
                    i.then_inc(l_hT, 1)

                pipelined(pe, [(0, mlp1), (1, mlp2), (3, h_T)], NT)
                pe.wait_ge(l_zT, (l + 1) * NT)

            def tok_T(t, s, turn):
                pe.wait_ge(t_t, t + 1)
                if not (isinstance(t, int) and t < 2):
                    pe.wait_ge(t_Ts, t - 1)
                for k in range(KD):
                    i = nc.tensor.transpose(bank[s][:, k * P:(k + 1) * P], xn[:, s, k * 128:(k + 1) * 128], ident[0:P, 0:P])
                i.then_inc(t_T, 1)

            def tok_lg(t, s, turn):
                pe.wait_ge(t_Ts, t + 1)
                if not (isinstance(t, int) and t < 2):
                    pe.wait_ge(t_lgs, t - 1)
                for k in range(KD):
                    i = mm(bank[2 + s][0:P, 0:X], lhsT=tTs[:, s, k, :], rhs=rwT[:, k, :], start=(k == 0), stop=(k == KD - 1))
                i.then_inc(t_lg, 1)

            pipelined(pe, [(0, tok_T), (1, tok_lg)], NT)

            def cmb_T(t, s, turn):
                pe.wait_ge(c_sl, t + 1)
                if not (isinstance(t, int) and t < 2):
                    pe.wait_ge(c_Ts, t - 1)
                nc.tensor.transpose(bank[4 + s][0:X, 0:P], cslot[:, s, :], ident[0:P, 0:P]).then_inc(c_T, 1)

            def cmb_b(t, s, turn):
                pe.wait_ge(c_Ts, t + 1)
                if not (isinstance(t, int) and t < 2):
                    pe.wait_ge(c_acc, t - 1)
                mm(bank[6 + s][0:P, 0:D], lhsT=combT[:, s, :], rhs=eb2[:, :], start=True, stop=True).then_inc(c_b, 1)

            pipelined(pe, [(0, cmb_T), (1, cmb_b)], NT)

            pe.wait_ge(e_w, 64)
            pe.wait_ge(t_cp, NT)

            def exp1(t, e, n):
                s = e % 2
                if not (isinstance(t, int) and t < 2):
                    pe.wait_ge(x_g, t - 1)
                for m in range(KD):
                    for k in range(KD):
                        i = mm(bank[s][:, m * P:(m + 1) * P], lhsT=w1e[:, e, k, m * 128:(m + 1) * 128],
                               rhs=tT[:, k, rows_of(n)], start=(k == 0), stop=(k == KD - 1))
                i.then_inc(x_m1, 1)

            def exp2(t, e, n):
                s = e % 2
                pe.wait_ge(x_g, t + 1)
                if not (isinstance(t, int) and t < 2):
                    pe.wait_ge(x_acc, t - 1)
                for k in range(KD):
                    i = mm(bank[2 + s][0:P, 0:D], lhsT=gT[:, s, k, :], rhs=w2e[:, e, k, :], start=(k == 0), stop=(k == KD - 1))
                i.then_inc(x_m2, 1)

            pipelined(pe, [(0, exp1), (1, exp2)], NT * X, unroll=X)

        @block.vector
        def _(dve):
            v = nc.vector
            v.memset(xn[:, :, D:D + 1], 1.0).then_inc(s_const, 1)
            v.memset(grow[0:1, D:D + 1], float(N)).then_inc(s_const, 1)
            dve.wait_ge(s_eps, 17)
            v.tensor_scalar(eps1[:, :], eps1[:, :], 1.0, None, ALU.add).then_inc(s_const, 1)
            dve.wait_ge(a_tab, 16)
            v.tensor_copy(dst_f[:, :], dst_sb[:, :]).then_inc(a_tab, 1)

            def stats(t, s, turn):
                dve.wait_ge(x_ld[s], 16 * (turn + 1))
                v.bn_stats(st[:, s, :], tin[:, s, :]).then_inc(s_bn, 1)
                dve.wait_ge(s_bn, t + 1)
                alone(dve)
                v.bn_aggr(mv[:, s, :], st[:, s, :]).then_inc(s_mv, 1)

            def norm(t, s, turn):
                dve.wait_ge(s_rs, t + 1)
                if not (isinstance(t, int) and t < 2):
                    dve.wait_ge(s_G, t - 1)
                    dve.wait_ge(xn_st[s], 16 * turn)
                v.tensor_scalar(xn[:, s, 0:D], tin[:, s, :], mv[:, s, 0:1], rs[:, s:s + 1], ALU.subtract, ALU.mult).then_inc(s_xn, 1)

            dve.wait_ge(s_const, 5)
            pipelined(dve, [(0, stats), (1, norm)], NT)

            dve.wait_ge(s_G, NT)
            for k in range(KD):
                i = v.tensor_copy(Gs[:, k, :], bank[2 + k][:, 0:D + 1])
            i.then_inc(f_dve, 1)
            dve.wait_ge(f_pe, 1)
            v.tensor_copy(grow[0:1, 0:D], bank[4][0:1, 0:D]).then_inc(f_dve, 1)
            dve.wait_ge(f_pe, 2)
            v.tensor_copy(wqT[:, :, :].rearrange("p a c -> p (a c)"), bank[5][:, 0:KD * D]).then_inc(f_dve, 1)
            dve.wait_ge(f_pe, 3)
            v.tensor_tensor(b1p[:, :], bank[6][:, 0:KF], bf1[:, :], ALU.add)
            for k in range(KD):
                i = v.tensor_scalar(fc1[:, k, :], fc1[:, k, :], ngcol[:, k:k + 1], None, ALU.mult)
            v.memset(attn[:, :, :], 0.0).then_inc(f_dve, 1)
            dve.wait_ge(f_pe, 4)
            for m in range(KD):
                v.tensor_copy(Ts[:, m, :], bank[m][:, 0:D])
            v.tensor_copy(trow[0:1, :], bank[4][0:1, 0:D]).then_inc(f_dve, 1)
            dve.wait_ge(f_pe, 5)
            for a in range(KD):
                for hh in range(2):
                    r = slice(hh * HD, (hh + 1) * HD)
                    i = v.reduce_max(amax[r, a:a + 1], bank[7][r, a * 128 + hh * HD:a * 128 + (hh + 1) * HD], AX.X)
            i.then_inc(r_d, 1)
            dve.wait_ge(r_d, 1)
            v.tensor_scalar(amax[:, :], amax[:, :], -float(HD) ** -0.5, None, ALU.mult).then_inc(f_dve, 1)
            dve.wait_ge(f_act, 1)
            v.reciprocal(arec[:, :], asum[:, :]).then_inc(r_d, 1)
            dve.wait_ge(r_d, 2)
            for a in range(KD):
                i = v.tensor_scalar(attn[:, a, :], attn[:, a, :], arec[:, a:a + 1], None, ALU.mult)
            i.then_inc(f_dve, 1)
            dve.wait_ge(f_pe, 6)
            v.tensor_copy(attnT[:, :, :].rearrange("p a c -> p (a c)"), bank[5][:, 0:D]).then_inc(f_dve, 1)
            dve.wait_ge(f_pe, 7)
            for m in range(KD):
                v.tensor_copy(Mw[:, m, :], bank[m][:, 0:D])
            v.tensor_copy(crow[0:1, :], bank[4][0:1, 0:D]).then_inc(f_dve, 1)
            dve.wait_ge(f_pe, 8)
            v.tensor_copy(cbc[:, :], bank[6][0:P, 0:D]).then_inc(f_dve, 1)

            def mix_pre(t, s, turn):
                dve.wait_ge(m_xf, t + 1)
                dve.wait_ge(m_xb, t + 1)
                if not (isinstance(t, int) and t < 2):
                    dve.wait_ge(m_st[s], 16 * turn)
                v.tensor_tensor(pre[:, s, :], bank[2][0:P, 0:D], base[:, s, :], ALU.add).then_inc(m_pre, 1)
                dve.wait_ge(m_pre, t + 1)
                v.bn_stats(st[:, s, :], pre[:, s, :]).then_inc(m_bn, 1)
                dve.wait_ge(m_bn, t + 1)
                alone(dve)
                v.bn_aggr(mv[:, s, :], st[:, s, :]).then_inc(m_mv, 1)

            def mix_norm(t, s, turn):
                dve.wait_ge(m_rs, t + 1)
                if not (isinstance(t, int) and t < 2):
                    dve.wait_ge(m_hT, t - 1)
                v.tensor_scalar(xn[:, s, 0:D], pre[:, s, :], mv[:, s, 0:1], rs[:, s:s + 1], ALU.subtract, ALU.mult).then_inc(m_hm, 1)

            def mix_out(t, s, turn):
                dve.wait_ge(m_f2, t + 1)
                dve.wait_ge(m_res, t + 1)
                v.tensor_tensor(pre[:, s, :], bank[3][0:P, 0:D], res[:, s, :], ALU.add).then_inc(m_out, 1)

            pipelined(dve, [(2, mix_out), (0, mix_pre), (0, mix_norm)], NT)

            with dve.Fori(0, L) as l:
                dve.wait_ge(a_iota, l + 1)
                for f in range(KD):
                    def one(t, s, turn):
                        if not (isinstance(t, int) and t < 2):
                            dve.wait_ge(a_mm, (l * KD + f) * ET + t - 1)
                        v.tensor_scalar(onehot[:, s, :], iota_n, dst_f[:, bass.ds(t, 1)], None, ALU.is_equal).then_inc(a_oh, 1)

                    if f:
                        dve.wait_ge(a_mm, (l * KD + f) * ET)
                    pipelined(dve, [(0, one)], ET)
                    dve.wait_ge(a_mm, (l * KD + f + 1) * ET)
                    for c in range(NC):
                        w = min(CH, N - c * CH)
                        i = v.tensor_tensor(zT[:, f, c * CH:c * CH + w], zT[:, f, c * CH:c * CH + w], bank[c][:, 0:w], ALU.add)
                    i.then_inc(a_add, 1)

                def pre_ln(t, s, turn):
                    dve.wait_ge(l_m2, l * NT + t + 1)
                    dve.wait_ge(l_hb, l * NT + t + 1)
                    if not (isinstance(t, int) and t < 2):
                        dve.wait_ge(l_nrm, l * NT + t - 1)
                    v.tensor_tensor(pre[:, s, :], bank[2 + s][0:P, 0:D], base[:, s, :], ALU.add).then_inc(l_pre, 1)
                    dve.wait_ge(l_pre, l * NT + t + 1)
                    v.bn_stats(st[:, s, :], pre[:, s, :]).then_inc(l_bn, 1)
                    dve.wait_ge(l_bn, l * NT + t + 1)
                    alone(dve)
                    v.bn_aggr(mv[:, s, :], st[:, s, :]).then_inc(l_mv, 1)

                def ln(t, s, turn):
                    dve.wait_ge(l_rs, l * NT + t + 1)
                    if not (isinstance(t, int) and t < 2):
                        dve.wait_ge(l_h, l * NT + t - 1)
                    v.tensor_scalar(xn[:, s, 0:D], pre[:, s, :], mv[:, s, 0:1], rs[:, s:s + 1], ALU.subtract, ALU.mult).then_inc(l_nrm, 1)

                pipelined(dve, [(0, pre_ln), (1, ln)], NT)

            def tok_st(t, s, turn):
                dve.wait_ge(t_x2, t + 1)
                v.bn_stats(st[:, s, :], pre[:, s, :]).then_inc(t_bn, 1)
                dve.wait_ge(t_bn, t + 1)
                alone(dve)
                v.bn_aggr(mv[:, s, :], st[:, s, :]).then_inc(t_mv, 1)

            def tok_n(t, s, turn):
                dve.wait_ge(t_rs, t + 1)
                if not (isinstance(t, int) and t < 2):
                    dve.wait_ge(t_T, t - 1)
                    dve.wait_ge(t_acc, t - 1)
                v.tensor_scalar(xn[:, s, 0:D], pre[:, s, :], mv[:, s, 0:1], rs[:, s:s + 1], ALU.subtract, ALU.mult).then_inc(t_t, 1)

            def tok_l(t, s, turn):
                dve.wait_ge(t_lg, t + 1)
                v.tensor_copy(lg[:, bass.ds(t, 1), :].rearrange("p a x -> p (a x)"), bank[2 + s][0:P, 0:X]).then_inc(t_lgs, 1)

            pipelined(dve, [(0, tok_st), (1, tok_n), (3, tok_l)], NT)

            n_r = [2]

            def done(i):
                n_r[0] += 1
                i.then_inc(r_d, 1)
                dve.wait_ge(r_d, n_r[0])

            def wide(k):
                return rmax[:, :, k:k + 1].broadcast_to([P, NT, X])

            def choose(oh):
                done(v.reduce_max(rmax[:, :, 1:2], key[:, :, :], AX.X))
                done(v.tensor_tensor(oh[:, :, :], key[:, :, :], wide(1), ALU.is_ge))
                done(v.tensor_tensor(oh[:, :, :], oh[:, :, :], rank8[:, :, :], ALU.mult))
                done(v.reduce_max(rmax[:, :, 2:3], oh[:, :, :], AX.X))
                done(v.tensor_tensor(oh[:, :, :], oh[:, :, :], wide(2), ALU.is_equal))

            dve.wait_ge(t_lgs, NT)
            for e in range(X):
                i = v.memset(rank8[:, :, e:e + 1], float(X - e))
            done(i)
            done(v.reduce_max(rmax[:, :, 0:1], lg[:, :, :], AX.X))
            done(v.tensor_tensor(lg[:, :, :], lg[:, :, :], wide(0), ALU.subtract))
            dve.wait_ge(r_a, 1)
            done(v.reduce_sum(rmax[:, :, 0:1], pr[:, :, :], AX.X))
            done(v.reciprocal(rmax[:, :, 0:1], rmax[:, :, 0:1]))
            done(v.tensor_tensor(pr[:, :, :], pr[:, :, :], wide(0), ALU.mult))
            done(v.tensor_copy(key[:, :, :], pr[:, :, :]))
            choose(oh1)
            done(v.scalar_tensor_tensor(key[:, :, :], oh1[:, :, :], -2.0, key[:, :, :], ALU.mult, ALU.add))
            choose(oh2)
            done(v.tensor_tensor(oh1[:, :, :], oh1[:, :, :], oh2[:, :, :], ALU.add))
            done(v.tensor_tensor(pr[:, :, :], pr[:, :, :], oh1[:, :, :], ALU.mult))
            done(v.reduce_sum(rmax[:, :, 0:1], pr[:, :, :], AX.X))
            done(v.tensor_scalar(rmax[:, :, 0:1], rmax[:, :, 0:1], 1e-12, None, ALU.max))
            done(v.reciprocal(rmax[:, :, 0:1], rmax[:, :, 0:1]))
            v.tensor_tensor(comb[:, :, :], pr[:, :, :], wide(0), ALU.mult).then_inc(r_p, 1)

            def cmb_cp(t, s, turn):
                dve.wait_ge(c_T, t + 1)
                if not (isinstance(t, int) and t < 2):
                    dve.wait_ge(c_b, t - 1)
                v.tensor_copy(combT[:, s, :], bank[4 + s][0:X, 0:P]).then_inc(c_Ts, 1)

            def acc_of(t):
                return acc[:, bass.ds(t, 1), :].rearrange("p a d -> p (a d)")

            def cmb_acc(t, s, turn):
                dve.wait_ge(c_b, t + 1)
                v.tensor_tensor(acc_of(t), acc_of(t), bank[6 + s][0:P, 0:D], ALU.add).then_inc(c_acc, 1)

            dve.wait_ge(t_acc, NT)
            pipelined(dve, [(0, cmb_cp), (1, cmb_acc)], NT)

            dve.wait_ge(c_acc, NT)
            dve.wait_ge(r_p, 1)

            def exp_acc(t, e, n):
                s = e % 2
                dve.wait_ge(x_m2, t + 1)
                if not (isinstance(t, int) and t == 0):
                    dve.wait_ge(x_acc, t)
                v.scalar_tensor_tensor(acc_of(n), bank[2 + s][0:P, 0:D],
                                       comb[:, bass.ds(n, 1), e:e + 1].rearrange("p a x -> p (a x)"),
                                       acc_of(n), ALU.mult, ALU.add).then_inc(x_acc, 1)

            pipelined(dve, [(0, exp_acc)], NT * X, unroll=X)

        @block.scalar
        def _(act):
            a = nc.scalar
            act.wait_ge(s_const, 5)

            def z0(t, s, turn):
                act.wait_ge(s_xT, t + 1)
                alone(act)
                a.activation(zT[:, :, rows_of(t)], bank[s][:, 0:KD * P].rearrange("p (k n) -> p k n", k=KD), ACT.Copy,
                             scale=eps1[:, 0:1]).then_inc(s_zT, 1)

            pipelined(act, [(0, z0)], NT)
            act.wait_ge(f_dve, 6)
            for b in range(KD):
                for hh in range(2):
                    r = slice(hh * HD, (hh + 1) * HD)
                    i = a.activation(attn[r, b, r], bank[7][r, b * 128 + hh * HD:b * 128 + (hh + 1) * HD], ACT.Exp,
                                     bias=amax[r, b:b + 1], scale=float(HD) ** -0.5, accum_out=asum[r, b:b + 1])
            i.then_inc(f_act, 1)

            def mix_xTs(t, s, turn):
                act.wait_ge(m_xT, t + 1)
                if not (isinstance(t, int) and t < 2):
                    act.wait_ge(m_xf, t - 1)
                a.activation(tTs[:, s, :, :], bank[0][:, 0:KD * P].rearrange("p (k n) -> p k n", k=KD), ACT.Copy).then_inc(m_xTs, 1)

            def mix_hTs(t, s, turn):
                act.wait_ge(m_hT, t + 1)
                if not (isinstance(t, int) and t < 2):
                    act.wait_ge(m_f1, t - 1)
                a.activation(hmT[:, s, :, :], bank[1][:, 0:KD * P].rearrange("p (k n) -> p k n", k=KD), ACT.Copy).then_inc(m_hTs, 1)

            def mix_gelu(t, s, turn):
                act.wait_ge(m_f1, t + 1)
                if not (isinstance(t, int) and t < 2):
                    act.wait_ge(m_f2, t - 1)
                for m in range(KF):
                    i = a.activation(gT[:, s, m, :], bank[4 + 2 * s + m // 4][:, m % 4 * P:(m % 4 + 1) * P], ACT.Gelu,
                                     bias=b1p[:, m:m + 1])
                i.then_inc(m_g, 1)

            pipelined(act, [(0, mix_xTs), (1, mix_hTs), (1, mix_gelu)], NT)

            with act.Fori(0, L) as l:
                act.wait_ge(l_w, 96 * (l + 1))

                def relu1(t, s, turn):
                    act.wait_ge(l_m1, l * NT + t + 1)
                    if not (isinstance(t, int) and t < 2):
                        act.wait_ge(l_m2, l * NT + t - 1)
                    for m in range(KD):
                        i = a.activation(tTs[:, s, m, :], bank[s][:, m * P:(m + 1) * P], ACT.Relu, bias=b1c[:, m:m + 1])
                    i.then_inc(l_re, 1)

                def relu2(t, s, turn):
                    act.wait_ge(l_be, l * NT + t + 1)
                    if not (isinstance(t, int) and t < 2):
                        act.wait_ge(l_hT, l * NT + t - 1)
                        act.wait_ge(l_st[s], 16 * (l * ((NT + 1 - s) // 2) + turn))
                    a.activation(res[:, s, :], xn[:, s, 0:D], ACT.Relu).then_inc(l_h, 1)

                def z_next(t, s, turn):
                    act.wait_ge(l_hT, l * NT + t + 1)
                    alone(act)
                    a.activation(zT[:, :, rows_of(t)], bank[4 + s][:, 0:KD * P].rearrange("p (k n) -> p k n", k=KD), ACT.Copy,
                                 scale=eps1[:, bass.ds(l + 1, 1)]).then_inc(l_zT, 1)

                pipelined(act, [(0, relu1), (2, relu2), (3, z_next)], NT)

            def tok_Ts(t, s, turn):
                act.wait_ge(t_T, t + 1)
                if not (isinstance(t, int) and t < 2):
                    act.wait_ge(t_lg, t - 1)
                    act.wait_ge(t_cp, t - 1)
                a.activation(tTs[:, s, :, :], bank[s][:, 0:KD * P].rearrange("p (k n) -> p k n", k=KD), ACT.Copy).then_inc(t_Ts, 1)

            pipelined(act, [(0, tok_Ts)], NT)
            act.wait_ge(r_d, 5)
            a.activation(pr[:, :, :], lg[:, :, :], ACT.Exp).then_inc(r_a, 1)

            act.wait_ge(s_wld, 16 * NW)

            def exp_g(t, e, n):
                s = e % 2
                act.wait_ge(x_m1, t + 1)
                if not (isinstance(t, int) and t < 2):
                    act.wait_ge(x_m2, t - 1)
                for m in range(KD):
                    i = a.activation(gT[:, s, m, :], bank[s][:, m * P:(m + 1) * P], ACT.Gelu, bias=eb1[:, e, m:m + 1])
                i.then_inc(x_g, 1)

            pipelined(act, [(0, exp_g)], NT * X, unroll=X)

        @block.gpsimd
        def _(pool):
            g = nc.gpsimd
            g.memset(eps1[:, L:L + 1], 0.0).then_inc(s_eps, 1)
            g.memset(half[:, :], -0.5).then_inc(s_const, 1)
            g.memset(ones_row[:, :], 1.0)
            g.memset(ident[:, :], 0.0).then_inc(a_idx, 1)
            pool.wait_ge(a_idx, 1)
            g.affine_select(out=ident[:, :], in_=ident[:, :], compare_op=ALU.not_equal, fill=1.0, base=0,
                            pattern=[[-1, 128]], channel_multiplier=1).then_inc(s_const, 1)
            pool.wait_ge(s_const, 5)

            def rsqrt(s, begin, mid, mid_n, end):
                alone(pool)
                g.tensor_scalar(ve[:, s:s + 1], mv[:, s, 1:2], EPS, None, ALU.add).then_inc(mid, 1)
                pool.wait_ge(mid, mid_n)
                g.tensor_tensor(rs[:, s:s + 1], ve[:, s:s + 1], half[0:P, :], ALU.pow).then_inc(end, 1)

            def norm_rs(t, s, turn):
                pool.wait_ge(s_mv, t + 1)
                rsqrt(s, s_mv, s_ve, t + 1, s_rs)

            pipelined(pool, [(0, norm_rs)], NT)
            pool.wait_ge(f_dve, 10)
            pool.wait_ge(s_wld, 16 * NW)

            def mix_xb(t, s, turn):
                pool.wait_ge(m_ld[s], 16 * (turn + 1))
                if not (isinstance(t, int) and t < 2):
                    pool.wait_ge(m_pre, t - 1)
                g.tensor_tensor(base[:, s, :], tin[:, s, :], cbc[:, :], ALU.add).then_inc(m_xb, 1)

            def mix_rs(t, s, turn):
                pool.wait_ge(m_mv, t + 1)
                rsqrt(s, m_mv, m_ve, t + 1, m_rs)

            def mix_res(t, s, turn):
                pool.wait_ge(m_ldx[s], 16 * (turn + 1))
                if not (isinstance(t, int) and t < 2):
                    pool.wait_ge(m_out, t - 1)
                g.tensor_tensor(res[:, s, :], pre[:, s, :], bf2[:, :], ALU.add).then_inc(m_r1, 1)
                pool.wait_ge(m_r1, t + 1)
                g.tensor_tensor(res[:, s, :], res[:, s, :], tin2[:, s, :], ALU.add).then_inc(m_res, 1)

            pipelined(pool, [(0, mix_xb), (0, mix_rs), (0, mix_res)], NT)

            with pool.Fori(0, L) as l:
                pool.wait_ge(m_out, NT)
                pool.wait_ge(l_zT, l * NT)
                pool.wait_ge(l_st[0], 16 * (NT - NT // 2) * l)
                pool.wait_ge(l_st[1], 16 * (NT // 2) * l)
                alone(pool)
                g.iota(iota_n, pattern=[[1, N]], base=0, channel_multiplier=0,
                       allow_small_or_imprecise_dtypes=True).then_inc(a_iota, 1)
                for f in range(KD):
                    def gather(t, s, turn):
                        if not (isinstance(t, int) and t < 2):
                            pool.wait_ge(a_mm, (l * KD + f) * ET + t - 1)
                        alone(pool)
                        g.tensor_copy(idx[:, s:s + 1], src_sb[:, bass.ds(t, 1)]).then_inc(a_idx, 1)
                        pool.wait_ge(a_idx, (l * KD + f) * ET + t + 2)
                        alone(pool)
                        g.indirect_dma_start(out=rows[:, s, :], out_offset=None, in_=h_dram,
                                             in_offset=bass.IndirectOffsetOnAxis(ap=idx[:, s:s + 1], axis=0)).then_inc(a_row[s], 16)

                    if f:
                        pool.wait_ge(a_mm, (l * KD + f) * ET)
                    pipelined(pool, [(0, gather)], ET)

                pool.wait_ge(l_w, 96 * (l + 1))

                def hb(t, s, turn):
                    pool.wait_ge(l_ld[s], 16 * (l * ((NT + 1 - s) // 2) + turn + 1))
                    if not (isinstance(t, int) and t < 2):
                        pool.wait_ge(l_pre, l * NT + t - 1)
                    g.tensor_tensor(base[:, s, :], tin[:, s, :], b2bc[:, :], ALU.add).then_inc(l_hb, 1)

                def ln_rs(t, s, turn):
                    pool.wait_ge(l_mv, l * NT + t + 1)
                    rsqrt(s, l_mv, l_ve, l * NT + t + 1, l_rs)

                def scale(t, s, turn):
                    pool.wait_ge(l_nrm, l * NT + t + 1)
                    g.tensor_tensor(xn[:, s, 0:D], xn[:, s, 0:D], gabc[:, :], ALU.mult).then_inc(l_ga, 1)
                    pool.wait_ge(l_ga, l * NT + t + 1)
                    g.tensor_tensor(xn[:, s, 0:D], xn[:, s, 0:D], bebc[:, :], ALU.add).then_inc(l_be, 1)

                pipelined(pool, [(0, hb), (1, ln_rs), (2, scale)], NT)

            pool.wait_ge(l_zT, L * NT)

            def x2(t, s, turn):
                pool.wait_ge(t_ld[s], 16 * (turn + 1))
                pool.wait_ge(t_ld2[s], 16 * (turn + 1))
                if not (isinstance(t, int) and t < 2):
                    pool.wait_ge(t_acc, t - 1)
                    pool.wait_ge(t_t, t - 1)
                g.tensor_tensor(pre[:, s, :], tin[:, s, :], tin2[:, s, :], ALU.add).then_inc(t_x2, 1)

            def tok_rs(t, s, turn):
                pool.wait_ge(t_mv, t + 1)
                rsqrt(s, t_mv, t_ve, t + 1, t_rs)

            def tok_acc(t, s, turn):
                pool.wait_ge(t_t, t + 1)
                g.tensor_tensor(acc[:, bass.ds(t, 1), :].rearrange("p a d -> p (a d)"), pre[:, s, :], xn[:, s, 0:D],
                                ALU.add).then_inc(t_acc, 1)

            def tok_cp(t, s, turn):
                pool.wait_ge(t_Ts, t + 1)
                alone(pool)
                g.tensor_copy(tT[:, :, rows_of(t)], tTs[:, s, :, :]).then_inc(t_cp, 1)

            pipelined(pool, [(0, x2), (0, tok_rs), (1, tok_acc), (2, tok_cp)], NT)

            pool.wait_ge(r_p, 1)

            def cmb_sl(t, s, turn):
                if not (isinstance(t, int) and t < 2):
                    pool.wait_ge(c_T, t - 1)
                alone(pool)
                g.tensor_copy(cslot[:, s, :], comb[:, bass.ds(t, 1), :].rearrange("p a x -> p (a x)")).then_inc(c_sl, 1)

            pipelined(pool, [(0, cmb_sl)], NT)


_INS = ['x', 'src', 'dst', 'L0_gnn_W1', 'L0_gnn_b1', 'L0_gnn_W2', 'L0_gnn_b2', 'L0_gnn_eps', 'L0_gnn_gamma',
        'L0_gnn_beta', 'L0_mix_w_qkv', 'L0_mix_b_qkv', 'L0_mix_norm_g', 'L0_mix_norm_b', 'L0_mix_w_fc1',
        'L0_mix_b_fc1', 'L0_mix_w_fc2', 'L0_mix_b_fc2', 'L0_ffn_router_w', 'L0_ffn_w1', 'L0_ffn_b1',
        'L0_ffn_w2', 'L0_ffn_b2']


def kernel(**inputs):
    import numpy as _np
    import concourse.bacc as _bacc
    from concourse import mybir as _mybir
    from concourse.bass_utils import run_bass_kernel_spmd as _run

    nc = _bacc.Bacc("TRN2", target_bir_lowering=False, num_devices=1, dynamic_dma_scratch_size=2048)
    arrays, args = {}, []
    for name in _INS:
        a = _np.ascontiguousarray(inputs[name])
        arrays[f"in_{name}"] = a
        args.append(nc.dram_tensor(f"in_{name}", a.shape, _mybir.dt.from_np(a.dtype), kind="ExternalInput").ap())
    shape = tuple(inputs['x'].shape)
    fp32 = _mybir.dt.float32
    args.append(nc.dram_tensor("out_x", shape, fp32, kind="ExternalOutput").ap())
    args.append(nc.dram_tensor("h_rows", shape, fp32, kind="Internal").ap())
    args.append(nc.dram_tensor("acc_rows", shape, fp32, kind="Internal").ap())
    graph_block_kernel(nc, *args)
    r = _run(nc, [arrays], core_ids=[0])
    return r.results[0]["out_x"]
```

```python
import concourse.bass as bass
from concourse import mybir
from contextlib import ExitStack


def pipelined(eng, steps, count, unroll=2, head=2):
    lag = max(l for l, _ in steps)
    start = -(-(lag + head) // unroll) * unroll
    end = count // unroll * unroll

    def peeled(i):
        for l, fn in steps:
            if 0 <= i - l < count:
                fn(i - l, (i - l) % unroll, (i - l) // unroll)

    if end - start < 2 * unroll:
        for i in range(count + lag):
            peeled(i)
        return
    for i in range(start):
        peeled(i)
    with eng.Fori(start // unroll, end // unroll) as turn:
        for u in range(unroll):
            for l, fn in steps:
                slot = (u - l) % unroll
                back = (u - l - slot) // unroll
                fn(turn * unroll + (u - l), slot, turn + back)
    for i in range(end, count + lag):
        peeled(i)


def graph_block_kernel(nc, x, src, dst, gW1, gb1, gW2, gb2, geps, ggamma, gbeta,
                       w_qkv, b_qkv, norm_g, norm_b, w_fc1, b_fc1, w_fc2, b_fc2,
                       router_w, e_w1, e_b1, e_w2, e_b2, out, h_dram, acc_dram):
    fp32 = mybir.dt.float32
    i32 = mybir.dt.int32
    fp16 = mybir.dt.float16
    ALU = mybir.AluOpType
    ACT = mybir.ActivationFunctionType
    AX = mybir.AxisListType

    N, D = x.shape
    E = src.shape[0]
    L = gW1.shape[0]
    X = router_w.shape[0]
    F = w_fc1.shape[1]
    P = 125
    NT = N // P
    KD = D // 128
    KF = F // 128
    HD = 64
    ET = E // P
    CH = 4 * P
    NC = -(-N // CH)
    EPS = 1e-5
    KW = 17
    WIN = 128 * KW
    NG = -(-NT // 4)
    MAGIC = 1.5 * 2 ** 23
    assert NT * P == N and ET * P == E and NT % 2 == 1

    ctx = ExitStack()
    with ctx:
        ctx.enter_context(nc.allow_non_contiguous_dma(reason="biases as columns, a few hundred elements"))

        def sb(name, shape, dt=fp32):
            return ctx.enter_context(nc.sbuf_tensor(name, shape, dt))

        def sem(name):
            return ctx.enter_context(nc.semaphore(name))

        def sems(name, n=2):
            return [ctx.enter_context(nc.semaphore(f"{name}{i}")) for i in range(n)]

        ident = sb("ident", [128, 128])
        zT = sb("zT", [128, KD, N])
        Hs = sb("Hs", [P, NT, 2, D], fp16)
        eps1 = sb("eps1", [128, L + 1])
        half = sb("half", [128, 1])
        st = sb("st", [P, 2, 6])
        mv = sb("mv", [P, 2, 2])
        ve = sb("ve", [P, 2])
        rs = sb("rs", [P, 2])
        b1c = sb("b1c", [128, KD])
        sorted_ok = sb("sorted_ok", [1, 1])
        fast = sb("fast", [1, 1], i32)
        arena = sb("arena", [128, NT * NT * P // 2 + 1])
        work = sb("work", [128, 4864])

        def carve(area, at=0):
            where = [at]

            def take(parts, *shape, dt=fp32):
                n = 1
                for d in shape:
                    n *= d
                words = n if dt in (fp32, i32) else (n + 1) // 2
                v = area[0:parts, where[0]:where[0] + words]
                where[0] += words
                assert where[0] <= area.shape[1], (where, area.shape)
                if dt != fp32:
                    v = v.bitcast(dt)[:, 0:n]
                if len(shape) == 2:
                    v = v.rearrange("p (a b) -> p a b", a=shape[0])
                if len(shape) == 3:
                    v = v.rearrange("p (a b c) -> p a b c", a=shape[0], b=shape[1])
                return v
            return take

        table = arena[0:P, 0:NT * NT * P // 2 + 1].bitcast(fp16)[:, 0:NT * NT * P].rearrange(
            "p (j i d) -> p j i d", j=NT, i=NT)

        take = carve(work)
        tin = take(P, 2, D)
        xn = take(P, 2, D + 1)
        pre = take(P, 2, D)
        base = take(P, 2, D)
        res = take(P, 2, D)
        tTs = take(128, 2, KD, P)
        W1 = take(128, KD, D)
        W2 = take(128, KD, D)
        b2bc = take(P, D)
        gabc = take(P, D)
        bebc = take(P, D)

        take = carve(arena)
        ones_row = take(1, 128)
        hmT = take(128, 2, KD, P)
        gT = take(128, 2, KF, P)
        wqkv = take(128, KD, 3 * D)
        bqkv = take(1, 3 * D)
        bqcol = take(128, KD)
        fc1 = take(128, KD, F)
        fc2 = take(128, KF, D)
        ngcol = take(128, KD)
        nbcol = take(128, KD)
        bf1 = take(128, KF)
        b1p = take(128, KF)
        bf2 = take(P, D)
        Gs = take(128, KD, D + 1)
        grow = take(1, D + 1)
        Ts = take(128, KD, D)
        trow = take(1, D)
        attn = take(128, KD, 128)
        attnT = take(128, KD, 128)
        amax = take(128, KD)
        asum = take(128, KD)
        arec = take(128, KD)
        wqT = take(128, KD, D)
        Mw = take(128, KD, D)
        crow = take(1, D)
        cbc = take(P, D)
        take = carve(arena, 13000)
        x_all = take(P, NT, D)
        take = carve(arena, 20000)
        dst_all = take(P, ET, dt=i32)
        dst_allf = take(P, ET)
        dst_next = take(P, 1, dt=i32)
        dst_nextf = take(P, 1)
        ones_col = take(P, ET)
        cmp_ = take(P, ET)
        cnt = take(P, NT)
        lo = take(1, NT + 1)
        span = take(1, NT)
        sflag = take(1, 4)
        start_f = take(1, NT)
        start_i = take(1, NT, dt=i32)
        wsrc = take(128, NT * KW, dt=i32)
        wdst = take(128, NT * KW, dt=i32)
        wsf = take(128, NT * KW)
        wdf = take(128, NT * KW)
        wbase = take(128, NT * KW)
        wt1 = take(128, NT * KW)
        wt2 = take(128, NT * KW)
        valid = take(128, NT * KW)
        take = carve(work)
        s1v = take(128, NT, KW, dt=fp16)
        s0p = take(128, NT, KW, dt=fp16)
        d0p = take(128, NT, KW, dt=fp16)
        iota25 = take(128, NT + 1, dt=fp16)
        iota0 = take(128, 128, dt=fp16)
        iota1 = take(128, 128, dt=fp16)
        tri = take(128, 128, dt=fp16)
        ones16 = take(128, 128, dt=fp16)
        OV = take(128, 2, KW, 2 * NT, dt=fp16)
        OR = take(128, KW, 128, dt=fp16)
        rk = take(128, 2, KW)
        rkm = take(128, KW)
        rkm1 = take(128, 1)
        rkT = take(1, 128)
        V = take(128, 2, 2 * NT)
        ohs = take(128, 8, 128, dt=fp16)
        ohd = take(128, 8, 128, dt=fp16)
        take = carve(arena, (NT - 1) * NT * P // 2)
        OH = take(128, 2, (KW + 1) * NT, dt=fp16)
        S2 = take(128, (KW + 2) * NT, dt=fp16)
        S4 = take(128, 2, KW * NT, dt=fp16)
        OHR = take(128, KW, NT)
        take = carve(arena)
        iota_n = take(P, N)
        onehot = take(P, 2, N)
        rows = take(P, 2, D)
        src_sb = take(P, ET, dt=i32)
        dst_sb = take(P, ET, dt=i32)
        dst_f = take(P, ET)
        idx = take(P, 2, dt=i32)
        take = carve(arena)
        tin3 = take(P, 2, D)
        gTe = take(128, 2, KD, P)
        tT = take(128, KD, N)
        acc = take(P, NT, D)
        w1e = take(128, X * KD, D)
        w2e = take(128, X * KD, D)
        rwT = take(128, KD, X)
        lg = take(P, NT, X)
        pr = take(P, NT, X)
        key = take(P, NT, X)
        oh1 = take(P, NT, X)
        oh2 = take(P, NT, X)
        rank8 = take(P, NT, X)
        rmax = take(P, NT, 3)
        comb = take(P, NT, X)
        cslot = take(P, 2, X)
        combT = take(X, 2, P)
        eb1 = take(128, X, KD)
        eb2 = take(X, D)

        bank = [ctx.enter_context(nc.psum_tensor(f"bank{i}", [128, 512], fp32)) for i in range(8)]

        s_const, s_wld, s_eps = sem("s_const"), sem("s_wld"), sem("s_eps")
        x_ld = sems("x_ld", 4); xn_st = sems("xn_st")
        s_bn, s_mv, s_ve, s_rs, s_xn = sem("s_bn"), sem("s_mv"), sem("s_ve"), sem("s_rs"), sem("s_xn")
        s_xT, s_zT, s_G = sem("s_xT"), sem("s_zT"), sem("s_G")
        f_pe, f_dve, f_act = sem("f_pe"), sem("f_dve"), sem("f_act")
        s_hi, s_lo = sem("s_hi"), sem("s_lo")
        w_ld, w_pool, w_dve, w_pe, w_win = sem("w_ld"), sem("w_pool"), sem("w_dve"), sem("w_pe"), sem("w_win")
        b_oh, b_s2, b_s4, b_ov, b_rank, b_x = sem("b_oh"), sem("b_s2"), sem("b_s4"), sem("b_ov"), sem("b_rank"), sem("b_x")
        b_rk, b_or, b_v, b_vs, b_g, b_tab, b_ev = (sem("b_rk"), sem("b_or"), sem("b_v"), sem("b_vs"), sem("b_g"),
                                                   sem("b_tab"), sem("b_ev"))
        w_step, w_tri = sem("w_step"), sem("w_tri")
        b_m, b_flag = sem("b_m"), sem("b_flag")
        d_mm = sem("d_mm")
        l_hi, l_lo = sem("l_hi"), sem("l_lo")
        m_ld = sems("m_ld"); m_st = sems("m_st")
        m_xTs, m_xf, m_xb, m_pre = sem("m_xTs"), sem("m_xf"), sem("m_xb"), sem("m_pre")
        m_bn, m_mv, m_ve, m_rs, m_hm = sem("m_bn"), sem("m_mv"), sem("m_ve"), sem("m_rs"), sem("m_hm")
        m_r1, m_res, m_hT, m_hTs, m_f1 = sem("m_r1"), sem("m_res"), sem("m_hT"), sem("m_hTs"), sem("m_f1")
        m_g, m_f2, m_out = sem("m_g"), sem("m_f2"), sem("m_out")
        a_tab, a_iota, a_idx, a_oh, a_mm, a_add = (sem("a_tab"), sem("a_iota"), sem("a_idx"), sem("a_oh"),
                                                   sem("a_mm"), sem("a_add"))
        a_dst = sem("a_dst")
        a_row = sems("a_row")
        l_w, l_open = sem("l_w"), sem("l_open")
        l_ld = sems("l_ld"); l_st = sems("l_st")
        l_m1, l_re, l_m2, l_hb, l_pre = sem("l_m1"), sem("l_re"), sem("l_m2"), sem("l_hb"), sem("l_pre")
        l_bn, l_mv, l_ve, l_rs, l_nrm = sem("l_bn"), sem("l_mv"), sem("l_ve"), sem("l_rs"), sem("l_nrm")
        l_ga, l_be, l_h, l_hT, l_zT = sem("l_ga"), sem("l_be"), sem("l_h"), sem("l_hT"), sem("l_zT")
        e_w = sem("e_w")
        t_ld = sems("t_ld"); t_ld2 = sems("t_ld2")
        t_x2, t_bn, t_mv, t_ve, t_rs, t_t = (sem("t_x2"), sem("t_bn"), sem("t_mv"), sem("t_ve"), sem("t_rs"), sem("t_t"))
        t_acc, t_T, t_Ts, t_cp, t_lg, t_lgs = (sem("t_acc"), sem("t_T"), sem("t_Ts"), sem("t_cp"), sem("t_lg"), sem("t_lgs"))
        r_d, r_a, r_p = sem("r_d"), sem("r_a"), sem("r_p")
        c_sl, c_T, c_Ts, c_b, c_acc = sem("c_sl"), sem("c_T"), sem("c_Ts"), sem("c_b"), sem("c_acc")
        x_m1, x_g, x_m2, x_acc, x_out = sem("x_m1"), sem("x_g"), sem("x_m2"), sem("x_acc"), sem("x_out")

        past = {e.engine: sem(f"past_{n}") for n, e in (('sp', nc.sync), ('pe', nc.tensor), ('dve', nc.vector),
                                                        ('act', nc.scalar), ('pool', nc.gpsimd))}

        x_t = x.rearrange("(t p) d -> t p d", p=P)

        def part_of(t, part):
            return Hs[:, bass.ds(t, 1), part, :].rearrange("p a d -> p (a d)")

        def row_of(area, t):
            return area[:, bass.ds(t, 1), :].rearrange("p a d -> p (a d)")

        def acc_of(t):
            return row_of(acc, t)

        def rows_of(t):
            return bass.ds(t * P, P)

        def over_tiles(t, j):
            return t[:, bass.ds(j, 1), :].rearrange("p a k -> p k a").broadcast_to([128, KW, NT])

        block = ctx.enter_context(nc.Block())

        def alone(eng):
            eng.sem_inc(past[eng.engine], 1)

        T_WIN = 8
        NW = 9
        NU = KD * NC

        @block.sync
        def _(sp):
            x_at = 0
            for n, (w, nth) in enumerate([(1, 0), (2, 1), (3, 2), (9, 3), (10, 3)]):
                sp.dma_start(x_all[:, x_at:x_at + w, :], x[x_at * P:(x_at + w) * P, :].rearrange("(t p) d -> p t d", p=P)).then_inc(x_ld[nth], 16)
                x_at += w
            sp.dma_start(eps1[:, 0:L], geps.rearrange("(a l) -> a l", a=1).broadcast_to([128, L])).then_inc(s_eps, 16)
            sp.dma_start(wqkv[:, :, :], w_qkv.rearrange("(k p) n -> p k n", p=128)).then_inc(s_wld, 16)
            sp.dma_start(bqkv[:, :], b_qkv.rearrange("(a n) -> a n", a=1)).then_inc(s_wld, 16)
            sp.dma_start(bqcol[:, :], b_qkv[0:D].rearrange("(k p) -> p k", p=128)).then_inc(s_wld, 16)
            sp.dma_start(fc1[:, :, :], w_fc1.rearrange("(k p) n -> p k n", p=128)).then_inc(s_wld, 16)
            sp.dma_start(fc2[:, :, :], w_fc2.rearrange("(k p) n -> p k n", p=128)).then_inc(s_wld, 16)
            sp.dma_start(ngcol[:, :], norm_g.rearrange("(k p) -> p k", p=128)).then_inc(s_wld, 16)
            sp.dma_start(nbcol[:, :], norm_b.rearrange("(k p) -> p k", p=128)).then_inc(s_wld, 16)
            sp.dma_start(bf1[:, :], b_fc1.rearrange("(k p) -> p k", p=128)).then_inc(s_wld, 16)
            sp.dma_start(bf2[:, :], b_fc2.rearrange("(a n) -> a n", a=1).broadcast_to([P, D])).then_inc(s_wld, 16)
            sp.dma_start(dst_all[:, :], dst.rearrange("(p t) -> p t", p=P)).then_inc(w_ld, 16)
            sp.wait_ge(w_pool, 1)
            sp.dma_start(dst_next[0:P - 1, :], dst[ET:E].rearrange("(p t) -> p t", t=ET)[:, 0:1]).then_inc(w_ld, 16)

            def store_xn(t, s, turn):
                sp.wait_ge(s_xn, t + 1)
                sp.dma_start(h_dram[rows_of(t), :], xn[:, s, 0:D]).then_inc(xn_st[s], 16)

            pipelined(sp, [(0, store_xn)], NT)
            sp.wait_ge(xn_st[0], 16 * (NT - NT // 2))
            sp.wait_ge(xn_st[1], 16 * (NT // 2))

            def load_mix(t, s, turn):
                if not (isinstance(t, int) and t < 2):
                    sp.wait_ge(m_xb, t - 1)
                sp.dma_start(tin[:, s, :], h_dram[rows_of(t), :]).then_inc(m_ld[s], 16)

            def store_mix(t, s, turn):
                sp.wait_ge(m_out, t + 1)
                sp.dma_start(acc_dram[rows_of(t), :], res[:, s, :]).then_inc(m_st[s], 16)

            def load_windows(t, s, turn):
                if isinstance(t, int) and t == T_WIN:
                    sp.wait_ge(w_dve, 3)
                    with sp.Fori(0, NT) as j:
                        at = sp.value_load(start_i[0:1, bass.ds(j, 1)], min_val=0, max_val=E - WIN)
                        sp.dma_start(wsrc[:, bass.ds(j * KW, KW)], src[bass.ds(at, WIN)].rearrange("(p k) -> p k", p=128)).then_inc(w_win, 16)
                        sp.dma_start(wdst[:, bass.ds(j * KW, KW)], dst[bass.ds(at, WIN)].rearrange("(p k) -> p k", p=128)).then_inc(w_win, 16)

            pipelined(sp, [(11, store_mix), (3, load_windows), (0, load_mix)], NT)
            sp.wait_ge(m_st[0], 16 * (NT - NT // 2))
            sp.wait_ge(m_st[1], 16 * (NT // 2))

            sp.wait_ge(b_ev, NT * NG)
            sp.wait_ge(b_flag, 1)
            with sp.Fori(0, L) as l:
                sp.sem_inc(l_open, 1)
                sp.dma_start(W1[:, :, :], gW1[bass.ds(l, 1), :, :].rearrange("a (k p) n -> p (a k) n", p=128)).then_inc(l_w, 16)
                sp.dma_start(W2[:, :, :], gW2[bass.ds(l, 1), :, :].rearrange("a (k p) n -> p (a k) n", p=128)).then_inc(l_w, 16)
                sp.dma_start(b1c[:, :], gb1[bass.ds(l, 1), :].rearrange("a (k p) -> p (a k)", p=128)).then_inc(l_w, 16)
                sp.dma_start(b2bc[:, :], gb2[bass.ds(l, 1), :].broadcast_to([P, D])).then_inc(l_w, 16)
                sp.dma_start(gabc[:, :], ggamma[bass.ds(l, 1), :].broadcast_to([P, D])).then_inc(l_w, 16)
                sp.dma_start(bebc[:, :], gbeta[bass.ds(l, 1), :].broadcast_to([P, D])).then_inc(l_w, 16)

                def load_h(t, s, turn):
                    if not (isinstance(t, int) and t < 2):
                        sp.wait_ge(l_hb, l * NT + t - 1)
                    sp.dma_start(tin[:, s, :], h_dram[rows_of(t), :]).then_inc(l_ld[s], 16)

                def store_h(t, s, turn):
                    sp.wait_ge(l_h, l * NT + t + 1)
                    sp.dma_start(h_dram[rows_of(t), :], res[:, s, :]).then_inc(l_st[s], 16)

                sp.wait_ge(a_add, (l + 1) * NU)
                pipelined(sp, [(6, store_h), (0, load_h)], NT)
                sp.wait_ge(l_st[0], 16 * (NT - NT // 2) * (l + 1))
                alone(sp)
                sp.wait_ge(l_st[1], 16 * (NT // 2) * (l + 1))
                alone(sp)
                sp.wait_ge(l_zT, NT * (l + 1))
                alone(sp)
                sp.wait_ge(l_lo, NT * (l + 1))
                alone(sp)

            for k in range(KD):
                sp.dma_start(rwT[:, k, :], router_w[:, k * 128:(k + 1) * 128].rearrange("e p -> p e")).then_inc(e_w, 16)
                sp.dma_start(eb1[:, :, k], e_b1[:, k * 128:(k + 1) * 128].rearrange("e p -> p e")).then_inc(e_w, 16)
            sp.dma_start(eb2[:, :], e_b2).then_inc(e_w, 16)
            for x0 in range(0, X, X // 2):
                sp.dma_start(w1e[:, x0 * KD:(x0 + X // 2) * KD, :],
                             e_w1[x0:x0 + X // 2, :, :].rearrange("x (k p) d -> p (x k) d", p=128)).then_inc(e_w, 16)
                sp.dma_start(w2e[:, x0 * KD:(x0 + X // 2) * KD, :],
                             e_w2[x0:x0 + X // 2, :, :].rearrange("x (k p) d -> p (x k) d", p=128)).then_inc(e_w, 16)

            def load_t(t, s, turn):
                if not (isinstance(t, int) and t < 2):
                    sp.wait_ge(t_x2, t - 1)
                sp.dma_start(tin[:, s, :], h_dram[rows_of(t), :]).then_inc(t_ld[s], 16)
                sp.dma_start(tin3[:, s, :], acc_dram[rows_of(t), :]).then_inc(t_ld2[s], 16)

            pipelined(sp, [(0, load_t)], NT)

            def store_out(t, s, turn):
                sp.wait_ge(x_acc, X * (t + 1))
                sp.dma_start(out[rows_of(t), :], acc[:, bass.ds(t, 1), :].rearrange("p a d -> p (a d)")).then_inc(x_out, 16)

            pipelined(sp, [(0, store_out)], NT)
            sp.wait_ge(x_out, 16 * NT)

        @block.tensor
        def _(pe):
            mm = nc.tensor.matmul
            pe.wait_ge(s_const, 5)

            def first(t):
                return isinstance(t, int) and t == 0

            def last(t):
                return isinstance(t, int) and t == NT - 1

            def norm_x(t, s, turn):
                pe.wait_ge(s_xn, t + 1)
                if not (isinstance(t, int) and t < 2):
                    pe.wait_ge(s_zT, t - 1)
                for k in range(KD):
                    i = nc.tensor.transpose(bank[s][:, k * P:(k + 1) * P], xn[:, s, k * 128:(k + 1) * 128], ident[0:P, 0:P])
                i.then_inc(s_xT, 1)
                for k in range(KD):
                    i = mm(bank[2 + k][:, 0:D + 1], lhsT=xn[:, s, k * 128:(k + 1) * 128], rhs=xn[:, s, :],
                           start=first(t), stop=last(t))
                i.then_inc(s_G, 1)

            pipelined(pe, [(3, norm_x)], NT)

            pe.wait_ge(s_wld, 16 * NW)
            pe.wait_ge(s_zT, NT)
            pe.wait_ge(f_dve, 1)
            for k in range(KD):
                i = mm(bank[4][0:1, k * 128:(k + 1) * 128], lhsT=Gs[:, k, D:D + 1], rhs=ident[:, :], start=True, stop=True)
            i.then_inc(f_pe, 1)
            for k in range(KD):
                for a in range(KD):
                    i = nc.tensor.transpose(bank[5][:, (a * KD + k) * 128:(a * KD + k + 1) * 128],
                                            wqkv[:, k, a * 128:(a + 1) * 128], ident[:, :])
            i.then_inc(f_pe, 1)
            for m in range(KF):
                for k in range(KD):
                    i = mm(bank[6][:, m:m + 1], lhsT=fc1[:, k, m * 128:(m + 1) * 128], rhs=nbcol[:, k:k + 1],
                           start=(k == 0), stop=(k == KD - 1))
            i.then_inc(f_pe, 1)
            pe.wait_ge(f_dve, 2)
            for m in range(KD + 1):
                cols = slice(m * 128, (m + 1) * 128) if m < KD else slice(D, D + 1)
                o = bank[m][:, 0:D] if m < KD else bank[4][0:1, 0:D]
                for k in range(KD):
                    mm(o, lhsT=Gs[:, k, cols], rhs=wqkv[:, k, 2 * D:3 * D], start=(k == 0), stop=False)
                i = mm(o, lhsT=grow[0:1, cols], rhs=bqkv[0:1, 2 * D:3 * D], start=False, stop=True)
            i.then_inc(f_pe, 1)
            pe.wait_ge(f_dve, 5)
            for a in range(KD):
                for k in range(KD):
                    mm(bank[7][:, a * 128:(a + 1) * 128], lhsT=wqkv[:, k, D + a * 128:D + (a + 1) * 128],
                       rhs=Ts[:, k, a * 128:(a + 1) * 128], start=(k == 0), stop=False)
                i = mm(bank[7][:, a * 128:(a + 1) * 128], lhsT=bqkv[0:1, D + a * 128:D + (a + 1) * 128],
                       rhs=trow[0:1, a * 128:(a + 1) * 128], start=False, stop=True)
            i.then_inc(f_pe, 1)
            pe.wait_ge(f_dve, 7)
            for a in range(KD):
                i = nc.tensor.transpose(bank[5][:, a * 128:(a + 1) * 128], attn[:, a, :], ident[:, :])
            i.then_inc(f_pe, 1)
            pe.wait_ge(f_dve, 8)
            for m in range(KD):
                for a in range(KD):
                    mm(bank[m][:, a * 128:(a + 1) * 128], lhsT=wqT[:, a, m * 128:(m + 1) * 128], rhs=attnT[:, a, :],
                       start=True, stop=True)
            for a in range(KD):
                i = mm(bank[4][0:1, a * 128:(a + 1) * 128], lhsT=bqcol[:, a:a + 1], rhs=attnT[:, a, :], start=True, stop=True)
            i.then_inc(f_pe, 1)
            pe.wait_ge(f_dve, 9)
            mm(bank[6][0:P, 0:D], lhsT=ones_row[0:1, 0:P], rhs=crow[0:1, :], start=True, stop=True).then_inc(f_pe, 1)
            pe.wait_ge(f_dve, 10)

            def mix_count(t, s, turn):
                if isinstance(t, int) and t == T_WIN:
                    pe.wait_ge(w_dve, 1)
                    mm(bank[0][0:1, 0:NT], lhsT=ones_col[:, 0:1], rhs=cnt[:, :], start=True, stop=True).then_inc(w_pe, 1)

            def mix_xf(t, s, turn):
                pe.wait_ge(m_xTs, t + 1)
                if not (isinstance(t, int) and t == 0):
                    pe.wait_ge(m_pre, t)
                for k in range(KD):
                    i = mm(bank[2][0:P, 0:D], lhsT=tTs[:, s, k, :], rhs=Mw[:, k, :], start=(k == 0), stop=(k == KD - 1))
                i.then_inc(m_xf, 1)

            def mix_hT(t, s, turn):
                pe.wait_ge(m_hm, t + 1)
                if not (isinstance(t, int) and t == 0):
                    pe.wait_ge(m_hTs, t)
                for k in range(KD):
                    i = nc.tensor.transpose(bank[1][:, k * P:(k + 1) * P], xn[:, s, k * 128:(k + 1) * 128], ident[0:P, 0:P])
                i.then_inc(m_hT, 1)

            def mix_f1(t, s, turn):
                pe.wait_ge(m_hTs, t + 1)
                if not (isinstance(t, int) and t < 2):
                    pe.wait_ge(m_g, t - 1)
                for m in range(KF):
                    o = bank[4 + 2 * s + m // 4][:, m % 4 * P:(m % 4 + 1) * P]
                    for k in range(KD):
                        i = mm(o, lhsT=fc1[:, k, m * 128:(m + 1) * 128], rhs=hmT[:, s, k, :], start=(k == 0), stop=(k == KD - 1))
                i.then_inc(m_f1, 1)

            def mix_f2(t, s, turn):
                pe.wait_ge(m_g, t + 1)
                if not (isinstance(t, int) and t == 0):
                    pe.wait_ge(m_out, t)
                for k in range(KF):
                    i = mm(bank[3][0:P, 0:D], lhsT=gT[:, s, k, :], rhs=fc2[:, k, :], start=(k == 0), stop=(k == KF - 1))
                i.then_inc(m_f2, 1)

            pipelined(pe, [(10, mix_f2), (8, mix_f1), (6, mix_hT), (2, mix_xf), (2, mix_count)], NT)
            pe.wait_ge(m_out, NT)

            def rank(j, s, turn):
                pe.wait_ge(b_s4, j + 1)
                if not (isinstance(j, int) and j < 2):
                    pe.wait_ge(b_x, j - 1)
                mm(bank[s][:, 0:KW * NT], lhsT=tri[:, :], rhs=OH[:, s, NT:], start=True, stop=False)
                for k in range(1, KW, 4):
                    i = mm(bank[s][:, k * NT:KW * NT], lhsT=ones16[:, :], rhs=S4[:, s, 0:(KW - k) * NT],
                           start=False, stop=(k + 4 >= KW))
                i.then_inc(b_rank, 1)

            def permute(j, s, turn):
                pe.wait_ge(b_or, j + 1)
                pe.wait_ge(b_ov, j + 1)
                if not (isinstance(j, int) and j < 2):
                    pe.wait_ge(b_vs, j - 1)
                for k in range(KW):
                    i = mm(bank[2 + s][:, 0:2 * NT], lhsT=OR[:, k, :], rhs=OV[:, s, k, :], start=(k == 0), stop=(k == KW - 1))
                i.then_inc(b_v, 1)

            def count(j, s, turn):
                for g in range(NG):
                    q = (s * NG + g) % 2
                    pe.wait_ge(b_g, j * NG + g + 1)
                    if not (isinstance(j, int) and j * NG + g < 2):
                        pe.wait_ge(b_ev, j * NG + g - 1)
                    for ii in range(min(4, NT - 4 * g)):
                        i = mm(bank[4 + q][0:P, ii * P:(ii + 1) * P], lhsT=ohs[:, 4 * q + ii, 0:P], rhs=ohd[:, 4 * q + ii, 0:P],
                               start=True, stop=True)
                    i.then_inc(b_tab, 1)

            pipelined(pe, [(0, rank), (1, permute), (2, count)], NT)
            pe.wait_ge(b_m, NT + 1)
            nc.tensor.transpose(bank[6][0:1, 0:128], rkm1, ident[:, :]).then_inc(w_pe, 1)
            pe.wait_ge(b_flag, 1)
            pe.wait_ge(b_ev, NT * NG)
            fast_pe = pe.value_load(fast[0:1, 0:1], min_val=0, max_val=1)

            with pe.Fori(0, L) as l:
                with pe.If(fast_pe):
                    pe.wait_ge(s_lo, NT)
                    pe.wait_ge(l_open, l + 1)

                    def dense(c, w, nth):
                        for f in range(KD):
                            b = 2 * (nth % 2) + f
                            if not (isinstance(c, int) and c < 2):
                                pe.wait_ge(a_add, l * NU + KD * (c - 2) + f + 1)
                            for i in range(NT):
                                for part in range(2):
                                    ins = mm(bank[b][:, 0:w * P], lhsT=Hs[:, i, part, f * 128:(f + 1) * 128],
                                             rhs=table[:, bass.ds(4 * c, w), i, :],
                                             start=(i == 0 and part == 0), stop=(i == NT - 1 and part == 1))
                            ins.then_inc(d_mm, 1)

                    dense(0, 4, 0)
                    dense(1, 4, 1)
                    with pe.Fori(1, (NC - 1) // 2) as turn:
                        dense(2 * turn, 4, 0)
                        dense(2 * turn + 1, 4, 1)
                    dense(NC - 1, NT - 4 * (NC - 1), 0)
                with pe.Else():
                    for f in range(KD):
                        def agg(t, s, turn):
                            pe.wait_ge(a_row[s], 16 * ((l * KD + f) * (ET // 2) + turn + 1))
                            pe.wait_ge(a_oh, (l * KD + f) * ET + t + 1)
                            for c in range(NC):
                                w = min(CH, N - c * CH)
                                i = mm(bank[c][:, 0:w], lhsT=rows[:, s, f * 128:(f + 1) * 128], rhs=onehot[:, s, c * CH:c * CH + w],
                                       start=(isinstance(t, int) and t == 0), stop=(isinstance(t, int) and t == ET - 1))
                            i.then_inc(a_mm, 1)

                        pe.wait_ge(l_open, l + 1)
                        if f:
                            pe.wait_ge(a_add, l * NU + f * NC)
                        agg(0, 0, 0)
                        agg(1, 1, 0)
                        with pe.Fori(1, ET // 2 - 1) as turn:
                            agg(2 * turn, 0, turn)
                            agg(2 * turn + 1, 1, turn)
                        agg(ET - 2, 0, ET // 2 - 1)
                        agg(ET - 1, 1, ET // 2 - 1)

                pe.wait_ge(a_add, (l + 1) * NU)
                pe.wait_ge(l_w, (l + 1) * 96)

                def mlp1(t, s, turn):
                    if not (isinstance(t, int) and t < 2):
                        pe.wait_ge(l_re, l * NT + t - 1)
                    for m in range(KD):
                        for k in range(KD):
                            i = mm(bank[s][:, m * P:(m + 1) * P], lhsT=W1[:, k, m * 128:(m + 1) * 128],
                                   rhs=zT[:, k, rows_of(t)], start=(k == 0), stop=(k == KD - 1))
                    i.then_inc(l_m1, 1)

                def mlp2(t, s, turn):
                    pe.wait_ge(l_re, l * NT + t + 1)
                    if not (isinstance(t, int) and t < 2):
                        pe.wait_ge(l_pre, l * NT + t - 1)
                    for k in range(KD):
                        i = mm(bank[2 + s][0:P, 0:D], lhsT=tTs[:, s, k, :], rhs=W2[:, k, :], start=(k == 0), stop=(k == KD - 1))
                    i.then_inc(l_m2, 1)

                def h_T(t, s, turn):
                    pe.wait_ge(l_h, l * NT + t + 1)
                    if not (isinstance(t, int) and t < 2):
                        pe.wait_ge(l_zT, l * NT + t - 1)
                    for k in range(KD):
                        i = nc.tensor.transpose(bank[4 + s][:, k * P:(k + 1) * P], res[:, s, k * 128:(k + 1) * 128], ident[0:P, 0:P])
                    i.then_inc(l_hT, 1)

                pipelined(pe, [(7, h_T), (2, mlp2), (0, mlp1)], NT)
                pe.wait_ge(l_zT, (l + 1) * NT)

            pe.wait_ge(e_w, 16 * 9)
            def tok_T(t, s, turn):
                pe.wait_ge(t_t, t + 1)
                if not (isinstance(t, int) and t < 2):
                    pe.wait_ge(t_cp, t - 1)
                for k in range(KD):
                    i = nc.tensor.transpose(bank[s][:, k * P:(k + 1) * P], xn[:, s, k * 128:(k + 1) * 128], ident[0:P, 0:P])
                i.then_inc(t_T, 1)

            def tok_lg(t, s, turn):
                pe.wait_ge(t_Ts, t + 1)
                if not (isinstance(t, int) and t < 2):
                    pe.wait_ge(t_lgs, t - 1)
                for k in range(KD):
                    i = mm(bank[2 + s][0:P, 0:X], lhsT=tTs[:, s, k, :], rhs=rwT[:, k, :], start=(k == 0), stop=(k == KD - 1))
                i.then_inc(t_lg, 1)

            pipelined(pe, [(5, tok_lg), (3, tok_T)], NT)

            def cmb_T(t, s, turn):
                pe.wait_ge(c_sl, t + 1)
                if not (isinstance(t, int) and t < 2):
                    pe.wait_ge(c_Ts, t - 1)
                nc.tensor.transpose(bank[4 + s][0:X, 0:P], cslot[:, s, :], ident[0:P, 0:P]).then_inc(c_T, 1)

            def cmb_b(t, s, turn):
                pe.wait_ge(c_Ts, t + 1)
                if not (isinstance(t, int) and t < 2):
                    pe.wait_ge(c_acc, t - 1)
                mm(bank[6 + s][0:P, 0:D], lhsT=combT[:, s, :], rhs=eb2[:, :], start=True, stop=True).then_inc(c_b, 1)

            pipelined(pe, [(3, cmb_b), (1, cmb_T)], NT)

            pe.wait_ge(e_w, 16 * 9)
            pe.wait_ge(t_cp, NT)

            def exp1(t, e, n):
                s = e % 2
                if not (isinstance(t, int) and t < 2):
                    pe.wait_ge(x_g, t - 1)
                for m in range(KD):
                    for k in range(KD):
                        i = mm(bank[s][:, m * P:(m + 1) * P], lhsT=w1e[:, e * KD + k, m * 128:(m + 1) * 128],
                               rhs=tT[:, k, rows_of(n)], start=(k == 0), stop=(k == KD - 1))
                i.then_inc(x_m1, 1)

            def exp2(t, e, n):
                s = e % 2
                pe.wait_ge(x_g, t + 1)
                if not (isinstance(t, int) and t < 2):
                    pe.wait_ge(x_acc, t - 1)
                for k in range(KD):
                    i = mm(bank[2 + s][0:P, 0:D], lhsT=gTe[:, s, k, :], rhs=w2e[:, e * KD + k, :], start=(k == 0), stop=(k == KD - 1))
                i.then_inc(x_m2, 1)

            pipelined(pe, [(2, exp2), (0, exp1)], NT * X, unroll=X)

        @block.vector
        def _(dve):
            v = nc.vector
            v.memset(xn[:, :, D:D + 1], 1.0).then_inc(s_const, 1)
            v.memset(grow[0:1, D:D + 1], float(N)).then_inc(s_const, 1)
            dve.wait_ge(s_eps, 17)
            v.tensor_scalar(eps1[:, :], eps1[:, :], 1.0, None, ALU.add).then_inc(s_const, 1)

            def stats(t, s, turn):
                early = isinstance(t, int) and t < 6
                dve.wait_ge(x_ld[(0 if t == 0 else 1 if t < 3 else 2) if early else 3], 16 if early else 32)
                alone(dve)
                v.bn_stats(st[:, s, :], row_of(x_all, t)).then_inc(s_bn, 1)
                dve.wait_ge(s_bn, t + 1)
                alone(dve)
                v.bn_aggr(mv[:, s, :], st[:, s, :]).then_inc(s_mv, 1)

            def norm(t, s, turn):
                dve.wait_ge(s_rs, t + 1)
                if not (isinstance(t, int) and t < 2):
                    dve.wait_ge(s_G, t - 1)
                    dve.wait_ge(xn_st[s], 16 * turn)
                    dve.wait_ge(s_lo, t - 1)
                alone(dve)
                v.tensor_scalar(xn[:, s, 0:D], row_of(x_all, t), mv[:, s, 0:1], rs[:, s:s + 1], ALU.subtract, ALU.mult).then_inc(s_xn, 1)

            def low(t, s, turn):
                dve.wait_ge(s_hi, t + 1)
                v.tensor_tensor(part_of(t, 1), xn[:, s, 0:D], part_of(t, 0), ALU.subtract).then_inc(s_lo, 1)

            dve.wait_ge(s_const, 5)
            pipelined(dve, [(4, low), (2, norm), (0, stats)], NT)

            dve.wait_ge(s_G, NT)
            for k in range(KD):
                i = v.tensor_copy(Gs[:, k, :], bank[2 + k][:, 0:D + 1])
            i.then_inc(f_dve, 1)
            dve.wait_ge(f_pe, 1)
            v.tensor_copy(grow[0:1, 0:D], bank[4][0:1, 0:D]).then_inc(f_dve, 1)
            dve.wait_ge(f_pe, 2)
            v.tensor_copy(wqT[:, :, :].rearrange("p a c -> p (a c)"), bank[5][:, 0:KD * D]).then_inc(f_dve, 1)
            dve.wait_ge(f_pe, 3)
            v.tensor_tensor(b1p[:, :], bank[6][:, 0:KF], bf1[:, :], ALU.add)
            for k in range(KD):
                i = v.tensor_scalar(fc1[:, k, :], fc1[:, k, :], ngcol[:, k:k + 1], None, ALU.mult)
            v.memset(attn[:, :, :], 0.0).then_inc(f_dve, 1)
            dve.wait_ge(f_pe, 4)
            for m in range(KD):
                v.tensor_copy(Ts[:, m, :], bank[m][:, 0:D])
            v.tensor_copy(trow[0:1, :], bank[4][0:1, 0:D]).then_inc(f_dve, 1)
            dve.wait_ge(f_pe, 5)
            for a in range(KD):
                for hh in range(2):
                    r = slice(hh * HD, (hh + 1) * HD)
                    i = v.reduce_max(amax[r, a:a + 1], bank[7][r, a * 128 + hh * HD:a * 128 + (hh + 1) * HD], AX.X)
            i.then_inc(r_d, 1)
            dve.wait_ge(r_d, 1)
            v.tensor_scalar(amax[:, :], amax[:, :], -float(HD) ** -0.5, None, ALU.mult).then_inc(f_dve, 1)
            dve.wait_ge(f_act, 1)
            v.reciprocal(arec[:, :], asum[:, :]).then_inc(r_d, 1)
            dve.wait_ge(r_d, 2)
            for a in range(KD):
                i = v.tensor_scalar(attn[:, a, :], attn[:, a, :], arec[:, a:a + 1], None, ALU.mult)
            i.then_inc(f_dve, 1)
            dve.wait_ge(f_pe, 6)
            v.tensor_copy(attnT[:, :, :].rearrange("p a c -> p (a c)"), bank[5][:, 0:D]).then_inc(f_dve, 1)
            dve.wait_ge(f_pe, 7)
            for m in range(KD):
                v.tensor_copy(Mw[:, m, :], bank[m][:, 0:D])
            v.tensor_copy(crow[0:1, :], bank[4][0:1, 0:D]).then_inc(f_dve, 1)
            dve.wait_ge(f_pe, 8)
            v.tensor_copy(cbc[:, :], bank[6][0:P, 0:D]).then_inc(f_dve, 1)

            n_w = [0]

            def step(i):
                n_w[0] += 1
                i.then_inc(w_step, 1)
                dve.wait_ge(w_step, n_w[0])

            dve.wait_ge(w_ld, 32)
            dve.wait_ge(w_pool, 2)
            v.memset(ones_col[:, :], 1.0)
            v.tensor_copy(dst_nextf[:, :], dst_next[:, :])
            step(v.tensor_copy(dst_allf[:, :], dst_all[:, :]))

            def below(t, s, turn):
                if isinstance(t, int) and t < T_WIN:
                    for j in range(1 + t * NT // T_WIN, 1 + (t + 1) * NT // T_WIN):
                        if j < NT:
                            step(v.scalar_tensor_tensor(cmp_[:, :], dst_allf[:, :], float(j * P), ones_col[:, :], ALU.is_lt,
                                                        ALU.mult, accum_out=cnt[:, j - 1:j]))
                if isinstance(t, int) and t == T_WIN:
                    step(v.tensor_tensor(cmp_[:, 0:ET - 1], dst_allf[:, 0:ET - 1], dst_allf[:, 1:ET], ALU.is_gt))
                    step(v.tensor_tensor(cmp_[:, ET - 1:ET], dst_allf[:, ET - 1:ET], dst_nextf[:, :], ALU.is_gt))
                    v.reduce_sum(cnt[:, NT - 1:NT], cmp_[:, :], AX.X).then_inc(w_dve, 1)

            def starts(t, s, turn):
                if not (isinstance(t, int) and t == T_WIN):
                    return
                dve.wait_ge(w_pe, 1)
                step(v.memset(lo[0:1, 0:1], 0.0))
                step(v.memset(lo[0:1, NT:NT + 1], float(E)))
                step(v.tensor_copy(lo[0:1, 1:NT], bank[0][0:1, 0:NT - 1]))
                step(v.tensor_copy(sflag[0:1, 0:1], bank[0][0:1, NT - 1:NT]))
                step(v.tensor_scalar(start_f[0:1, :], lo[0:1, 0:NT], float(E - WIN), None, ALU.min))
                step(v.tensor_copy(start_i[0:1, :], start_f[0:1, :]))
                step(v.tensor_tensor(span[0:1, :], lo[0:1, 1:NT + 1], lo[0:1, 0:NT], ALU.subtract))
                step(v.reduce_max(sflag[0:1, 1:2], span[0:1, :], AX.X))
                step(v.tensor_scalar(sflag[0:1, 2:3], sflag[0:1, 1:2], float(WIN), None, ALU.is_le))
                step(v.tensor_scalar(sflag[0:1, 3:4], sflag[0:1, 0:1], 0.5, None, ALU.is_lt))
                v.tensor_tensor(sorted_ok[0:1, :], sflag[0:1, 2:3], sflag[0:1, 3:4], ALU.mult).then_inc(w_dve, 2)

            def mix_pre(t, s, turn):
                dve.wait_ge(m_xf, t + 1)
                dve.wait_ge(m_xb, t + 1)
                if not (isinstance(t, int) and t < 2):
                    dve.wait_ge(m_res, t - 1)
                    dve.wait_ge(m_hm, t - 1)
                v.tensor_tensor(pre[:, s, :], bank[2][0:P, 0:D], base[:, s, :], ALU.add).then_inc(m_pre, 1)
                dve.wait_ge(m_pre, t + 1)
                v.bn_stats(st[:, s, :], pre[:, s, :]).then_inc(m_bn, 1)
                dve.wait_ge(m_bn, t + 1)
                alone(dve)
                v.bn_aggr(mv[:, s, :], st[:, s, :]).then_inc(m_mv, 1)

            def mix_norm(t, s, turn):
                dve.wait_ge(m_rs, t + 1)
                if not (isinstance(t, int) and t < 2):
                    dve.wait_ge(m_hT, t - 1)
                v.tensor_scalar(xn[:, s, 0:D], pre[:, s, :], mv[:, s, 0:1], rs[:, s:s + 1], ALU.subtract, ALU.mult).then_inc(m_hm, 1)

            def mix_out(t, s, turn):
                dve.wait_ge(m_f2, t + 1)
                dve.wait_ge(m_res, t + 1)
                if not (isinstance(t, int) and t < 2):
                    dve.wait_ge(m_st[s], 16 * turn)
                alone(dve)
                v.tensor_tensor(res[:, s, :], bank[3][0:P, 0:D], row_of(x_all, t), ALU.add).then_inc(m_out, 1)

            pipelined(dve, [(11, mix_out), (5, mix_norm), (3, mix_pre), (3, starts), (2, below)], NT)

            W = NT * KW
            dve.wait_ge(w_win, 32 * NT)
            step(v.tensor_copy(wsf[:, :], wsrc[:, :]))
            step(v.tensor_copy(wdf[:, :], wdst[:, :]))
            step(v.tensor_tensor(wdf[:, :], wdf[:, :], wbase[:, :], ALU.subtract))
            step(v.tensor_scalar(wt1[:, :], wdf[:, :], 0.0, None, ALU.is_ge))
            step(v.scalar_tensor_tensor(valid[:, :], wdf[:, :], float(P), wt1[:, :], ALU.is_lt, ALU.mult))
            step(v.tensor_scalar(wt1[:, :], wsf[:, :], 1.0 / P, -(0.5 - 0.5 / P), ALU.mult, ALU.add))
            step(v.tensor_scalar(wt2[:, :], wt1[:, :], MAGIC, None, ALU.add))
            step(v.tensor_scalar(wt1[:, :], wt2[:, :], MAGIC, None, ALU.subtract))
            step(v.scalar_tensor_tensor(wt2[:, :], wt1[:, :], -float(P), wsf[:, :], ALU.mult, ALU.add))
            dve.wait_ge(m_out, NT)
            dve.wait_ge(m_st[0], 16 * (NT - NT // 2))
            dve.wait_ge(m_st[1], 16 * (NT // 2))
            flat = "p a b -> p (a b)"
            step(v.tensor_scalar(s0p.rearrange(flat), wt2[:, :], 1.0, None, ALU.add))
            step(v.tensor_scalar(d0p.rearrange(flat), wdf[:, :], 1.0, None, ALU.add))
            step(v.scalar_tensor_tensor(wt2[:, :], wt1[:, :], 1.0, valid[:, :], ALU.add, ALU.mult))
            v.memset(ones16[:, :], 1.0)
            v.memset(rkm[:, :], 0.0)
            v.tensor_scalar(s1v.rearrange(flat), wt2[:, :], 1.0, None, ALU.subtract).then_inc(w_dve, 1)

            def sources(j, s, turn):
                if not (isinstance(j, int) and j < 2):
                    dve.wait_ge(b_rank, j - 1)
                    dve.wait_ge(b_x, j - 1)
                    dve.wait_ge(b_ov, j - 1)
                tiles = iota25[:, 0:NT].rearrange("p (a i) -> p a i", a=1).broadcast_to([128, KW, NT])
                v.tensor_tensor(OH[:, s, NT:].rearrange("p (k i) -> p k i", k=KW), over_tiles(s1v, j), tiles,
                                ALU.is_equal).then_inc(b_oh, 1)

            def rank_x(j, s, turn):
                dve.wait_ge(b_rank, j + 1)
                if not (isinstance(j, int) and j == 0):
                    dve.wait_ge(b_rk, j)
                v.tensor_tensor(OHR[:, :, :].rearrange(flat), bank[s][:, 0:KW * NT], OH[:, s, NT:], ALU.mult).then_inc(b_x, 1)
                dve.wait_ge(b_x, j + 1)
                if not (isinstance(j, int) and j < 2):
                    dve.wait_ge(b_or, j - 1)
                v.reduce_sum(rk[:, s, :], OHR[:, :, :], AX.X).then_inc(b_rk, 1)
                dve.wait_ge(b_rk, j + 1)
                v.tensor_tensor(rkm[:, :], rkm[:, :], rk[:, s, :], ALU.max).then_inc(b_m, 1)
                if not (isinstance(j, int) and j == 0):
                    dve.wait_ge(b_v, j)
                for k in range(KW):
                    i = v.tensor_scalar(OR[:, k, :], iota0[:, :], rk[:, s, k:k + 1], None, ALU.is_equal)
                i.then_inc(b_or, 1)

            def places(j, s, turn):
                dve.wait_ge(b_v, j + 1)
                if not (isinstance(j, int) and j < 2):
                    dve.wait_ge(b_g, (j - 1) * NG)
                v.tensor_copy(V[:, s, :], bank[2 + s][:, 0:2 * NT]).then_inc(b_vs, 1)
                dve.wait_ge(b_vs, j + 1)
                for g in range(NG):
                    q = (s * NG + g) % 2
                    if not (isinstance(j, int) and j * NG + g < 2):
                        dve.wait_ge(b_tab, j * NG + g - 1)
                    for ii in range(min(4, NT - 4 * g)):
                        c = 4 * g + ii
                        v.tensor_scalar(ohs[:, 4 * q + ii, :], iota1[:, :], V[:, s, c:c + 1], None, ALU.is_equal)
                        i = v.tensor_scalar(ohd[:, 4 * q + ii, :], iota1[:, :], V[:, s, NT + c:NT + c + 1], None, ALU.is_equal)
                    i.then_inc(b_g, 1)

            dve.wait_ge(w_pool, 3)
            dve.wait_ge(w_dve, 4)
            pipelined(dve, [(0, sources), (1, rank_x), (2, places)], NT)
            dve.wait_ge(b_m, NT)
            v.reduce_max(rkm1, rkm[:, :], AX.X).then_inc(b_m, 1)
            dve.wait_ge(w_pe, 2)
            step(v.reduce_max(rkT[0:1, 0:1], bank[6][0:1, 0:128], AX.X))
            step(v.tensor_scalar(rkT[0:1, 1:2], rkT[0:1, 0:1], 127.5, None, ALU.is_lt))
            step(v.tensor_tensor(rkT[0:1, 2:3], rkT[0:1, 1:2], sorted_ok[0:1, :], ALU.mult))
            v.tensor_copy(fast[0:1, :], rkT[0:1, 2:3]).then_inc(b_flag, 1)
            dve.wait_ge(b_flag, 1)
            dve.wait_ge(b_ev, NT * NG)
            fast_dve = dve.value_load(fast[0:1, 0:1], min_val=0, max_val=1)

            with dve.Fori(0, L) as l:
                dve.wait_ge(l_open, l + 1)
                alone(dve)
                with dve.If(fast_dve):
                    def add_sums(c, w, nth):
                        for f in range(KD):
                            b = 2 * (nth % 2) + f
                            dve.wait_ge(d_mm, l * NU + KD * c + f + 1)
                            part = zT[:, f, bass.ds(c * CH, w * P)]
                            alone(dve)
                            v.scalar_tensor_tensor(part, part, eps1[:, bass.ds(l, 1)], bank[b][:, 0:w * P], ALU.mult,
                                                   ALU.add).then_inc(a_add, 1)

                    add_sums(0, 4, 0)
                    add_sums(1, 4, 1)
                    with dve.Fori(1, (NC - 1) // 2) as turn:
                        add_sums(2 * turn, 4, 0)
                        add_sums(2 * turn + 1, 4, 1)
                    add_sums(NC - 1, NT - 4 * (NC - 1), 0)
                with dve.Else():
                    dve.wait_ge(a_tab, l * 32 + 32)
                    v.tensor_copy(dst_f[:, :], dst_sb[:, :]).then_inc(a_dst, 1)
                    dve.wait_ge(a_dst, l + 1)
                    dve.wait_ge(a_iota, l + 1)
                    for f in range(KD):
                        def one(t, s, turn):
                            if not (isinstance(t, int) and t < 2):
                                dve.wait_ge(a_mm, (l * KD + f) * ET + t - 1)
                            v.tensor_scalar(onehot[:, s, :], iota_n, dst_f[:, bass.ds(t, 1)], None, ALU.is_equal).then_inc(a_oh, 1)

                        if f:
                            dve.wait_ge(a_mm, (l * KD + f) * ET)
                        pipelined(dve, [(0, one)], ET)
                        dve.wait_ge(a_mm, (l * KD + f + 1) * ET)
                        for c in range(NC):
                            w = min(CH, N - c * CH)
                            v.scalar_tensor_tensor(zT[:, f, c * CH:c * CH + w], zT[:, f, c * CH:c * CH + w],
                                                   eps1[:, bass.ds(l, 1)], bank[c][:, 0:w], ALU.mult,
                                                   ALU.add).then_inc(a_add, 1)

                def pre_ln(t, s, turn):
                    dve.wait_ge(l_m2, l * NT + t + 1)
                    dve.wait_ge(l_hb, l * NT + t + 1)
                    if not (isinstance(t, int) and t < 2):
                        dve.wait_ge(l_nrm, l * NT + t - 1)
                    v.tensor_tensor(pre[:, s, :], bank[2 + s][0:P, 0:D], base[:, s, :], ALU.add).then_inc(l_pre, 1)

                def stats_ln(t, s, turn):
                    dve.wait_ge(l_pre, l * NT + t + 1)
                    v.bn_stats(st[:, s, :], pre[:, s, :]).then_inc(l_bn, 1)
                    dve.wait_ge(l_bn, l * NT + t + 1)
                    alone(dve)
                    v.bn_aggr(mv[:, s, :], st[:, s, :]).then_inc(l_mv, 1)

                def ln(t, s, turn):
                    dve.wait_ge(l_rs, l * NT + t + 1)
                    if not (isinstance(t, int) and t < 2):
                        dve.wait_ge(l_h, l * NT + t - 1)
                    v.scalar_tensor_tensor(xn[:, s, 0:D], pre[:, s, :], mv[:, s, 0:1], gabc[:, :], ALU.subtract,
                                           ALU.mult).then_inc(l_nrm, 1)
                    dve.wait_ge(l_nrm, l * NT + t + 1)
                    v.scalar_tensor_tensor(xn[:, s, 0:D], xn[:, s, 0:D], rs[:, s:s + 1], bebc[:, :], ALU.mult,
                                           ALU.add).then_inc(l_be, 1)

                dve.wait_ge(a_add, (l + 1) * NU)
                dve.wait_ge(l_w, 96 * (l + 1))
                pipelined(dve, [(5, ln), (3, pre_ln), (3, stats_ln)], NT)

            def x2(t, s, turn):
                dve.wait_ge(t_ld[s], 16 * (turn + 1))
                dve.wait_ge(t_ld2[s], 16 * (turn + 1))
                alone(dve)
                v.tensor_tensor(acc_of(t), tin[:, s, :], tin3[:, s, :], ALU.add).then_inc(t_x2, 1)

            def tok_st(t, s, turn):
                dve.wait_ge(t_x2, t + 1)
                alone(dve)
                v.bn_stats(st[:, s, :], acc_of(t)).then_inc(t_bn, 1)
                dve.wait_ge(t_bn, t + 1)
                alone(dve)
                v.bn_aggr(mv[:, s, :], st[:, s, :]).then_inc(t_mv, 1)

            def tok_n(t, s, turn):
                dve.wait_ge(t_rs, t + 1)
                if not (isinstance(t, int) and t < 2):
                    dve.wait_ge(t_T, t - 1)
                    dve.wait_ge(t_acc, t - 1)
                alone(dve)
                v.tensor_scalar(xn[:, s, 0:D], acc_of(t), mv[:, s, 0:1], rs[:, s:s + 1], ALU.subtract, ALU.mult).then_inc(t_t, 1)

            def tok_l(t, s, turn):
                dve.wait_ge(t_lg, t + 1)
                v.tensor_copy(lg[:, bass.ds(t, 1), :].rearrange("p a x -> p (a x)"), bank[2 + s][0:P, 0:X]).then_inc(t_lgs, 1)

            dve.wait_ge(l_zT, L * NT)
            pipelined(dve, [(6, tok_l), (2, tok_n), (0, x2), (0, tok_st)], NT)

            n_r = [2]

            def done(i):
                n_r[0] += 1
                i.then_inc(r_d, 1)
                dve.wait_ge(r_d, n_r[0])

            def wide(k):
                return rmax[:, :, k:k + 1].broadcast_to([P, NT, X])

            def choose(oh):
                done(v.reduce_max(rmax[:, :, 1:2], key[:, :, :], AX.X))
                done(v.tensor_tensor(oh[:, :, :], key[:, :, :], wide(1), ALU.is_ge))
                done(v.tensor_tensor(oh[:, :, :], oh[:, :, :], rank8[:, :, :], ALU.mult))
                done(v.reduce_max(rmax[:, :, 2:3], oh[:, :, :], AX.X))
                done(v.tensor_tensor(oh[:, :, :], oh[:, :, :], wide(2), ALU.is_equal))

            dve.wait_ge(t_lgs, NT)
            for e in range(X):
                i = v.memset(rank8[:, :, e:e + 1], float(X - e))
            done(i)
            done(v.reduce_max(rmax[:, :, 0:1], lg[:, :, :], AX.X))
            done(v.tensor_tensor(lg[:, :, :], lg[:, :, :], wide(0), ALU.subtract))
            dve.wait_ge(r_a, 1)
            done(v.reduce_sum(rmax[:, :, 0:1], pr[:, :, :], AX.X))
            done(v.reciprocal(rmax[:, :, 0:1], rmax[:, :, 0:1]))
            done(v.tensor_tensor(pr[:, :, :], pr[:, :, :], wide(0), ALU.mult))
            done(v.tensor_copy(key[:, :, :], pr[:, :, :]))
            choose(oh1)
            done(v.scalar_tensor_tensor(key[:, :, :], oh1[:, :, :], -2.0, key[:, :, :], ALU.mult, ALU.add))
            choose(oh2)
            done(v.tensor_tensor(oh1[:, :, :], oh1[:, :, :], oh2[:, :, :], ALU.add))
            done(v.tensor_tensor(pr[:, :, :], pr[:, :, :], oh1[:, :, :], ALU.mult))
            done(v.reduce_sum(rmax[:, :, 0:1], pr[:, :, :], AX.X))
            done(v.tensor_scalar(rmax[:, :, 0:1], rmax[:, :, 0:1], 1e-12, None, ALU.max))
            done(v.reciprocal(rmax[:, :, 0:1], rmax[:, :, 0:1]))
            v.tensor_tensor(comb[:, :, :], pr[:, :, :], wide(0), ALU.mult).then_inc(r_p, 1)

            def cmb_cp(t, s, turn):
                dve.wait_ge(c_T, t + 1)
                if not (isinstance(t, int) and t < 2):
                    dve.wait_ge(c_b, t - 1)
                v.tensor_copy(combT[:, s, :], bank[4 + s][0:X, 0:P]).then_inc(c_Ts, 1)

            def cmb_acc(t, s, turn):
                dve.wait_ge(c_b, t + 1)
                v.tensor_tensor(acc_of(t), acc_of(t), bank[6 + s][0:P, 0:D], ALU.add).then_inc(c_acc, 1)

            dve.wait_ge(t_acc, NT)
            pipelined(dve, [(4, cmb_acc), (2, cmb_cp)], NT)

            dve.wait_ge(c_acc, NT)
            dve.wait_ge(r_p, 1)

            def exp_acc(t, e, n):
                s = e % 2
                dve.wait_ge(x_m2, t + 1)
                if not (isinstance(t, int) and t == 0):
                    dve.wait_ge(x_acc, t)
                v.scalar_tensor_tensor(acc_of(n), bank[2 + s][0:P, 0:D],
                                       comb[:, bass.ds(n, 1), e:e + 1].rearrange("p a x -> p (a x)"),
                                       acc_of(n), ALU.mult, ALU.add).then_inc(x_acc, 1)

            pipelined(dve, [(0, exp_acc)], NT * X, unroll=X)

        @block.scalar
        def _(act):
            a = nc.scalar
            act.wait_ge(s_const, 5)

            def z0(t, s, turn):
                act.wait_ge(s_xT, t + 1)
                alone(act)
                a.activation(zT[:, :, rows_of(t)], bank[s][:, 0:KD * P].rearrange("p (k n) -> p k n", k=KD), ACT.Copy).then_inc(s_zT, 1)

            def high(t, s, turn):
                act.wait_ge(s_xn, t + 1)
                alone(act)
                a.activation(part_of(t, 0), xn[:, s, 0:D], ACT.Copy).then_inc(s_hi, 1)

            pipelined(act, [(4, z0), (3, high)], NT)
            act.wait_ge(f_dve, 6)
            for b in range(KD):
                for hh in range(2):
                    r = slice(hh * HD, (hh + 1) * HD)
                    i = a.activation(attn[r, b, r], bank[7][r, b * 128 + hh * HD:b * 128 + (hh + 1) * HD], ACT.Exp,
                                     bias=amax[r, b:b + 1], scale=float(HD) ** -0.5, accum_out=asum[r, b:b + 1])
            i.then_inc(f_act, 1)

            def mix_xTs(t, s, turn):
                if not (isinstance(t, int) and t < 2):
                    act.wait_ge(m_xf, t - 1)
                alone(act)
                a.activation(tTs[:, s, :, :], zT[:, :, rows_of(t)], ACT.Copy).then_inc(m_xTs, 1)

            def mix_hTs(t, s, turn):
                act.wait_ge(m_hT, t + 1)
                if not (isinstance(t, int) and t < 2):
                    act.wait_ge(m_f1, t - 1)
                a.activation(hmT[:, s, :, :], bank[1][:, 0:KD * P].rearrange("p (k n) -> p k n", k=KD), ACT.Copy).then_inc(m_hTs, 1)

            def mix_gelu(t, s, turn):
                act.wait_ge(m_f1, t + 1)
                if not (isinstance(t, int) and t < 2):
                    act.wait_ge(m_f2, t - 1)
                for m in range(KF):
                    i = a.activation(gT[:, s, m, :], bank[4 + 2 * s + m // 4][:, m % 4 * P:(m % 4 + 1) * P], ACT.Gelu,
                                     bias=b1p[:, m:m + 1])
                i.then_inc(m_g, 1)

            act.wait_ge(s_zT, NT)
            pipelined(act, [(9, mix_gelu), (7, mix_hTs), (1, mix_xTs)], NT)

            def evict(j, s, turn):
                for g in range(NG):
                    q = (s * NG + g) % 2
                    w = min(4, NT - 4 * g)
                    act.wait_ge(b_tab, j * NG + g + 1)
                    alone(act)
                    a.activation(table[:, bass.ds(j, 1), 4 * g:4 * g + w, :].rearrange("p a i d -> p (a i d)"),
                                 bank[4 + q][0:P, 0:w * P], ACT.Copy).then_inc(b_ev, 1)

            pipelined(act, [(0, evict)], NT)

            with act.Fori(0, L) as l:
                act.wait_ge(l_w, 96 * (l + 1))

                def relu1(t, s, turn):
                    act.wait_ge(l_m1, l * NT + t + 1)
                    if not (isinstance(t, int) and t < 2):
                        act.wait_ge(l_m2, l * NT + t - 1)
                    for m in range(KD):
                        i = a.activation(tTs[:, s, m, :], bank[s][:, m * P:(m + 1) * P], ACT.Relu, bias=b1c[:, m:m + 1])
                    i.then_inc(l_re, 1)

                def relu2(t, s, turn):
                    act.wait_ge(l_be, l * NT + t + 1)
                    if not (isinstance(t, int) and t < 2):
                        act.wait_ge(l_hT, l * NT + t - 1)
                        act.wait_ge(l_st[s], 16 * (l * ((NT + 1 - s) // 2) + turn))
                        act.wait_ge(l_lo, l * NT + t - 1)
                    a.activation(res[:, s, :], xn[:, s, 0:D], ACT.Relu).then_inc(l_h, 1)
                    act.wait_ge(l_h, l * NT + t + 1)
                    alone(act)
                    a.activation(part_of(t, 0), res[:, s, :], ACT.Copy).then_inc(l_hi, 1)

                def z_next(t, s, turn):
                    act.wait_ge(l_hT, l * NT + t + 1)
                    alone(act)
                    a.activation(zT[:, :, rows_of(t)], bank[4 + s][:, 0:KD * P].rearrange("p (k n) -> p k n", k=KD), ACT.Copy).then_inc(l_zT, 1)

                pipelined(act, [(8, z_next), (6, relu2), (1, relu1)], NT)

            def tok_Ts(t, s, turn):
                act.wait_ge(t_T, t + 1)
                if not (isinstance(t, int) and t < 2):
                    act.wait_ge(t_lg, t - 1)
                alone(act)
                transposed = bank[s][:, 0:KD * P].rearrange("p (k n) -> p k n", k=KD)
                a.activation(tTs[:, s, :, :], transposed, ACT.Copy).then_inc(t_Ts, 1)
                a.activation(tT[:, :, rows_of(t)], transposed, ACT.Copy).then_inc(t_cp, 1)

            act.wait_ge(l_zT, L * NT)
            pipelined(act, [(4, tok_Ts)], NT)
            act.wait_ge(r_d, 5)
            a.activation(pr[:, :, :], lg[:, :, :], ACT.Exp).then_inc(r_a, 1)

            act.wait_ge(e_w, 16 * 9)

            def exp_g(t, e, n):
                s = e % 2
                act.wait_ge(x_m1, t + 1)
                if not (isinstance(t, int) and t < 2):
                    act.wait_ge(x_m2, t - 1)
                for m in range(KD):
                    i = a.activation(gTe[:, s, m, :], bank[s][:, m * P:(m + 1) * P], ACT.Gelu, bias=eb1[:, e, m:m + 1])
                i.then_inc(x_g, 1)

            pipelined(act, [(1, exp_g)], NT * X, unroll=X)

        @block.gpsimd
        def _(pool):
            g = nc.gpsimd
            g.memset(eps1[:, L:L + 1], 0.0).then_inc(s_eps, 1)
            g.memset(half[:, :], -0.5).then_inc(s_const, 1)
            g.memset(ones_row[:, :], 1.0)
            g.memset(ident[:, :], 0.0).then_inc(a_idx, 1)
            pool.wait_ge(a_idx, 1)
            g.affine_select(out=ident[:, :], in_=ident[:, :], compare_op=ALU.not_equal, fill=1.0, base=0,
                            pattern=[[-1, 128]], channel_multiplier=1).then_inc(s_const, 1)
            pool.wait_ge(s_const, 5)

            def rsqrt(s, begin, mid, mid_n, end):
                alone(pool)
                g.tensor_scalar(ve[:, s:s + 1], mv[:, s, 1:2], EPS, None, ALU.add).then_inc(mid, 1)
                pool.wait_ge(mid, mid_n)
                g.tensor_tensor(rs[:, s:s + 1], ve[:, s:s + 1], half[0:P, :], ALU.pow).then_inc(end, 1)

            def norm_rs(t, s, turn):
                pool.wait_ge(s_mv, t + 1)
                rsqrt(s, s_mv, s_ve, t + 1, s_rs)

            g.memset(dst_next[:, :], N).then_inc(w_pool, 1)
            g.iota(wbase[:, :].rearrange("p (j k) -> p j k", k=KW), pattern=[[P, NT], [0, KW]], base=0, channel_multiplier=0,
                   allow_small_or_imprecise_dtypes=True).then_inc(w_pool, 1)
            pipelined(pool, [(1, norm_rs)], NT)
            pool.wait_ge(f_dve, 10)
            pool.wait_ge(s_wld, 16 * NW)

            def mix_xb(t, s, turn):
                pool.wait_ge(m_ld[s], 16 * (turn + 1))
                if not (isinstance(t, int) and t < 2):
                    pool.wait_ge(m_pre, t - 1)
                g.tensor_tensor(base[:, s, :], tin[:, s, :], cbc[:, :], ALU.add).then_inc(m_xb, 1)

            def mix_rs(t, s, turn):
                pool.wait_ge(m_mv, t + 1)
                rsqrt(s, m_mv, m_ve, t + 1, m_rs)

            def mix_res(t, s, turn):
                pool.wait_ge(m_pre, t + 1)
                alone(pool)
                g.tensor_tensor(row_of(x_all, t), row_of(x_all, t), pre[:, s, :], ALU.add).then_inc(m_res, 1)

            def mix_r1(t, s, turn):
                alone(pool)
                g.tensor_tensor(row_of(x_all, t), row_of(x_all, t), bf2[:, :], ALU.add).then_inc(m_r1, 1)
                pool.wait_ge(m_r1, t + 1)
                alone(pool)

            pipelined(pool, [(4, mix_rs), (4, mix_res), (0, mix_r1), (0, mix_xb)], NT)

            pool.wait_ge(w_dve, 4)
            g.iota(iota25[:, 0:NT], pattern=[[1, NT]], base=0, channel_multiplier=0, allow_small_or_imprecise_dtypes=True)
            g.iota(iota0[:, :], pattern=[[1, 128]], base=0, channel_multiplier=0, allow_small_or_imprecise_dtypes=True)
            g.iota(iota1[:, :], pattern=[[1, 128]], base=1, channel_multiplier=0, allow_small_or_imprecise_dtypes=True)
            g.memset(OH[:, :, 0:NT], 0.0)
            g.memset(S2[:, 0:2 * NT], 0.0)
            g.memset(tri[:, :], 1.0).then_inc(w_tri, 1)
            pool.wait_ge(w_tri, 1)
            g.affine_select(out=tri[:, :], in_=tri[:, :], compare_op=ALU.is_gt, fill=0.0, base=0,
                            pattern=[[1, 128]], channel_multiplier=-1).then_inc(w_pool, 1)
            pool.wait_ge(w_pool, 3)

            def sources(j, s, turn):
                if not (isinstance(j, int) and j < 2):
                    pool.wait_ge(b_rank, j - 1)
                    pool.wait_ge(b_v, j - 1)
                oh = OH[:, s, NT:].rearrange("p (k i) -> p k i", k=KW)
                if not (isinstance(j, int) and j == 0):
                    pool.wait_ge(b_s4, j)
                pool.wait_ge(b_oh, j + 1)
                g.tensor_tensor(S2[:, 2 * NT:], OH[:, s, NT:], OH[:, s, 0:KW * NT], ALU.add).then_inc(b_s2, 1)
                pool.wait_ge(b_s2, j + 1)
                g.tensor_tensor(S4[:, s, :], S2[:, 2 * NT:], S2[:, 0:KW * NT], ALU.add).then_inc(b_s4, 1)
                g.tensor_tensor(OV[:, s, :, 0:NT], oh, over_tiles(s0p, j), ALU.mult)
                g.tensor_tensor(OV[:, s, :, NT:2 * NT], oh, over_tiles(d0p, j), ALU.mult).then_inc(b_ov, 1)

            pipelined(pool, [(0, sources)], NT)
            pool.wait_ge(b_flag, 1)
            pool.wait_ge(b_ev, NT * NG)
            fast_pool = pool.value_load(fast[0:1, 0:1], min_val=0, max_val=1)

            with pool.Fori(0, L) as l:
                with pool.If(fast_pool):
                    pool.wait_ge(l_open, l + 1)
                    alone(pool)
                with pool.Else():
                    pool.wait_ge(l_open, l + 1)
                    alone(pool)
                    pool.dma_start(src_sb[:, :], src.rearrange("(p t) -> p t", p=P)).then_inc(a_tab, 16)
                    pool.dma_start(dst_sb[:, :], dst.rearrange("(p t) -> p t", p=P)).then_inc(a_tab, 16)
                    pool.wait_ge(a_tab, l * 32 + 32)
                    alone(pool)
                    g.iota(iota_n, pattern=[[1, N]], base=0, channel_multiplier=0,
                           allow_small_or_imprecise_dtypes=True).then_inc(a_iota, 1)
                    for f in range(KD):
                        def gather(t, s, turn):
                            if not (isinstance(t, int) and t < 2):
                                pool.wait_ge(a_mm, (l * KD + f) * ET + t - 1)
                            alone(pool)
                            g.tensor_copy(idx[:, s:s + 1], src_sb[:, bass.ds(t, 1)]).then_inc(a_idx, 1)
                            pool.wait_ge(a_idx, (l * KD + f) * ET + t + 2)
                            alone(pool)
                            g.indirect_dma_start(out=rows[:, s, :], out_offset=None, in_=h_dram,
                                                 in_offset=bass.IndirectOffsetOnAxis(ap=idx[:, s:s + 1], axis=0)).then_inc(a_row[s], 16)

                        if f:
                            pool.wait_ge(a_mm, (l * KD + f) * ET)
                        pipelined(pool, [(0, gather)], ET)

                pool.wait_ge(l_w, 96 * (l + 1))

                def hb(t, s, turn):
                    pool.wait_ge(l_ld[s], 16 * (l * ((NT + 1 - s) // 2) + turn + 1))
                    if not (isinstance(t, int) and t < 2):
                        pool.wait_ge(l_pre, l * NT + t - 1)
                    g.tensor_tensor(base[:, s, :], tin[:, s, :], b2bc[:, :], ALU.add).then_inc(l_hb, 1)

                def ln_rs(t, s, turn):
                    pool.wait_ge(l_mv, l * NT + t + 1)
                    rsqrt(s, l_mv, l_ve, l * NT + t + 1, l_rs)

                def h_low(t, s, turn):
                    pool.wait_ge(l_hi, l * NT + t + 1)
                    alone(pool)
                    g.tensor_tensor(part_of(t, 1), res[:, s, :], part_of(t, 0), ALU.subtract).then_inc(l_lo, 1)

                pipelined(pool, [(7, h_low), (4, ln_rs), (2, hb)], NT)

            pool.wait_ge(l_zT, L * NT)

            def tok_rs(t, s, turn):
                pool.wait_ge(t_mv, t + 1)
                rsqrt(s, t_mv, t_ve, t + 1, t_rs)

            def tok_acc(t, s, turn):
                pool.wait_ge(t_t, t + 1)
                alone(pool)
                g.tensor_tensor(acc_of(t), acc_of(t), xn[:, s, 0:D], ALU.add).then_inc(t_acc, 1)

            pipelined(pool, [(3, tok_acc), (1, tok_rs)], NT)

            pool.wait_ge(r_p, 1)

            def cmb_sl(t, s, turn):
                if not (isinstance(t, int) and t < 2):
                    pool.wait_ge(c_T, t - 1)
                alone(pool)
                g.tensor_copy(cslot[:, s, :], comb[:, bass.ds(t, 1), :].rearrange("p a x -> p (a x)")).then_inc(c_sl, 1)

            pipelined(pool, [(0, cmb_sl)], NT)


_INS = ['x', 'src', 'dst', 'L0_gnn_W1', 'L0_gnn_b1', 'L0_gnn_W2', 'L0_gnn_b2', 'L0_gnn_eps', 'L0_gnn_gamma',
        'L0_gnn_beta', 'L0_mix_w_qkv', 'L0_mix_b_qkv', 'L0_mix_norm_g', 'L0_mix_norm_b', 'L0_mix_w_fc1',
        'L0_mix_b_fc1', 'L0_mix_w_fc2', 'L0_mix_b_fc2', 'L0_ffn_router_w', 'L0_ffn_w1', 'L0_ffn_b1',
        'L0_ffn_w2', 'L0_ffn_b2']


def kernel(**inputs):
    import numpy as _np
    import concourse.bacc as _bacc
    from concourse import mybir as _mybir
    from concourse.bass_utils import run_bass_kernel_spmd as _run

    nc = _bacc.Bacc("TRN2", target_bir_lowering=False, num_devices=1, dynamic_dma_scratch_size=2048)
    arrays, args = {}, []
    for name in _INS:
        a = _np.ascontiguousarray(inputs[name])
        arrays[f"in_{name}"] = a
        args.append(nc.dram_tensor(f"in_{name}", a.shape, _mybir.dt.from_np(a.dtype), kind="ExternalInput").ap())
    shape = tuple(inputs['x'].shape)
    fp32 = _mybir.dt.float32
    args.append(nc.dram_tensor("out_x", shape, fp32, kind="ExternalOutput").ap())
    args.append(nc.dram_tensor("h_rows", shape, fp32, kind="Internal").ap())
    args.append(nc.dram_tensor("acc_rows", shape, fp32, kind="Internal").ap())
    graph_block_kernel(nc, *args)
    r = _run(nc, [arrays], core_ids=[0])
    return r.results[0]["out_x"]
```

```python
import math

import concourse.bass as bass
from concourse import mybir
from contextlib import ExitStack


def pipelined(eng, steps, count, unroll=2, head=2):
    lag = max(l for l, _ in steps)
    start = -(-(lag + head) // unroll) * unroll
    end = count // unroll * unroll

    def peeled(i):
        for l, fn in steps:
            if 0 <= i - l < count:
                fn(i - l, (i - l) % unroll, (i - l) // unroll)

    if end - start < 2 * unroll:
        for i in range(count + lag):
            peeled(i)
        return
    for i in range(start):
        peeled(i)
    with eng.Fori(start // unroll, end // unroll) as turn:
        for u in range(unroll):
            for l, fn in steps:
                slot = (u - l) % unroll
                back = (u - l - slot) // unroll
                fn(turn * unroll + (u - l), slot, turn + back)
    for i in range(end, count + lag):
        peeled(i)


def graph_block_kernel(nc, x, src, dst, gW1, gb1, gW2, gb2, geps, ggamma, gbeta,
                       w_qkv, b_qkv, norm_g, norm_b, w_fc1, b_fc1, w_fc2, b_fc2,
                       router_w, e_w1, e_b1, e_w2, e_b2, out, h_dram, acc_dram):
    fp32 = mybir.dt.float32
    i32 = mybir.dt.int32
    fp16 = mybir.dt.float16
    ALU = mybir.AluOpType
    ACT = mybir.ActivationFunctionType
    AX = mybir.AxisListType

    N, D = x.shape
    E = src.shape[0]
    L = gW1.shape[0]
    X = router_w.shape[0]
    F = w_fc1.shape[1]
    P = 125
    NT = N // P
    KD = D // 128
    KF = F // 128
    HD = 64
    ET = E // P
    CH = 4 * P
    NC = -(-N // CH)
    EPS = 1e-5
    KW = 17
    WIN = 128 * KW
    NG = -(-NT // 4)
    MAGIC = 1.5 * 2 ** 23
    assert NT * P == N and ET * P == E and NT % 2 == 1

    ctx = ExitStack()
    with ctx:
        ctx.enter_context(nc.allow_non_contiguous_dma(reason="biases as columns, a few hundred elements"))

        def sb(name, shape, dt=fp32):
            return ctx.enter_context(nc.sbuf_tensor(name, shape, dt))

        def sem(name):
            return ctx.enter_context(nc.semaphore(name))

        def sems(name, n=2):
            return [ctx.enter_context(nc.semaphore(f"{name}{i}")) for i in range(n)]

        ident = sb("ident", [128, 128])
        zT = sb("zT", [128, KD, N])
        Hs = sb("Hs", [P, NT, 2, D], fp16)
        eps1 = sb("eps1", [128, L])
        half = sb("half", [128, 1])
        st = sb("st", [P, 2, 6])
        mv = sb("mv", [P, 2, 2])
        ve = sb("ve", [P, 2])
        rs = sb("rs", [P, 2])
        b1c = sb("b1c", [128, KD])
        sorted_ok = sb("sorted_ok", [1, 1])
        flags = sb("flags", [1, 2 * L], i32)
        arena = sb("arena", [128, NT * NT * P // 2 + 1])
        work = sb("work", [128, 4856])

        def carve(area, at=0):
            where = [at]

            def take(parts, *shape, dt=fp32):
                n = 1
                for d in shape:
                    n *= d
                words = n if dt in (fp32, i32) else (n + 1) // 2
                v = area[0:parts, where[0]:where[0] + words]
                where[0] += words
                assert where[0] <= area.shape[1], (where, area.shape)
                if dt != fp32:
                    v = v.bitcast(dt)[:, 0:n]
                if len(shape) == 2:
                    v = v.rearrange("p (a b) -> p a b", a=shape[0])
                if len(shape) == 3:
                    v = v.rearrange("p (a b c) -> p a b c", a=shape[0], b=shape[1])
                return v
            return take

        table = arena[0:P, 0:NT * NT * P // 2 + 1].bitcast(fp16)[:, 0:NT * NT * P].rearrange(
            "p (j i d) -> p j i d", j=NT, i=NT)

        take = carve(work)
        tin = take(P, 2, D)
        xn = take(P, 2, D)
        pre = take(P, 2, D)
        base = take(P, 2, D)
        res = take(P, 2, D)
        tTs = take(128, 2, KD, P)
        W1 = take(128, KD, D)
        W2 = take(128, KD, D)
        b2bc = take(P, D)
        gabc = take(P, D)
        bebc = take(P, D)

        take = carve(arena)
        ones_row = take(1, 128)
        hmT = take(128, 2, KD, P)
        gT = take(128, 2, KF, P)
        wqkv = take(128, KD, 3 * D)
        bqkv = take(1, 3 * D)
        bqcol = take(128, KD)
        fc1 = take(128, KD, F)
        fc2 = take(128, KF, D)
        ngcol = take(128, KD)
        nbcol = take(128, KD)
        bf1 = take(128, KF)
        b1p = take(128, KF)
        bf2 = take(P, D)
        Gs = take(128, KD, D + 1)
        grow = take(1, D + 1)
        Ts = take(128, KD, D)
        trow = take(1, D)
        attn = take(128, KD, 128)
        attnT = take(128, KD, 128)
        amax = take(128, KD)
        asum = take(128, KD)
        arec = take(128, KD)
        wqT = take(128, KD, D)
        Mw = take(128, KD, D)
        crow = take(1, D)
        cbc = take(P, D)
        take = carve(arena, 13000)
        x_all = take(P, NT, D)
        xn4 = take(P, 4, D + 1)
        assert 13000 + NT * D + 4 * (D + 1) + 4 <= 20500
        take = carve(arena, 20500)
        dst_all = take(P, ET, dt=i32)
        dst_allf = take(P, ET)
        dst_next = take(P, 1, dt=i32)
        dst_nextf = take(P, 1)
        ones_col = take(P, ET)
        cmp_ = take(P, ET)
        cnt = take(P, NT)
        lo = take(1, NT + 1)
        span = take(1, NT)
        sflag = take(1, 4)
        start_f = take(1, NT)
        start_i = take(1, NT, dt=i32)
        wsrc = take(128, NT * KW, dt=i32)
        wdst = take(128, NT * KW, dt=i32)
        wsf = take(128, NT * KW)
        wdf = take(128, NT * KW)
        wbase = take(128, NT * KW)
        wt1 = take(128, NT * KW)
        wt2 = take(128, NT * KW)
        valid = take(128, NT * KW)
        take = carve(work)
        s1v = take(128, NT, KW, dt=fp16)
        s0p = take(128, NT, KW, dt=fp16)
        d0p = take(128, NT, KW, dt=fp16)
        iota25 = take(128, NT + 1, dt=fp16)
        iota0 = take(128, 128, dt=fp16)
        iota1 = take(128, 128, dt=fp16)
        tri = take(128, 128, dt=fp16)
        ones16 = take(128, 128, dt=fp16)
        OV = take(128, 2, KW, 2 * NT, dt=fp16)
        OR = take(128, KW, 128, dt=fp16)
        rk = take(128, 2, KW)
        rkm = take(128, KW)
        rkm1 = take(128, 1)
        rkT = take(1, 128)
        V = take(128, 2, 2 * NT)
        ohs = take(128, 8, 128, dt=fp16)
        ohd = take(128, 8, 128, dt=fp16)
        take = carve(arena, (NT - 1) * NT * P // 2)
        OH = take(128, 2, (KW + 1) * NT, dt=fp16)
        S2 = take(128, (KW + 2) * NT, dt=fp16)
        S4 = take(128, 2, KW * NT, dt=fp16)
        OHR = take(128, KW, NT)
        take = carve(arena)
        iota_n = take(P, N)
        onehot = take(P, 2, N)
        rows = take(P, 2, D)
        src_sb = take(P, ET, dt=i32)
        dst_sb = take(P, ET, dt=i32)
        dst_f = take(P, ET)
        idx = take(P, 2, dt=i32)
        take = carve(arena)
        tinh = take(P, 2, D)
        tinm = take(P, 2, D)
        gTe = take(128, 2, KD, P)
        tT = take(128, KD, N)
        acc = take(P, NT, D)
        w1e = take(128, X * KD, D)
        w2e = take(128, X * KD, D)
        rwT = take(128, KD, X)
        lg = take(P, 2, X)
        pr = take(P, 2, X)
        key = take(P, 2, X)
        oh1 = take(P, 2, X)
        oh2 = take(P, 2, X)
        rank8 = take(P, X)
        euler = take(P, X)
        rmax = take(P, 2, 8)
        comb = take(P, NT, X)
        cslot = take(P, 2, X)
        combT = take(X, 2, P)
        eb1 = take(128, X, KD)
        eb2 = take(X, D)

        bank = [ctx.enter_context(nc.psum_tensor(f"bank{i}", [128, 512], fp32)) for i in range(8)]

        s_const, s_clear, s_wld, s_eps = sem("s_const"), sem("s_clear"), sem("s_wld"), sem("s_eps")
        x_ld = sems("x_ld", 4); xn_st = sems("xn_st", 4)
        s_bn, s_mv, s_ve, s_rs, s_xn = sem("s_bn"), sem("s_mv"), sem("s_ve"), sem("s_rs"), sem("s_xn")
        s_xT, s_zT, s_G = sem("s_xT"), sem("s_zT"), sem("s_G")
        f_pe, f_dve, f_act = sem("f_pe"), sem("f_dve"), sem("f_act")
        s_hi, s_lo = sem("s_hi"), sem("s_lo")
        w_ld, w_pool, w_dve, w_pe, w_win = sem("w_ld"), sem("w_pool"), sem("w_dve"), sem("w_pe"), sem("w_win")
        b_oh, b_s2, b_s4, b_ov, b_rank, b_x = sem("b_oh"), sem("b_s2"), sem("b_s4"), sem("b_ov"), sem("b_rank"), sem("b_x")
        b_rk, b_or, b_v, b_vs, b_g, b_tab, b_ev = (sem("b_rk"), sem("b_or"), sem("b_v"), sem("b_vs"), sem("b_g"),
                                                   sem("b_tab"), sem("b_ev"))
        w_step, w_tri = sem("w_step"), sem("w_tri")
        b_m, b_flag, b_abs, b_oa = sem("b_m"), sem("b_flag"), sem("b_abs"), sem("b_oa")
        d_mm, l_sum = sem("d_mm"), sem("l_sum")
        d_first, a_first = sem("d_first"), sem("a_first")
        a_slow = sem("a_slow")
        z_T, z_cp = sem("z_T"), sem("z_cp"); z_ld = sems("z_ld")
        l_hi, l_lo = sem("l_hi"), sem("l_lo")
        m_ld = sems("m_ld"); m_st = sems("m_st")
        m_xTs, m_xf, m_xb, m_pre = sem("m_xTs"), sem("m_xf"), sem("m_xb"), sem("m_pre")
        m_bn, m_mv, m_ve, m_rs, m_hm = sem("m_bn"), sem("m_mv"), sem("m_ve"), sem("m_rs"), sem("m_hm")
        m_r1, m_res, m_hT, m_hTs, m_f1 = sem("m_r1"), sem("m_res"), sem("m_hT"), sem("m_hTs"), sem("m_f1")
        m_g, m_f2, m_out = sem("m_g"), sem("m_f2"), sem("m_out")
        a_tab, a_iota, a_idx, a_oh, a_mm, a_add = (sem("a_tab"), sem("a_iota"), sem("a_idx"), sem("a_oh"),
                                                   sem("a_mm"), sem("a_add"))
        a_dst = sem("a_dst")
        a_row = sems("a_row")
        l_w, l_open = sem("l_w"), sem("l_open")
        l_ld = sems("l_ld"); l_st = sems("l_st")
        l_m1, l_re, l_m2, l_hb, l_pre = sem("l_m1"), sem("l_re"), sem("l_m2"), sem("l_hb"), sem("l_pre")
        l_bn, l_mv, l_ve, l_rs, l_nrm = sem("l_bn"), sem("l_mv"), sem("l_ve"), sem("l_rs"), sem("l_nrm")
        l_be, l_h, l_hT, l_zT = sem("l_be"), sem("l_h"), sem("l_hT"), sem("l_zT")
        e_w, e_rw = sem("e_w"), sem("e_rw")
        t_ld = sems("t_ld"); t_ld2 = sems("t_ld2")
        t_x2, t_bn, t_mv, t_ve, t_rs, t_t = (sem("t_x2"), sem("t_bn"), sem("t_mv"), sem("t_ve"), sem("t_rs"), sem("t_t"))
        t_acc, t_T, t_Ts, t_cp, t_lg, t_lgs = (sem("t_acc"), sem("t_T"), sem("t_Ts"), sem("t_cp"), sem("t_lg"), sem("t_lgs"))
        r_d, r_p, r_max, r_op, r_const = sem("r_d"), sem("r_p"), sem("r_max"), sem("r_op"), sem("r_const")
        c_sl, c_T, c_Ts, c_b, c_acc = sem("c_sl"), sem("c_T"), sem("c_Ts"), sem("c_b"), sem("c_acc")
        x_m1, x_g, x_m2, x_acc, x_out = sem("x_m1"), sem("x_g"), sem("x_m2"), sem("x_acc"), sem("x_out")

        past = {e.engine: sem(f"past_{n}") for n, e in (('sp', nc.sync), ('pe', nc.tensor), ('dve', nc.vector),
                                                        ('act', nc.scalar), ('pool', nc.gpsimd))}

        x_t = x.rearrange("(t p) d -> t p d", p=P)

        def part_of(t, part):
            return Hs[:, bass.ds(t, 1), part, :].rearrange("p a d -> p (a d)")

        def row_of(area, t):
            return area[:, bass.ds(t, 1), :].rearrange("p a d -> p (a d)")

        def acc_of(t):
            return row_of(acc, t)

        def rows_of(t):
            return bass.ds(t * P, P)

        def over_tiles(t, j):
            return t[:, bass.ds(j, 1), :].rearrange("p a k -> p k a").broadcast_to([128, KW, NT])

        block = ctx.enter_context(nc.Block())

        def alone(eng):
            eng.sem_inc(past[eng.engine], 1)

        KA = 11
        def experts_of(unit_steps, between):
            steps = []
            for e in range(X):
                more = between.get(e, [])
                steps += more if isinstance(more, list) else [more]
                for delay, make in unit_steps:
                    steps.append((X_LAG + (e < delay), make((e - delay) % X)))
            return steps

        X_LAG = 5
        NE = KD + 1 + 2 * 4
        T_WIN = 8
        NW = 9
        NU = KD * NC

        @block.sync
        def _(sp):
            sp.dma_start(eps1[:, 0:L], geps.rearrange("(a l) -> a l", a=1).broadcast_to([128, L])).then_inc(s_eps, 16)

            def load_x(first, count, nth):
                sp.dma_start(x_all[:, first:first + count, :],
                             x[first * P:(first + count) * P, :].rearrange("(t p) d -> p t d", p=P)).then_inc(x_ld[nth], 16)

            load_x(0, 1, 0)
            load_x(1, 2, 1)
            load_x(3, 5, 2)

            def store_xn(t, s, turn):
                sp.wait_ge(s_xn, t + 1)
                sp.dma_start(h_dram[rows_of(t), :], xn4[:, s, 0:D]).then_inc(xn_st[s], 16)

            def load_more(t, s, turn):
                if not isinstance(t, int):
                    return
                if t < 3:
                    load_x(8 + 6 * t, (6, 6, 5)[t], 3)
                if t == 4:
                    sp.dma_start(wqkv[:, :, :], w_qkv.rearrange("(k p) n -> p k n", p=128)).then_inc(s_wld, 16)
                if t == 6:
                    sp.dma_start(fc1[:, :, :], w_fc1.rearrange("(k p) n -> p k n", p=128)).then_inc(s_wld, 16)
                if t == 8:
                    sp.dma_start(fc2[:, :, :], w_fc2.rearrange("(k p) n -> p k n", p=128)).then_inc(s_wld, 16)
                if t == 10:
                    sp.dma_start(bqkv[:, :], b_qkv.rearrange("(a n) -> a n", a=1)).then_inc(s_wld, 16)
                    sp.dma_start(bqcol[:, :], b_qkv[0:D].rearrange("(k p) -> p k", p=128)).then_inc(s_wld, 16)
                    sp.dma_start(ngcol[:, :], norm_g.rearrange("(k p) -> p k", p=128)).then_inc(s_wld, 16)
                    sp.dma_start(nbcol[:, :], norm_b.rearrange("(k p) -> p k", p=128)).then_inc(s_wld, 16)
                    sp.dma_start(bf1[:, :], b_fc1.rearrange("(k p) -> p k", p=128)).then_inc(s_wld, 16)
                    sp.dma_start(bf2[:, :], b_fc2.rearrange("(a n) -> a n", a=1).broadcast_to([P, D])).then_inc(s_wld, 16)
                if t == 11:
                    sp.dma_start(dst_all[:, :], dst.rearrange("(p t) -> p t", p=P)).then_inc(w_ld, 16)
                    sp.wait_ge(w_pool, 1)
                    sp.dma_start(dst_next[0:P - 1, :], dst[ET:E].rearrange("(p t) -> p t", t=ET)[:, 0:1]).then_inc(w_ld, 16)

            pipelined(sp, [(0, store_xn), (0, load_more)], NT, unroll=4, head=12)
            for s in range(4):
                sp.wait_ge(xn_st[s], 16 * ((NT + 3 - s) // 4))

            def load_mix(t, s, turn):
                if not (isinstance(t, int) and t < 2):
                    sp.wait_ge(m_xb, t - 1)
                sp.dma_start(tin[:, s, :], h_dram[rows_of(t), :]).then_inc(m_ld[s], 16)

            def store_mix(t, s, turn):
                sp.wait_ge(m_out, t + 1)
                sp.dma_start(acc_dram[rows_of(t), :], res[:, s, :]).then_inc(m_st[s], 16)

            def load_windows(t, s, turn):
                if isinstance(t, int) and t == 0:
                    sp.wait_ge(w_dve, 2)
                for j in (2 * t, 2 * t + 1):
                    if not isinstance(t, int) or j < NT:
                        at = sp.value_load(start_i[0:1, bass.ds(j, 1)], min_val=0, max_val=E - WIN)
                        sp.dma_start(wsrc[:, bass.ds(j * KW, KW)], src[bass.ds(at, WIN)].rearrange("(p k) -> p k", p=128)).then_inc(w_win, 16)
                        sp.dma_start(wdst[:, bass.ds(j * KW, KW)], dst[bass.ds(at, WIN)].rearrange("(p k) -> p k", p=128)).then_inc(w_win, 16)

            pipelined(sp, [(11, store_mix), (0, load_mix), (12, load_windows)], NT)
            sp.wait_ge(m_st[0], 16 * (NT - NT // 2))
            sp.wait_ge(m_st[1], 16 * (NT // 2))

            sp.wait_ge(b_ev, NT * NG)
            sp.wait_ge(b_flag, 1)
            def load_tokens(t, s):
                sp.dma_start(tinh[:, s, :], h_dram[rows_of(t), :]).then_inc(t_ld[s], 16)
                sp.dma_start(tinm[:, s, :], acc_dram[rows_of(t), :]).then_inc(t_ld2[s], 16)

            def layer(l, last):
                sp.sem_inc(l_open, 1)
                sp.dma_start(W1[:, :, :], gW1[bass.ds(l, 1), :, :].rearrange("a (k p) n -> p (a k) n", p=128)).then_inc(l_w, 16)
                sp.dma_start(W2[:, :, :], gW2[bass.ds(l, 1), :, :].rearrange("a (k p) n -> p (a k) n", p=128)).then_inc(l_w, 16)
                sp.dma_start(b1c[:, :], gb1[bass.ds(l, 1), :].rearrange("a (k p) -> p (a k)", p=128)).then_inc(l_w, 16)
                sp.dma_start(b2bc[:, :], gb2[bass.ds(l, 1), :].broadcast_to([P, D])).then_inc(l_w, 16)
                sp.dma_start(gabc[:, :], ggamma[bass.ds(l, 1), :].broadcast_to([P, D])).then_inc(l_w, 16)
                sp.dma_start(bebc[:, :], gbeta[bass.ds(l, 1), :].broadcast_to([P, D])).then_inc(l_w, 16)

                def load_h(t, s, turn):
                    if not (isinstance(t, int) and t < 2):
                        sp.wait_ge(l_hb, l * NT + t - 1)
                    sp.dma_start(tin[:, s, :], h_dram[rows_of(t), :]).then_inc(l_ld[s], 16)

                def store_h(t, s, turn):
                    sp.wait_ge(l_h, l * NT + t + 1)
                    sp.dma_start(h_dram[rows_of(t), :], res[:, s, :]).then_inc(l_st[s], 16)

                sp.wait_ge(l_sum, l + 1)
                def load_experts(t, s, turn):
                    if last and isinstance(t, int) and t < 7:
                        if t < KD:
                            k = t
                            sp.dma_start(rwT[:, k, :], router_w[:, k * 128:(k + 1) * 128].rearrange("e p -> p e")).then_inc(e_rw, 16)
                            sp.dma_start(eb1[:, :, k], e_b1[:, k * 128:(k + 1) * 128].rearrange("e p -> p e")).then_inc(e_w, 16)
                        elif t == KD:
                            sp.dma_start(eb2[:, :], e_b2).then_inc(e_w, 16)
                        else:
                            x0 = (t - KD - 1) * X // 4
                            sp.dma_start(w1e[:, x0 * KD:(x0 + X // 4) * KD, :],
                                         e_w1[x0:x0 + X // 4, :, :].rearrange("x (k p) d -> p (x k) d", p=128)).then_inc(e_w, 16)
                            sp.dma_start(w2e[:, x0 * KD:(x0 + X // 4) * KD, :],
                                         e_w2[x0:x0 + X // 4, :, :].rearrange("x (k p) d -> p (x k) d", p=128)).then_inc(e_w, 16)

                pipelined(sp, [(6, store_h), (0, load_h), (0, load_experts)], NT)
                if last:
                    load_tokens(0, 0)
                    load_tokens(1, 1)
                sp.wait_ge(l_st[0], 16 * (NT - NT // 2) * (l + 1))
                alone(sp)
                sp.wait_ge(l_st[1], 16 * (NT // 2) * (l + 1))
                alone(sp)
                sp.wait_ge(l_zT, NT * (l + 1))
                alone(sp)
                sp.wait_ge(l_lo, NT * (l + 1))
                alone(sp)

            with sp.Fori(0, L - 1) as l:
                layer(l, False)
            layer(L - 1, True)

            def load_rest(t, s, turn):
                if not (isinstance(t, int) and t < 2):
                    sp.wait_ge(t_x2, t - 1)
                    load_tokens(t, s)

            def store_out(t, s, turn):
                sp.wait_ge(x_acc, X * (t + 1))
                sp.wait_ge(c_acc, t + 1)
                sp.dma_start(out[rows_of(t), :], acc_of(t)).then_inc(x_out, 16)

            pipelined(sp, [(0, load_rest), (8, store_out)], NT)
            sp.wait_ge(x_out, 16 * NT)

        @block.tensor
        def _(pe):
            mm = nc.tensor.matmul
            pe.wait_ge(s_const, 5)

            def first(t):
                return isinstance(t, int) and t == 0

            def last(t):
                return isinstance(t, int) and t == NT - 1

            def norm_x(t, s, turn):
                pe.wait_ge(s_xn, t + 1)
                if not (isinstance(t, int) and t < 2):
                    pe.wait_ge(s_zT, t - 1)
                for k in range(KD):
                    i = nc.tensor.transpose(bank[s % 2][:, k * P:(k + 1) * P], xn4[:, s, k * 128:(k + 1) * 128], ident[0:P, 0:P])
                i.then_inc(s_xT, 1)
                for k in range(KD):
                    i = mm(bank[2 + k][:, 0:D + 1], lhsT=xn4[:, s, k * 128:(k + 1) * 128], rhs=xn4[:, s, :],
                           start=first(t), stop=last(t))
                i.then_inc(s_G, 1)

            pipelined(pe, [(3, norm_x)], NT, unroll=4, head=4)

            pe.wait_ge(s_wld, 16 * NW)
            pe.wait_ge(s_zT, NT)
            pe.wait_ge(f_dve, 1)
            for k in range(KD):
                i = mm(bank[4][0:1, k * 128:(k + 1) * 128], lhsT=Gs[:, k, D:D + 1], rhs=ident[:, :], start=True, stop=True)
            i.then_inc(f_pe, 1)
            for k in range(KD):
                for a in range(KD):
                    i = nc.tensor.transpose(bank[5][:, (a * KD + k) * 128:(a * KD + k + 1) * 128],
                                            wqkv[:, k, a * 128:(a + 1) * 128], ident[:, :])
            i.then_inc(f_pe, 1)
            for m in range(KF):
                for k in range(KD):
                    i = mm(bank[6][:, m:m + 1], lhsT=fc1[:, k, m * 128:(m + 1) * 128], rhs=nbcol[:, k:k + 1],
                           start=(k == 0), stop=(k == KD - 1))
            i.then_inc(f_pe, 1)
            pe.wait_ge(f_dve, 2)
            for m in range(KD + 1):
                cols = slice(m * 128, (m + 1) * 128) if m < KD else slice(D, D + 1)
                o = bank[m][:, 0:D] if m < KD else bank[4][0:1, 0:D]
                for k in range(KD):
                    mm(o, lhsT=Gs[:, k, cols], rhs=wqkv[:, k, 2 * D:3 * D], start=(k == 0), stop=False)
                i = mm(o, lhsT=grow[0:1, cols], rhs=bqkv[0:1, 2 * D:3 * D], start=False, stop=True)
            i.then_inc(f_pe, 1)
            pe.wait_ge(f_dve, 5)
            for a in range(KD):
                for k in range(KD):
                    mm(bank[7][:, a * 128:(a + 1) * 128], lhsT=wqkv[:, k, D + a * 128:D + (a + 1) * 128],
                       rhs=Ts[:, k, a * 128:(a + 1) * 128], start=(k == 0), stop=False)
                i = mm(bank[7][:, a * 128:(a + 1) * 128], lhsT=bqkv[0:1, D + a * 128:D + (a + 1) * 128],
                       rhs=trow[0:1, a * 128:(a + 1) * 128], start=False, stop=True)
            i.then_inc(f_pe, 1)
            pe.wait_ge(f_dve, 7)
            for a in range(KD):
                i = nc.tensor.transpose(bank[5][:, a * 128:(a + 1) * 128], attn[:, a, :], ident[:, :])
            i.then_inc(f_pe, 1)
            pe.wait_ge(f_dve, 8)
            for m in range(KD):
                for a in range(KD):
                    mm(bank[m][:, a * 128:(a + 1) * 128], lhsT=wqT[:, a, m * 128:(m + 1) * 128], rhs=attnT[:, a, :],
                       start=True, stop=True)
            for a in range(KD):
                i = mm(bank[4][0:1, a * 128:(a + 1) * 128], lhsT=bqcol[:, a:a + 1], rhs=attnT[:, a, :], start=True, stop=True)
            i.then_inc(f_pe, 1)
            pe.wait_ge(f_dve, 9)
            mm(bank[6][0:P, 0:D], lhsT=ones_row[0:1, 0:P], rhs=crow[0:1, :], start=True, stop=True).then_inc(f_pe, 1)
            pe.wait_ge(f_dve, 10)

            def mix_count(t, s, turn):
                if isinstance(t, int) and t == T_WIN:
                    pe.wait_ge(w_dve, 1)
                    mm(bank[0][0:1, 0:NT], lhsT=ones_col[:, 0:1], rhs=cnt[:, :], start=True, stop=True).then_inc(w_pe, 1)

            def mix_xf(t, s, turn):
                pe.wait_ge(m_xTs, t + 1)
                if not (isinstance(t, int) and t == 0):
                    pe.wait_ge(m_pre, t)
                for k in range(KD):
                    i = mm(bank[2][0:P, 0:D], lhsT=tTs[:, s, k, :], rhs=Mw[:, k, :], start=(k == 0), stop=(k == KD - 1))
                i.then_inc(m_xf, 1)

            def mix_hT(t, s, turn):
                pe.wait_ge(m_hm, t + 1)
                if not (isinstance(t, int) and t == 0):
                    pe.wait_ge(m_hTs, t)
                for k in range(KD):
                    i = nc.tensor.transpose(bank[1][:, k * P:(k + 1) * P], xn[:, s, k * 128:(k + 1) * 128], ident[0:P, 0:P])
                i.then_inc(m_hT, 1)

            def mix_f1(t, s, turn):
                pe.wait_ge(m_hTs, t + 1)
                if not (isinstance(t, int) and t < 2):
                    pe.wait_ge(m_g, t - 1)
                for m in range(KF):
                    o = bank[4 + 2 * s + m // 4][:, m % 4 * P:(m % 4 + 1) * P]
                    for k in range(KD):
                        i = mm(o, lhsT=fc1[:, k, m * 128:(m + 1) * 128], rhs=hmT[:, s, k, :], start=(k == 0), stop=(k == KD - 1))
                i.then_inc(m_f1, 1)

            def mix_f2(t, s, turn):
                pe.wait_ge(m_g, t + 1)
                if not (isinstance(t, int) and t == 0):
                    pe.wait_ge(m_out, t)
                for k in range(KF):
                    i = mm(bank[3][0:P, 0:D], lhsT=gT[:, s, k, :], rhs=fc2[:, k, :], start=(k == 0), stop=(k == KF - 1))
                i.then_inc(m_f2, 1)

            pipelined(pe, [(10, mix_f2), (8, mix_f1), (6, mix_hT), (2, mix_xf), (2, mix_count)], NT)
            pe.wait_ge(m_out, NT)

            def rank(j, s, turn):
                pe.wait_ge(b_s4, j + 1)
                if not (isinstance(j, int) and j < 2):
                    pe.wait_ge(b_x, j - 1)
                mm(bank[s][:, 0:KW * NT], lhsT=tri[:, :], rhs=OH[:, s, NT:], start=True, stop=False)
                for k in range(1, KW, 4):
                    i = mm(bank[s][:, k * NT:KW * NT], lhsT=ones16[:, :], rhs=S4[:, s, 0:(KW - k) * NT],
                           start=False, stop=(k + 4 >= KW))
                i.then_inc(b_rank, 1)

            def permute(j, s, turn):
                pe.wait_ge(b_or, j + 1)
                pe.wait_ge(b_oa, j + 1)
                pe.wait_ge(b_ov, j + 1)
                if not (isinstance(j, int) and j < 2):
                    pe.wait_ge(b_vs, j - 1)
                for k in range(KW):
                    i = mm(bank[2 + s][:, 0:2 * NT], lhsT=OR[:, k, :], rhs=OV[:, s, k, :], start=(k == 0), stop=(k == KW - 1))
                i.then_inc(b_v, 1)

            def count(g):
                def fn(j, s, turn):
                    q = (s * NG + g) % 2
                    pe.wait_ge(b_g, j * NG + g + 1)
                    if not (isinstance(j, int) and j * NG + g < 2):
                        pe.wait_ge(b_ev, j * NG + g - 1)
                    for ii in range(min(4, NT - 4 * g)):
                        i = mm(bank[4 + q][0:P, ii * P:(ii + 1) * P], lhsT=ohs[:, 4 * q + ii, 0:P], rhs=ohd[:, 4 * q + ii, 0:P],
                               start=True, stop=True)
                    i.then_inc(b_tab, 1)
                return fn

            def first_sums(g):
                def fn(t, s, turn):
                    end = isinstance(t, int) and t == NT - 1
                    w = 1 if end else 2
                    for f in ((0, 1) if end else (s,)):
                        if g == 0:
                            if isinstance(t, int) and t == 0:
                                pe.wait_ge(s_lo, NT)
                            pe.wait_ge(b_ev, NG * NT if end else (t - s + 2) * NG)
                            if not (isinstance(t, int) and t < 2):
                                pe.wait_ge(a_first, t - 1 + f * end)
                        for i in range(g * NT // NG, (g + 1) * NT // NG):
                            for part in range(2):
                                ins = mm(bank[6 + f][:, 0:w * P], lhsT=Hs[:, i, part, f * 128:(f + 1) * 128],
                                         rhs=table[:, bass.ds(t - (0 if end else s), w), i, :],
                                         start=(i == 0 and part == 0), stop=(i == NT - 1 and part == 1))
                        if g == NG - 1:
                            ins.then_inc(d_first, 1)
                return fn

            pipelined(pe, [(2, permute), (0, rank)] + [st for g in range(NG) for st in ((3, count(g)), (6, first_sums(g)))], NT)
            pe.wait_ge(a_first, NT + 1)
            pe.sem_inc(d_mm, NU)

            pe.wait_ge(b_m, NT + 1)
            nc.tensor.transpose(bank[6][0:1, 0:128], rkm1, ident[:, :]).then_inc(w_pe, 1)
            pe.wait_ge(b_flag, 1)
            pe.wait_ge(b_ev, NT * NG)

            with pe.Fori(0, L) as l:
                pe.wait_ge(l_open, l + 1)
                by_table = pe.value_load(flags[0:1, bass.ds(l, 1)], min_val=0, max_val=1)
                with pe.If(by_table):

                    def dense(c, w, nth):
                        for f in range(KD):
                            b = 2 * (nth % 2) + f
                            if not (isinstance(c, int) and c < 2):
                                pe.wait_ge(a_add, l * NU + KD * (c - 2) + f + 1)
                            for i in range(NT):
                                for part in range(2):
                                    ins = mm(bank[b][:, 0:w * P], lhsT=Hs[:, i, part, f * 128:(f + 1) * 128],
                                             rhs=table[:, bass.ds(4 * c, w), i, :],
                                             start=(i == 0 and part == 0), stop=(i == NT - 1 and part == 1))
                            ins.then_inc(d_mm, 1)

                    dense(0, 4, 0)
                    dense(1, 4, 1)
                    with pe.Fori(1, (NC - 1) // 2) as turn:
                        dense(2 * turn, 4, 0)
                        dense(2 * turn + 1, 4, 1)
                    dense(NC - 1, NT - 4 * (NC - 1), 0)
                without = pe.value_load(flags[0:1, bass.ds(l + L, 1)], min_val=0, max_val=1)
                with pe.If(without):
                    def h_again(t, s, turn):
                        pe.wait_ge(z_ld[s], 16 * (l * ((NT + 1 - s) // 2) + turn + 1))
                        if not (isinstance(t, int) and t < 2):
                            pe.wait_ge(z_cp, l * NT + t - 1)
                        for k in range(KD):
                            i = nc.tensor.transpose(bank[s][:, k * P:(k + 1) * P], rows[:, s, k * 128:(k + 1) * 128], ident[0:P, 0:P])
                        i.then_inc(z_T, 1)

                    pipelined(pe, [(0, h_again)], NT)
                    pe.wait_ge(z_cp, (l + 1) * NT)

                    for f in range(KD):
                        def agg(t, s, turn):
                            pe.wait_ge(a_row[s], 16 * ((l * KD + f) * (ET // 2) + turn + 1))
                            pe.wait_ge(a_oh, (l * KD + f) * ET + t + 1)
                            for c in range(NC):
                                w = min(CH, N - c * CH)
                                i = mm(bank[c][:, 0:w], lhsT=rows[:, s, f * 128:(f + 1) * 128], rhs=onehot[:, s, c * CH:c * CH + w],
                                       start=(isinstance(t, int) and t == 0), stop=(isinstance(t, int) and t == ET - 1))
                            i.then_inc(a_mm, 1)

                        if f:
                            pe.wait_ge(a_slow, l * NU + f * NC)
                        agg(0, 0, 0)
                        agg(1, 1, 0)
                        with pe.Fori(1, ET // 2 - 1) as turn:
                            agg(2 * turn, 0, turn)
                            agg(2 * turn + 1, 1, turn)
                        agg(ET - 2, 0, ET // 2 - 1)
                        agg(ET - 1, 1, ET // 2 - 1)

                pe.wait_ge(l_sum, l + 1)
                pe.wait_ge(l_w, (l + 1) * 96)

                def mlp1(t, s, turn):
                    if not (isinstance(t, int) and t < 2):
                        pe.wait_ge(l_re, l * NT + t - 1)
                    for m in range(KD):
                        for k in range(KD):
                            i = mm(bank[s][:, m * P:(m + 1) * P], lhsT=W1[:, k, m * 128:(m + 1) * 128],
                                   rhs=zT[:, k, rows_of(t)], start=(k == 0), stop=(k == KD - 1))
                    i.then_inc(l_m1, 1)

                def mlp2(t, s, turn):
                    pe.wait_ge(l_re, l * NT + t + 1)
                    if not (isinstance(t, int) and t < 2):
                        pe.wait_ge(l_pre, l * NT + t - 1)
                    for k in range(KD):
                        i = mm(bank[2 + s][0:P, 0:D], lhsT=tTs[:, s, k, :], rhs=W2[:, k, :], start=(k == 0), stop=(k == KD - 1))
                    i.then_inc(l_m2, 1)

                def h_T(t, s, turn):
                    pe.wait_ge(l_h, l * NT + t + 1)
                    if not (isinstance(t, int) and t < 2):
                        pe.wait_ge(l_zT, l * NT + t - 1)
                    for k in range(KD):
                        i = nc.tensor.transpose(bank[4 + s][:, k * P:(k + 1) * P], res[:, s, k * 128:(k + 1) * 128], ident[0:P, 0:P])
                    i.then_inc(l_hT, 1)

                pipelined(pe, [(7, h_T), (2, mlp2), (0, mlp1)], NT)
                pe.wait_ge(l_zT, (l + 1) * NT)

            pe.wait_ge(e_rw, 16 * KD)
            pe.wait_ge(e_w, 16 * NE)
            pe.wait_ge(l_zT, L * NT)

            def tok_T(t, s, turn):
                pe.wait_ge(t_t, t + 1)
                if not (isinstance(t, int) and t == 0):
                    pe.wait_ge(t_cp, t)
                for k in range(KD):
                    i = nc.tensor.transpose(bank[4][:, k * P:(k + 1) * P], xn[:, s, k * 128:(k + 1) * 128], ident[0:P, 0:P])
                i.then_inc(t_T, 1)

            def tok_lg(t, s, turn):
                pe.wait_ge(t_Ts, t + 1)
                if not (isinstance(t, int) and t == 0):
                    pe.wait_ge(t_lgs, t)
                for k in range(KD):
                    i = mm(bank[5][0:P, 0:X], lhsT=tTs[:, s, k, :], rhs=rwT[:, k, :], start=(k == 0), stop=(k == KD - 1))
                i.then_inc(t_lg, 1)

            def cmb_T(t, s, turn):
                pe.wait_ge(c_sl, t + 1)
                if not (isinstance(t, int) and t == 0):
                    pe.wait_ge(c_Ts, t)
                nc.tensor.transpose(bank[6][0:X, 0:P], cslot[:, s, :], ident[0:P, 0:P]).then_inc(c_T, 1)

            def cmb_b(t, s, turn):
                pe.wait_ge(c_Ts, t + 1)
                if not (isinstance(t, int) and t == 0):
                    pe.wait_ge(c_acc, t)
                mm(bank[7][0:P, 0:D], lhsT=combT[:, s, :], rhs=eb2[:, :], start=True, stop=True).then_inc(c_b, 1)

            def exp1(e):
                def fn(t, s, turn):
                    if e == 0:
                        pe.wait_ge(t_cp, t + 1)
                    if not (isinstance(t, int) and t * X + e < 2):
                        pe.wait_ge(x_g, t * X + e - 1)
                    for m in range(KD):
                        for k in range(KD):
                            i = mm(bank[e % 2][:, m * P:(m + 1) * P], lhsT=w1e[:, e * KD + k, m * 128:(m + 1) * 128],
                                   rhs=tT[:, k, rows_of(t)], start=(k == 0), stop=(k == KD - 1))
                    i.then_inc(x_m1, 1)
                return fn

            def exp2(e):
                def fn(t, s, turn):
                    pe.wait_ge(x_g, t * X + e + 1)
                    if not (isinstance(t, int) and t * X + e < 2):
                        pe.wait_ge(x_acc, t * X + e - 1)
                    for k in range(KD):
                        i = mm(bank[2 + e % 2][0:P, 0:D], lhsT=gTe[:, e % 2, k, :], rhs=w2e[:, e * KD + k, :],
                               start=(k == 0), stop=(k == KD - 1))
                    i.then_inc(x_m2, 1)
                return fn

            between = {3: (2, tok_T), 5: (3, tok_lg), 6: (5, cmb_T), 7: (6, cmb_b)}
            pipelined(pe, experts_of([(2, exp2), (0, exp1)], between), NT)

        @block.vector
        def _(dve):
            v = nc.vector
            v.memset(xn4[:, :, D:D + 1], 1.0).then_inc(s_const, 1)
            v.memset(grow[0:1, D:D + 1], float(N)).then_inc(s_const, 1)
            dve.wait_ge(s_eps, 16)
            v.tensor_scalar(eps1[:, :], eps1[:, :], 1.0, None, ALU.add).then_inc(s_const, 1)

            def stats(t, s, turn):
                early = isinstance(t, int) and t < 8
                dve.wait_ge(x_ld[(0 if t == 0 else 1 if t < 3 else 2) if early else 3], 16 if early else 48)
                alone(dve)
                v.bn_stats(st[:, s % 2, :], row_of(x_all, t)).then_inc(s_bn, 1)
                dve.wait_ge(s_bn, t + 1)
                alone(dve)
                v.bn_aggr(mv[:, s % 2, :], st[:, s % 2, :]).then_inc(s_mv, 1)

            def norm(t, s, turn):
                dve.wait_ge(s_rs, t + 1)
                if not (isinstance(t, int) and t < 4):
                    dve.wait_ge(s_G, t - 3)
                    dve.wait_ge(xn_st[s], 16 * turn)
                    dve.wait_ge(s_lo, t - 3)
                alone(dve)
                v.tensor_scalar(xn4[:, s, 0:D], row_of(x_all, t), mv[:, s % 2, 0:1], rs[:, s % 2:s % 2 + 1], ALU.subtract, ALU.mult).then_inc(s_xn, 1)

            def low(t, s, turn):
                dve.wait_ge(s_hi, t + 1)
                v.tensor_tensor(part_of(t, 1), xn4[:, s, 0:D], part_of(t, 0), ALU.subtract).then_inc(s_lo, 1)

            dve.wait_ge(s_const, 5)
            pipelined(dve, [(4, low), (2, norm), (0, stats)], NT, unroll=4, head=4)

            n_w = [0]

            def step(i):
                n_w[0] += 1
                i.then_inc(w_step, 1)
                dve.wait_ge(w_step, n_w[0])

            dve.wait_ge(w_ld, 32)
            dve.wait_ge(w_pool, 2)
            v.memset(ones_col[:, :], 1.0)
            v.tensor_copy(dst_nextf[:, :], dst_next[:, :])
            step(v.tensor_copy(dst_allf[:, :], dst_all[:, :]))

            next_tile = [1]

            def count_below(n):
                for j in range(next_tile[0], min(next_tile[0] + n, NT)):
                    step(v.scalar_tensor_tensor(cmp_[:, :], dst_allf[:, :], float(j * P), ones_col[:, :], ALU.is_lt,
                                                ALU.mult, accum_out=cnt[:, j - 1:j]))
                    next_tile[0] = j + 1

            dve.wait_ge(s_G, NT)
            for k in range(KD):
                i = v.tensor_copy(Gs[:, k, :], bank[2 + k][:, 0:D + 1])
            i.then_inc(f_dve, 1)
            dve.wait_ge(f_pe, 1)
            v.tensor_copy(grow[0:1, 0:D], bank[4][0:1, 0:D]).then_inc(f_dve, 1)
            dve.wait_ge(f_pe, 2)
            v.tensor_copy(wqT[:, :, :].rearrange("p a c -> p (a c)"), bank[5][:, 0:KD * D]).then_inc(f_dve, 1)
            dve.wait_ge(f_pe, 3)
            v.tensor_tensor(b1p[:, :], bank[6][:, 0:KF], bf1[:, :], ALU.add)
            for k in range(KD):
                i = v.tensor_scalar(fc1[:, k, :], fc1[:, k, :], ngcol[:, k:k + 1], None, ALU.mult)
            v.memset(attn[:, :, :], 0.0).then_inc(f_dve, 1)
            count_below(8)
            dve.wait_ge(f_pe, 4)
            for m in range(KD):
                v.tensor_copy(Ts[:, m, :], bank[m][:, 0:D])
            v.tensor_copy(trow[0:1, :], bank[4][0:1, 0:D]).then_inc(f_dve, 1)
            count_below(2)
            dve.wait_ge(f_pe, 5)
            for a in range(KD):
                for hh in range(2):
                    r = slice(hh * HD, (hh + 1) * HD)
                    i = v.reduce_max(amax[r, a:a + 1], bank[7][r, a * 128 + hh * HD:a * 128 + (hh + 1) * HD], AX.X)
            i.then_inc(r_d, 1)
            dve.wait_ge(r_d, 1)
            v.tensor_scalar(amax[:, :], amax[:, :], -float(HD) ** -0.5, None, ALU.mult).then_inc(f_dve, 1)
            dve.wait_ge(f_act, 1)
            v.reciprocal(arec[:, :], asum[:, :]).then_inc(r_d, 1)
            dve.wait_ge(r_d, 2)
            for a in range(KD):
                i = v.tensor_scalar(attn[:, a, :], attn[:, a, :], arec[:, a:a + 1], None, ALU.mult)
            i.then_inc(f_dve, 1)
            dve.wait_ge(f_pe, 6)
            v.tensor_copy(attnT[:, :, :].rearrange("p a c -> p (a c)"), bank[5][:, 0:D]).then_inc(f_dve, 1)
            count_below(4)
            dve.wait_ge(f_pe, 7)
            for m in range(KD):
                v.tensor_copy(Mw[:, m, :], bank[m][:, 0:D])
            v.tensor_copy(crow[0:1, :], bank[4][0:1, 0:D]).then_inc(f_dve, 1)
            dve.wait_ge(f_pe, 8)
            v.tensor_copy(cbc[:, :], bank[6][0:P, 0:D]).then_inc(f_dve, 1)

            def below(t, s, turn):
                if isinstance(t, int) and 2 <= t < T_WIN:
                    count_below((NT - 1 - next_tile[0]) // (T_WIN - t) + 1)
                if isinstance(t, int) and t == T_WIN:
                    step(v.tensor_tensor(cmp_[:, 0:ET - 1], dst_allf[:, 0:ET - 1], dst_allf[:, 1:ET], ALU.is_gt))
                    step(v.tensor_tensor(cmp_[:, ET - 1:ET], dst_allf[:, ET - 1:ET], dst_nextf[:, :], ALU.is_gt))
                    v.reduce_sum(cnt[:, NT - 1:NT], cmp_[:, :], AX.X).then_inc(w_dve, 1)

            def starts(t, s, turn):
                if not (isinstance(t, int) and t == T_WIN):
                    return
                dve.wait_ge(w_pe, 1)
                step(v.memset(lo[0:1, 0:1], 0.0))
                step(v.memset(lo[0:1, NT:NT + 1], float(E)))
                step(v.tensor_copy(lo[0:1, 1:NT], bank[0][0:1, 0:NT - 1]))
                step(v.tensor_copy(sflag[0:1, 0:1], bank[0][0:1, NT - 1:NT]))
                step(v.tensor_scalar(start_f[0:1, :], lo[0:1, 0:NT], float(E - WIN), None, ALU.min))
                step(v.tensor_copy(start_i[0:1, :], start_f[0:1, :]))
                step(v.tensor_tensor(span[0:1, :], lo[0:1, 1:NT + 1], lo[0:1, 0:NT], ALU.subtract))
                step(v.reduce_max(sflag[0:1, 1:2], span[0:1, :], AX.X))
                step(v.tensor_scalar(sflag[0:1, 2:3], sflag[0:1, 1:2], float(WIN), None, ALU.is_le))
                step(v.tensor_scalar(sflag[0:1, 3:4], sflag[0:1, 0:1], 0.5, None, ALU.is_lt))
                v.tensor_tensor(sorted_ok[0:1, :], sflag[0:1, 2:3], sflag[0:1, 3:4], ALU.mult).then_inc(w_dve, 1)

            def mix_pre(t, s, turn):
                dve.wait_ge(m_xf, t + 1)
                dve.wait_ge(m_xb, t + 1)
                if not (isinstance(t, int) and t < 2):
                    dve.wait_ge(m_res, t - 1)
                    dve.wait_ge(m_hm, t - 1)
                v.tensor_tensor(pre[:, s, :], bank[2][0:P, 0:D], base[:, s, :], ALU.add).then_inc(m_pre, 1)
                dve.wait_ge(m_pre, t + 1)
                v.bn_stats(st[:, s, :], pre[:, s, :]).then_inc(m_bn, 1)
                dve.wait_ge(m_bn, t + 1)
                alone(dve)
                v.bn_aggr(mv[:, s, :], st[:, s, :]).then_inc(m_mv, 1)

            def mix_norm(t, s, turn):
                dve.wait_ge(m_rs, t + 1)
                if not (isinstance(t, int) and t < 2):
                    dve.wait_ge(m_hT, t - 1)
                v.tensor_scalar(xn[:, s, 0:D], pre[:, s, :], mv[:, s, 0:1], rs[:, s:s + 1], ALU.subtract, ALU.mult).then_inc(m_hm, 1)

            def mix_out(t, s, turn):
                dve.wait_ge(m_f2, t + 1)
                dve.wait_ge(m_res, t + 1)
                if not (isinstance(t, int) and t < 2):
                    dve.wait_ge(m_st[s], 16 * turn)
                alone(dve)
                v.tensor_tensor(res[:, s, :], bank[3][0:P, 0:D], row_of(x_all, t), ALU.add).then_inc(m_out, 1)

            flat = "p a b -> p (a b)"

            def convert(t, s, turn):
                if not (isinstance(t, int) and t == NT - 1):
                    return
                W = NT * KW
                dve.wait_ge(w_win, 32 * NT)
                step(v.tensor_copy(wsf[:, :], wsrc[:, :]))
                step(v.tensor_copy(wdf[:, :], wdst[:, :]))
                step(v.tensor_tensor(wdf[:, :], wdf[:, :], wbase[:, :], ALU.subtract))
                step(v.tensor_scalar(wt1[:, :], wdf[:, :], 0.0, None, ALU.is_ge))
                step(v.scalar_tensor_tensor(valid[:, :], wdf[:, :], float(P), wt1[:, :], ALU.is_lt, ALU.mult))
                step(v.tensor_scalar(wt1[:, :], wsf[:, :], 1.0 / P, -(0.5 - 0.5 / P), ALU.mult, ALU.add))
                step(v.tensor_scalar(wt2[:, :], wt1[:, :], MAGIC, None, ALU.add))
                step(v.tensor_scalar(wt1[:, :], wt2[:, :], MAGIC, None, ALU.subtract))
                step(v.scalar_tensor_tensor(wt2[:, :], wt1[:, :], -float(P), wsf[:, :], ALU.mult, ALU.add))

            def tables(t, s, turn):
                if not (isinstance(t, int) and t == NT - 1):
                    return
                dve.wait_ge(m_xb, NT)
                dve.wait_ge(m_hT, NT)
                dve.wait_ge(m_xf, NT)
                step(v.tensor_scalar(s0p.rearrange(flat), wt2[:, :], 1.0, None, ALU.add))
                step(v.tensor_scalar(d0p.rearrange(flat), wdf[:, :], 1.0, None, ALU.add))
                step(v.scalar_tensor_tensor(wt2[:, :], wt1[:, :], 1.0, valid[:, :], ALU.add, ALU.mult))
                v.memset(ones16[:, :], 1.0)
                v.memset(rkm[:, :], 0.0)
                v.tensor_scalar(s1v.rearrange(flat), wt2[:, :], 1.0, None, ALU.subtract).then_inc(w_dve, 1)

            pipelined(dve, [(11, mix_out), (5, mix_norm), (3, mix_pre), (3, starts), (2, below), (7, convert), (9, tables)], NT)

            def sources(j, s, turn):
                if not (isinstance(j, int) and j < 2):
                    dve.wait_ge(b_rank, j - 1)
                    dve.wait_ge(b_x, j - 1)
                    dve.wait_ge(b_ov, j - 1)
                tiles = iota25[:, 0:NT].rearrange("p (a i) -> p a i", a=1).broadcast_to([128, KW, NT])
                v.tensor_tensor(OH[:, s, NT:].rearrange("p (k i) -> p k i", k=KW), over_tiles(s1v, j), tiles,
                                ALU.is_equal).then_inc(b_oh, 1)

            def rank_x(j, s, turn):
                dve.wait_ge(b_rank, j + 1)
                if not (isinstance(j, int) and j == 0):
                    dve.wait_ge(b_rk, j)
                v.tensor_tensor(OHR[:, :, :].rearrange(flat), bank[s][:, 0:KW * NT], OH[:, s, NT:], ALU.mult).then_inc(b_x, 1)
                dve.wait_ge(b_x, j + 1)
                if not (isinstance(j, int) and j < 2):
                    dve.wait_ge(b_or, j - 1)
                    dve.wait_ge(b_oa, j - 1)
                v.reduce_sum(rk[:, s, :], OHR[:, :, :], AX.X).then_inc(b_rk, 1)
                dve.wait_ge(b_rk, j + 1)
                v.tensor_tensor(rkm[:, :], rkm[:, :], rk[:, s, :], ALU.max).then_inc(b_m, 1)

            def ranks(j, s, turn):
                if isinstance(j, int) and j == 0:
                    dve.wait_ge(m_st[0], 16 * (NT - NT // 2))
                    dve.wait_ge(m_st[1], 16 * (NT // 2))
                else:
                    dve.wait_ge(b_v, j)
                for k in range(KA, KW):
                    i = v.tensor_scalar(OR[:, k, :], iota0[:, :], rk[:, s, k:k + 1], None, ALU.is_equal)
                i.then_inc(b_or, 1)

            def places(j, s, turn):
                dve.wait_ge(b_v, j + 1)
                if not (isinstance(j, int) and j < 2):
                    dve.wait_ge(b_g, (j - 1) * NG)
                v.tensor_copy(V[:, s, :], bank[2 + s][:, 0:2 * NT]).then_inc(b_vs, 1)
                dve.wait_ge(b_vs, j + 1)
                for g in range(NG):
                    q = (s * NG + g) % 2
                    if not (isinstance(j, int) and j * NG + g < 2):
                        dve.wait_ge(b_tab, j * NG + g - 1)
                    for ii in range(min(4, NT - 4 * g)):
                        c = 4 * g + ii
                        v.tensor_scalar(ohs[:, 4 * q + ii, :], iota1[:, :], V[:, s, c:c + 1], None, ALU.is_equal)
                        i = v.tensor_scalar(ohd[:, 4 * q + ii, :], iota1[:, :], V[:, s, NT + c:NT + c + 1], None, ALU.is_equal)
                    i.then_inc(b_g, 1)

            dve.wait_ge(w_pool, 3)
            dve.wait_ge(w_dve, 3)

            def first_add(t, s, turn):
                end = isinstance(t, int) and t == NT - 1
                w = 1 if end else 2
                for f in ((0, 1) if end else (s,)):
                    dve.wait_ge(d_first, t + 1 + f * end)
                    alone(dve)
                    sums = zT[:, f, bass.ds((t - (0 if end else s)) * P, w * P)]
                    v.scalar_tensor_tensor(sums, sums, eps1[:, 0:1], bank[6 + f][:, 0:w * P], ALU.mult, ALU.add).then_inc(a_first, 1)

            pipelined(dve, [(0, sources), (1, rank_x), (7, first_add), (3, places), (1, ranks)], NT)

            dve.wait_ge(b_m, NT)
            v.reduce_max(rkm1, rkm[:, :], AX.X).then_inc(b_m, 1)
            dve.wait_ge(w_pe, 2)
            step(v.reduce_max(rkT[0:1, 0:1], bank[6][0:1, 0:128], AX.X))
            step(v.tensor_scalar(rkT[0:1, 1:2], rkT[0:1, 0:1], 127.5, None, ALU.is_lt))
            step(v.tensor_tensor(rkT[0:1, 2:3], rkT[0:1, 1:2], sorted_ok[0:1, :], ALU.mult))
            step(v.memset(rkT[0:1, 8:9], 0.0))
            for l in range(1, L):
                i = v.tensor_copy(rkT[0:1, 8 + l:9 + l], rkT[0:1, 2:3])
            for l in range(L):
                i = v.tensor_scalar(rkT[0:1, 8 + L + l:9 + L + l], rkT[0:1, 2:3], -1.0, 1.0, ALU.mult, ALU.add)
            step(i)
            v.tensor_copy(flags[0:1, :], rkT[0:1, 8:8 + 2 * L]).then_inc(b_flag, 1)
            dve.wait_ge(b_flag, 1)
            dve.wait_ge(b_ev, NT * NG)
            dve.wait_ge(a_first, NT + 1)
            dve.sem_inc(a_add, NU)

            with dve.Fori(0, L) as l:
                dve.wait_ge(l_open, l + 1)
                by_table = dve.value_load(flags[0:1, bass.ds(l, 1)], min_val=0, max_val=1)
                with dve.If(by_table):
                    def add_sums(c, w, nth):
                        for f in range(KD):
                            b = 2 * (nth % 2) + f
                            dve.wait_ge(d_mm, l * NU + KD * c + f + 1)
                            part = zT[:, f, bass.ds(c * CH, w * P)]
                            alone(dve)
                            v.scalar_tensor_tensor(part, part, eps1[:, bass.ds(l, 1)], bank[b][:, 0:w * P], ALU.mult,
                                                   ALU.add).then_inc(a_add, 1)

                    add_sums(0, 4, 0)
                    add_sums(1, 4, 1)
                    with dve.Fori(1, (NC - 1) // 2) as turn:
                        add_sums(2 * turn, 4, 0)
                        add_sums(2 * turn + 1, 4, 1)
                    add_sums(NC - 1, NT - 4 * (NC - 1), 0)
                    dve.wait_ge(a_add, (l + 1) * NU)
                    alone(dve)
                without = dve.value_load(flags[0:1, bass.ds(l + L, 1)], min_val=0, max_val=1)
                with dve.If(without):
                    def z_again(t, s, turn):
                        dve.wait_ge(z_T, l * NT + t + 1)
                        alone(dve)
                        v.tensor_copy(zT[:, :, rows_of(t)], bank[s][:, 0:KD * P].rearrange("p (k n) -> p k n", k=KD)).then_inc(z_cp, 1)

                    pipelined(dve, [(0, z_again)], NT)
                    dve.wait_ge(z_cp, (l + 1) * NT)

                    dve.wait_ge(a_tab, l * 32 + 32)
                    v.tensor_copy(dst_f[:, :], dst_sb[:, :]).then_inc(a_dst, 1)
                    dve.wait_ge(a_dst, l + 1)
                    dve.wait_ge(a_iota, l + 1)
                    for f in range(KD):
                        def one(t, s, turn):
                            if not (isinstance(t, int) and t < 2):
                                dve.wait_ge(a_mm, (l * KD + f) * ET + t - 1)
                            v.tensor_scalar(onehot[:, s, :], iota_n, dst_f[:, bass.ds(t, 1)], None, ALU.is_equal).then_inc(a_oh, 1)

                        if f:
                            dve.wait_ge(a_mm, (l * KD + f) * ET)
                        pipelined(dve, [(0, one)], ET)
                        dve.wait_ge(a_mm, (l * KD + f + 1) * ET)
                        for c in range(NC):
                            w = min(CH, N - c * CH)
                            v.scalar_tensor_tensor(zT[:, f, c * CH:c * CH + w], zT[:, f, c * CH:c * CH + w],
                                                   eps1[:, bass.ds(l, 1)], bank[c][:, 0:w], ALU.mult,
                                                   ALU.add).then_inc(a_slow, 1)
                    dve.wait_ge(a_slow, (l + 1) * NU)
                    alone(dve)

                dve.sem_inc(l_sum, 1)

                def pre_ln(t, s, turn):
                    dve.wait_ge(l_m2, l * NT + t + 1)
                    dve.wait_ge(l_hb, l * NT + t + 1)
                    if not (isinstance(t, int) and t < 2):
                        dve.wait_ge(l_nrm, l * NT + t - 1)
                    v.tensor_tensor(pre[:, s, :], bank[2 + s][0:P, 0:D], base[:, s, :], ALU.add).then_inc(l_pre, 1)

                def stats_ln(t, s, turn):
                    dve.wait_ge(l_pre, l * NT + t + 1)
                    v.bn_stats(st[:, s, :], pre[:, s, :]).then_inc(l_bn, 1)
                    dve.wait_ge(l_bn, l * NT + t + 1)
                    alone(dve)
                    v.bn_aggr(mv[:, s, :], st[:, s, :]).then_inc(l_mv, 1)

                def ln(t, s, turn):
                    dve.wait_ge(l_rs, l * NT + t + 1)
                    if not (isinstance(t, int) and t < 2):
                        dve.wait_ge(l_h, l * NT + t - 1)
                    v.scalar_tensor_tensor(xn[:, s, 0:D], pre[:, s, :], mv[:, s, 0:1], gabc[:, :], ALU.subtract,
                                           ALU.mult).then_inc(l_nrm, 1)
                    dve.wait_ge(l_nrm, l * NT + t + 1)
                    v.scalar_tensor_tensor(xn[:, s, 0:D], xn[:, s, 0:D], rs[:, s:s + 1], bebc[:, :], ALU.mult,
                                           ALU.add).then_inc(l_be, 1)

                dve.wait_ge(l_sum, l + 1)
                dve.wait_ge(l_w, 96 * (l + 1))
                pipelined(dve, [(5, ln), (3, pre_ln), (3, stats_ln)], NT)

            def x2(t, s, turn):
                dve.wait_ge(t_ld[s], 16 * (turn + 1))
                dve.wait_ge(t_ld2[s], 16 * (turn + 1))
                alone(dve)
                v.tensor_tensor(acc_of(t), tinh[:, s, :], tinm[:, s, :], ALU.add).then_inc(t_x2, 1)

            def tok_st(t, s, turn):
                dve.wait_ge(t_x2, t + 1)
                alone(dve)
                v.bn_stats(st[:, s, :], acc_of(t)).then_inc(t_bn, 1)
                dve.wait_ge(t_bn, t + 1)
                alone(dve)
                v.bn_aggr(mv[:, s, :], st[:, s, :]).then_inc(t_mv, 1)

            def tok_n(t, s, turn):
                dve.wait_ge(t_rs, t + 1)
                if not (isinstance(t, int) and t < 2):
                    dve.wait_ge(t_T, t - 1)
                    dve.wait_ge(t_acc, t - 1)
                alone(dve)
                v.tensor_scalar(xn[:, s, 0:D], acc_of(t), mv[:, s, 0:1], rs[:, s:s + 1], ALU.subtract, ALU.mult).then_inc(t_t, 1)

            def logits(t, s, turn):
                dve.wait_ge(t_lg, t + 1)
                if not (isinstance(t, int) and t < 2):
                    dve.wait_ge(r_p, t - 1)
                alone(dve)
                v.reduce_max(rmax[:, s, 0:1], bank[5][0:P, 0:X], AX.X).then_inc(r_max, 1)
                dve.wait_ge(r_max, t + 1)
                alone(dve)
                v.tensor_scalar(lg[:, s, :], bank[5][0:P, 0:X], rmax[:, s, 0:1], None, ALU.subtract).then_inc(t_lgs, 1)

            NR = 17

            def routing(part):
                def fn(t, s, turn):
                    def col(k):
                        return rmax[:, s, k:k + 1]

                    p_, k_, o1, o2 = pr[:, s, :], key[:, s, :], oh1[:, s, :], oh2[:, s, :]
                    ops = [
                        lambda: v.reduce_sum(col(1), p_, AX.X),
                        lambda: v.reciprocal(col(1), col(1)),
                        lambda: v.tensor_scalar(p_, p_, col(1), None, ALU.mult),
                        lambda: v.reduce_max(col(2), p_, AX.X),
                        lambda: v.scalar_tensor_tensor(o1, p_, col(2), rank8[:, :], ALU.is_ge, ALU.mult),
                        lambda: v.reduce_max(col(3), o1, AX.X),
                        lambda: v.tensor_scalar(o1, o1, col(3), None, ALU.is_equal),
                        lambda: v.scalar_tensor_tensor(k_, o1, -2.0, p_, ALU.mult, ALU.add),
                        lambda: v.reduce_max(col(4), k_, AX.X),
                        lambda: v.scalar_tensor_tensor(o2, k_, col(4), rank8[:, :], ALU.is_ge, ALU.mult),
                        lambda: v.reduce_max(col(5), o2, AX.X),
                        lambda: v.scalar_tensor_tensor(o1, o2, col(5), o1, ALU.is_equal, ALU.add),
                        lambda: v.tensor_tensor(p_, p_, o1, ALU.mult),
                        lambda: v.reduce_sum(col(6), p_, AX.X),
                        lambda: v.tensor_scalar(col(6), col(6), 1e-12, None, ALU.max),
                        lambda: v.reciprocal(col(6), col(6)),
                        lambda: v.tensor_scalar(comb[:, bass.ds(t, 1), :].rearrange("p a x -> p (a x)"), p_, col(6), None, ALU.mult),
                    ]
                    assert len(ops) == NR
                    if part == 0:
                        dve.wait_ge(r_p, t + 1)
                        alone(dve)
                    for n in range(part * NR // 5, (part + 1) * NR // 5):
                        ops[n]().then_inc(r_op, 1)
                        dve.wait_ge(r_op, NR * t + n + 1)
                        alone(dve)
                    if part == 4:
                        v.tensor_scalar(cslot[:, s, :], p_, col(6), None, ALU.mult).then_inc(c_sl, 1)
                return fn

            def cmb_cp(t, s, turn):
                dve.wait_ge(c_T, t + 1)
                if not (isinstance(t, int) and t < 2):
                    dve.wait_ge(c_b, t - 1)
                v.tensor_copy(combT[:, s, :], bank[6][0:X, 0:P]).then_inc(c_Ts, 1)

            def cmb_acc(t, s, turn):
                dve.wait_ge(c_b, t + 1)
                dve.wait_ge(x_acc, X * (t + 1))
                alone(dve)
                v.tensor_tensor(acc_of(t), acc_of(t), bank[7][0:P, 0:D], ALU.add).then_inc(c_acc, 1)

            def exp_acc(e):
                def fn(t, s, turn):
                    dve.wait_ge(x_m2, t * X + e + 1)
                    if e == 0:
                        dve.wait_ge(t_acc, t + 1)
                        dve.wait_ge(c_sl, t + 1)
                    if not (e == 0 and isinstance(t, int) and t == 0):
                        dve.wait_ge(x_acc, t * X + e)
                    alone(dve)
                    v.scalar_tensor_tensor(acc_of(t), bank[2 + e % 2][0:P, 0:D],
                                           comb[:, bass.ds(t, 1), e:e + 1].rearrange("p a x -> p (a x)"),
                                           acc_of(t), ALU.mult, ALU.add).then_inc(x_acc, 1)
                return fn

            dve.wait_ge(l_zT, L * NT)
            for e in range(X):
                i = v.memset(rank8[:, e:e + 1], float(X - e))
            i.then_inc(r_const, 1)
            dve.wait_ge(r_const, 2)
            between = {0: [(6, cmb_cp), (7, cmb_acc)], 6: [(1, tok_n), (3, logits)], 7: [(0, x2), (0, tok_st)]}
            between.update({1 + part: (4, routing(part)) for part in range(5)})
            pipelined(dve, experts_of([(3, exp_acc)], between), NT)

        @block.scalar
        def _(act):
            a = nc.scalar
            act.wait_ge(s_const, 5)

            def z0(t, s, turn):
                act.wait_ge(s_xT, t + 1)
                alone(act)
                a.activation(zT[:, :, rows_of(t)], bank[s % 2][:, 0:KD * P].rearrange("p (k n) -> p k n", k=KD), ACT.Copy).then_inc(s_zT, 1)

            def high(t, s, turn):
                act.wait_ge(s_xn, t + 1)
                alone(act)
                a.activation(part_of(t, 0), xn4[:, s, 0:D], ACT.Copy).then_inc(s_hi, 1)

            pipelined(act, [(4, z0), (3, high)], NT, unroll=4, head=4)
            act.wait_ge(f_dve, 6)
            for b in range(KD):
                for hh in range(2):
                    r = slice(hh * HD, (hh + 1) * HD)
                    i = a.activation(attn[r, b, r], bank[7][r, b * 128 + hh * HD:b * 128 + (hh + 1) * HD], ACT.Exp,
                                     bias=amax[r, b:b + 1], scale=float(HD) ** -0.5, accum_out=asum[r, b:b + 1])
            i.then_inc(f_act, 1)

            def mix_xTs(t, s, turn):
                if not (isinstance(t, int) and t < 2):
                    act.wait_ge(m_xf, t - 1)
                alone(act)
                a.activation(tTs[:, s, :, :], zT[:, :, rows_of(t)], ACT.Copy).then_inc(m_xTs, 1)

            def mix_hTs(t, s, turn):
                act.wait_ge(m_hT, t + 1)
                if not (isinstance(t, int) and t < 2):
                    act.wait_ge(m_f1, t - 1)
                a.activation(hmT[:, s, :, :], bank[1][:, 0:KD * P].rearrange("p (k n) -> p k n", k=KD), ACT.Copy).then_inc(m_hTs, 1)

            def mix_gelu(t, s, turn):
                act.wait_ge(m_f1, t + 1)
                if not (isinstance(t, int) and t < 2):
                    act.wait_ge(m_f2, t - 1)
                for m in range(KF):
                    i = a.activation(gT[:, s, m, :], bank[4 + 2 * s + m // 4][:, m % 4 * P:(m % 4 + 1) * P], ACT.Gelu,
                                     bias=b1p[:, m:m + 1])
                i.then_inc(m_g, 1)

            act.wait_ge(s_zT, NT)
            pipelined(act, [(9, mix_gelu), (7, mix_hTs), (1, mix_xTs)], NT)

            def ranks(g):
                def fn(j, s, turn):
                    if g == 0:
                        act.wait_ge(b_rk, j + 1)
                        if isinstance(j, int) and j == 0:
                            act.wait_ge(m_st[0], 16 * (NT - NT // 2))
                            act.wait_ge(m_st[1], 16 * (NT // 2))
                        else:
                            act.wait_ge(b_v, j)
                    for k in range(g * KA // NG, (g + 1) * KA // NG):
                        i = a.activation(OR[:, k, :], iota0[:, :], ACT.Abs, bias=rk[:, s, k:k + 1], scale=-1.0)
                    if g == NG - 1:
                        i.then_inc(b_abs, 1)
                return fn

            def ranks_end(j, s, turn):
                act.wait_ge(b_abs, j + 1)
                a.activation(OR[:, 0:KA, :], OR[:, 0:KA, :], ACT.Relu, bias=1.0, scale=-1.0).then_inc(b_oa, 1)

            def evict(g):
                def fn(j, s, turn):
                    q = (s * NG + g) % 2
                    w = min(4, NT - 4 * g)
                    act.wait_ge(b_tab, j * NG + g + 1)
                    alone(act)
                    a.activation(table[:, bass.ds(j, 1), 4 * g:4 * g + w, :].rearrange("p a i d -> p (a i d)"),
                                 bank[4 + q][0:P, 0:w * P], ACT.Copy).then_inc(b_ev, 1)
                return fn

            act.wait_ge(w_pool, 3)
            pipelined(act, [step for g in range(NG) for step in ((3, evict(g)), (1, ranks(g)))] + [(1, ranks_end)], NT)

            with act.Fori(0, L) as l:
                act.wait_ge(l_w, 96 * (l + 1))

                def relu1(t, s, turn):
                    act.wait_ge(l_m1, l * NT + t + 1)
                    if not (isinstance(t, int) and t < 2):
                        act.wait_ge(l_m2, l * NT + t - 1)
                    for m in range(KD):
                        i = a.activation(tTs[:, s, m, :], bank[s][:, m * P:(m + 1) * P], ACT.Relu, bias=b1c[:, m:m + 1])
                    i.then_inc(l_re, 1)

                def relu2(t, s, turn):
                    act.wait_ge(l_be, l * NT + t + 1)
                    if not (isinstance(t, int) and t < 2):
                        act.wait_ge(l_hT, l * NT + t - 1)
                        act.wait_ge(l_st[s], 16 * (l * ((NT + 1 - s) // 2) + turn))
                        act.wait_ge(l_lo, l * NT + t - 1)
                    a.activation(res[:, s, :], xn[:, s, 0:D], ACT.Relu).then_inc(l_h, 1)
                    act.wait_ge(l_h, l * NT + t + 1)
                    alone(act)
                    a.activation(part_of(t, 0), res[:, s, :], ACT.Copy).then_inc(l_hi, 1)

                def z_next(t, s, turn):
                    act.wait_ge(l_hT, l * NT + t + 1)
                    alone(act)
                    a.activation(zT[:, :, rows_of(t)], bank[4 + s][:, 0:KD * P].rearrange("p (k n) -> p k n", k=KD), ACT.Copy).then_inc(l_zT, 1)

                pipelined(act, [(8, z_next), (6, relu2), (1, relu1)], NT)

            def tok_Ts(t, s, turn):
                act.wait_ge(t_T, t + 1)
                if not (isinstance(t, int) and t < 2):
                    act.wait_ge(t_lg, t - 1)
                alone(act)
                transposed = bank[4][:, 0:KD * P].rearrange("p (k n) -> p k n", k=KD)
                a.activation(tTs[:, s, :, :], transposed, ACT.Copy).then_inc(t_Ts, 1)
                a.activation(tT[:, :, rows_of(t)], transposed, ACT.Copy).then_inc(t_cp, 1)

            def exp_g(e):
                def fn(t, s, turn):
                    act.wait_ge(x_m1, t * X + e + 1)
                    if not (isinstance(t, int) and t * X + e < 2):
                        act.wait_ge(x_m2, t * X + e - 1)
                    for m in range(KD):
                        i = a.activation(gTe[:, e % 2, m, :], bank[e % 2][:, m * P:(m + 1) * P], ACT.Gelu, bias=eb1[:, e, m:m + 1])
                    i.then_inc(x_g, 1)
                return fn

            act.wait_ge(l_zT, L * NT)
            act.wait_ge(e_w, 16 * NE)
            pipelined(act, experts_of([(1, exp_g)], {6: (2, tok_Ts)}), NT)

        @block.gpsimd
        def _(pool):
            g = nc.gpsimd
            g.memset(half[:, :], -0.5).then_inc(s_const, 1)
            g.memset(ones_row[:, :], 1.0)
            g.memset(ident[:, :], 0.0).then_inc(s_clear, 1)
            pool.wait_ge(s_clear, 1)
            g.affine_select(out=ident[:, :], in_=ident[:, :], compare_op=ALU.not_equal, fill=1.0, base=0,
                            pattern=[[-1, 128]], channel_multiplier=1).then_inc(s_const, 1)
            pool.wait_ge(s_const, 5)

            def rsqrt(s, begin, mid, mid_n, end):
                alone(pool)
                g.tensor_scalar(ve[:, s:s + 1], mv[:, s, 1:2], EPS, None, ALU.add).then_inc(mid, 1)
                pool.wait_ge(mid, mid_n)
                g.tensor_tensor(rs[:, s:s + 1], ve[:, s:s + 1], half[0:P, :], ALU.pow).then_inc(end, 1)

            def norm_rs(t, s, turn):
                pool.wait_ge(s_mv, t + 1)
                rsqrt(s % 2, s_mv, s_ve, t + 1, s_rs)

            g.memset(dst_next[:, :], N).then_inc(w_pool, 1)
            g.iota(wbase[:, :].rearrange("p (j k) -> p j k", k=KW), pattern=[[P, NT], [0, KW]], base=0, channel_multiplier=0,
                   allow_small_or_imprecise_dtypes=True).then_inc(w_pool, 1)
            pipelined(pool, [(1, norm_rs)], NT, unroll=4, head=4)
            pool.wait_ge(f_dve, 10)
            pool.wait_ge(s_wld, 16 * NW)

            def mix_xb(t, s, turn):
                pool.wait_ge(m_ld[s], 16 * (turn + 1))
                if not (isinstance(t, int) and t < 2):
                    pool.wait_ge(m_pre, t - 1)
                g.tensor_tensor(base[:, s, :], tin[:, s, :], cbc[:, :], ALU.add).then_inc(m_xb, 1)

            def mix_rs(t, s, turn):
                pool.wait_ge(m_mv, t + 1)
                rsqrt(s, m_mv, m_ve, t + 1, m_rs)

            def mix_res(t, s, turn):
                pool.wait_ge(m_pre, t + 1)
                alone(pool)
                g.tensor_tensor(row_of(x_all, t), row_of(x_all, t), pre[:, s, :], ALU.add).then_inc(m_res, 1)

            def mix_r1(t, s, turn):
                alone(pool)
                g.tensor_tensor(row_of(x_all, t), row_of(x_all, t), bf2[:, :], ALU.add).then_inc(m_r1, 1)
                pool.wait_ge(m_r1, t + 1)
                alone(pool)

            pipelined(pool, [(4, mix_rs), (4, mix_res), (0, mix_r1), (0, mix_xb)], NT)

            pool.wait_ge(w_dve, 3)
            g.iota(iota25[:, 0:NT], pattern=[[1, NT]], base=0, channel_multiplier=0, allow_small_or_imprecise_dtypes=True)
            g.iota(iota0[:, :], pattern=[[1, 128]], base=0, channel_multiplier=0, allow_small_or_imprecise_dtypes=True)
            g.iota(iota1[:, :], pattern=[[1, 128]], base=1, channel_multiplier=0, allow_small_or_imprecise_dtypes=True)
            g.memset(OH[:, :, 0:NT], 0.0)
            g.memset(S2[:, 0:2 * NT], 0.0)
            g.memset(tri[:, :], 1.0).then_inc(w_tri, 1)
            pool.wait_ge(w_tri, 1)
            g.affine_select(out=tri[:, :], in_=tri[:, :], compare_op=ALU.is_gt, fill=0.0, base=0,
                            pattern=[[1, 128]], channel_multiplier=-1).then_inc(w_pool, 1)
            pool.wait_ge(w_pool, 3)

            def sources(j, s, turn):
                if not (isinstance(j, int) and j < 2):
                    pool.wait_ge(b_rank, j - 1)
                if not (isinstance(j, int) and j == 0):
                    pool.wait_ge(b_s4, j)
                pool.wait_ge(b_oh, j + 1)
                g.tensor_tensor(S2[:, 2 * NT:], OH[:, s, NT:], OH[:, s, 0:KW * NT], ALU.add).then_inc(b_s2, 1)
                pool.wait_ge(b_s2, j + 1)
                g.tensor_tensor(S4[:, s, :], S2[:, 2 * NT:], S2[:, 0:KW * NT], ALU.add).then_inc(b_s4, 1)

            def edge_places(j, s, turn):
                oh = OH[:, s, NT:].rearrange("p (k i) -> p k i", k=KW)
                if not (isinstance(j, int) and j < 2):
                    pool.wait_ge(b_v, j - 1)
                g.tensor_tensor(OV[:, s, :, 0:NT], oh, over_tiles(s0p, j), ALU.mult)
                g.tensor_tensor(OV[:, s, :, NT:2 * NT], oh, over_tiles(d0p, j), ALU.mult).then_inc(b_ov, 1)

            pipelined(pool, [(1, edge_places), (0, sources)], NT)
            pool.wait_ge(b_flag, 1)
            pool.wait_ge(b_ev, NT * NG)
            pool.wait_ge(a_first, NT + 1)

            with pool.Fori(0, L) as l:
                pool.wait_ge(l_open, l + 1)
                without = pool.value_load(flags[0:1, bass.ds(l + L, 1)], min_val=0, max_val=1)
                with pool.If(without):
                    def h_rows(t, s, turn):
                        if not (isinstance(t, int) and t < 2):
                            pool.wait_ge(z_T, l * NT + t - 1)
                        alone(pool)
                        pool.dma_start(rows[:, s, :], h_dram[rows_of(t), :]).then_inc(z_ld[s], 16)

                    pipelined(pool, [(0, h_rows)], NT)
                    pool.wait_ge(z_cp, (l + 1) * NT)
                    alone(pool)
                    pool.dma_start(src_sb[:, :], src.rearrange("(p t) -> p t", p=P)).then_inc(a_tab, 16)
                    pool.dma_start(dst_sb[:, :], dst.rearrange("(p t) -> p t", p=P)).then_inc(a_tab, 16)
                    pool.wait_ge(a_tab, l * 32 + 32)
                    alone(pool)
                    g.iota(iota_n, pattern=[[1, N]], base=0, channel_multiplier=0,
                           allow_small_or_imprecise_dtypes=True).then_inc(a_iota, 1)
                    for f in range(KD):
                        def gather(t, s, turn):
                            if not (isinstance(t, int) and t < 2):
                                pool.wait_ge(a_mm, (l * KD + f) * ET + t - 1)
                            alone(pool)
                            g.tensor_copy(idx[:, s:s + 1], src_sb[:, bass.ds(t, 1)]).then_inc(a_idx, 1)
                            pool.wait_ge(a_idx, (l * KD + f) * ET + t + 1)
                            alone(pool)
                            g.indirect_dma_start(out=rows[:, s, :], out_offset=None, in_=h_dram,
                                                 in_offset=bass.IndirectOffsetOnAxis(ap=idx[:, s:s + 1], axis=0)).then_inc(a_row[s], 16)

                        if f:
                            pool.wait_ge(a_mm, (l * KD + f) * ET)
                        pipelined(pool, [(0, gather)], ET)

                pool.wait_ge(l_w, 96 * (l + 1))

                def hb(t, s, turn):
                    pool.wait_ge(l_ld[s], 16 * (l * ((NT + 1 - s) // 2) + turn + 1))
                    if not (isinstance(t, int) and t < 2):
                        pool.wait_ge(l_pre, l * NT + t - 1)
                    g.tensor_tensor(base[:, s, :], tin[:, s, :], b2bc[:, :], ALU.add).then_inc(l_hb, 1)

                def ln_rs(t, s, turn):
                    pool.wait_ge(l_mv, l * NT + t + 1)
                    rsqrt(s, l_mv, l_ve, l * NT + t + 1, l_rs)

                def h_low(t, s, turn):
                    pool.wait_ge(l_hi, l * NT + t + 1)
                    alone(pool)
                    g.tensor_tensor(part_of(t, 1), res[:, s, :], part_of(t, 0), ALU.subtract).then_inc(l_lo, 1)

                pipelined(pool, [(7, h_low), (4, ln_rs), (2, hb)], NT)

            pool.wait_ge(l_zT, L * NT)

            def tok_rs(t, s, turn):
                pool.wait_ge(t_mv, t + 1)
                rsqrt(s, t_mv, t_ve, t + 1, t_rs)

            def tok_acc(t, s, turn):
                pool.wait_ge(t_t, t + 1)
                alone(pool)
                g.tensor_tensor(acc_of(t), acc_of(t), xn[:, s, 0:D], ALU.add).then_inc(t_acc, 1)

            def exponentials(t, s, turn):
                pool.wait_ge(t_lgs, t + 1)
                if not (isinstance(t, int) and t < 2):
                    pool.wait_ge(c_sl, t - 1)
                g.tensor_tensor(pr[:, s, :], euler[:, :], lg[:, s, :], ALU.pow).then_inc(r_p, 1)

            g.memset(euler[:, :], math.e).then_inc(r_const, 1)
            pool.wait_ge(r_const, 2)
            pipelined(pool, [(3, exponentials), (1, tok_acc), (0, tok_rs)], NT)


_INS = ['x', 'src', 'dst', 'L0_gnn_W1', 'L0_gnn_b1', 'L0_gnn_W2', 'L0_gnn_b2', 'L0_gnn_eps', 'L0_gnn_gamma',
        'L0_gnn_beta', 'L0_mix_w_qkv', 'L0_mix_b_qkv', 'L0_mix_norm_g', 'L0_mix_norm_b', 'L0_mix_w_fc1',
        'L0_mix_b_fc1', 'L0_mix_w_fc2', 'L0_mix_b_fc2', 'L0_ffn_router_w', 'L0_ffn_w1', 'L0_ffn_b1',
        'L0_ffn_w2', 'L0_ffn_b2']


def kernel(**inputs):
    import numpy as _np
    import concourse.bacc as _bacc
    from concourse import mybir as _mybir
    from concourse.bass_utils import run_bass_kernel_spmd as _run

    nc = _bacc.Bacc("TRN2", target_bir_lowering=False, num_devices=1, dynamic_dma_scratch_size=2048)
    arrays, args = {}, []
    for name in _INS:
        a = _np.ascontiguousarray(inputs[name])
        arrays[f"in_{name}"] = a
        args.append(nc.dram_tensor(f"in_{name}", a.shape, _mybir.dt.from_np(a.dtype), kind="ExternalInput").ap())
    shape = tuple(inputs['x'].shape)
    fp32 = _mybir.dt.float32
    args.append(nc.dram_tensor("out_x", shape, fp32, kind="ExternalOutput").ap())
    args.append(nc.dram_tensor("h_rows", shape, fp32, kind="Internal").ap())
    args.append(nc.dram_tensor("acc_rows", shape, fp32, kind="Internal").ap())
    graph_block_kernel(nc, *args)
    r = _run(nc, [arrays], core_ids=[0])
    return r.results[0]["out_x"]
```
